# Optimizing a Trainium2 kernel written in Bass

```python
import numpy as np
import jax
import jax.numpy as jnp

def _softmax(x, axis=-1):
    return jax.nn.softmax(x, axis=axis)

def _gelu(x):
    return jax.nn.gelu(x, approximate=True)

def _silu(x):
    return jax.nn.silu(x)

def _sigmoid(x):
    return jax.nn.sigmoid(x)

def _layernorm(x, axis=-1, eps=1e-05):
    m = jnp.mean(x, axis=axis, keepdims=True)
    v = jnp.var(x, axis=axis, keepdims=True)
    return (x - m) / jnp.sqrt(v + eps)

def _scatter_add(tgt, idx, src, axis=0):
    return tgt.at[idx].add(src)

def _segment_sum(src, seg, n):
    return jax.ops.segment_sum(src, seg, n)
kernel_name = 'mk_decoder_preln_d1_seqx_r8_d272f7'

def setup_inputs(seed: int=0):
    np.random.seed(seed)
    _w = jnp.asarray

    def _rec_inputs():
        import jax
        import jax.numpy as jnp
        _rk = jax.random.key(seed)
        x = 7.22e-05 + 1 * jax.random.normal(jax.random.fold_in(_rk, 1), (64, 64, 256), jnp.float32)
        _lenS = 64 - jax.random.randint(jax.random.fold_in(_rk, 7), (64,), 0, max(1, 64 // 4) + 1, jnp.int32)
        _lenS2 = 64 - jax.random.randint(jax.random.fold_in(_rk, 8), (64,), 0, max(1, 64 // 4) + 1, jnp.int32)
        _ctx_512P = jax.random.normal(jax.random.fold_in(_rk, 11), (64, 16, 64), jnp.float32)
        _ctx_512c = jax.random.dirichlet(jax.random.fold_in(_rk, 511), 0.3 * jnp.ones((16,), jnp.float32), (64, 64))
        _ctx_512t = jnp.einsum('bsk,bkd->bsd', _ctx_512c, _ctx_512P)
        _ctx_512t = _ctx_512t * jax.lax.rsqrt(jnp.mean(jnp.square(_ctx_512t)) + 1e-12) * 0.953939
        ctx_512 = -0.000514642 + 1.00011 * (_ctx_512t + 0.3 * jax.random.normal(jax.random.fold_in(_rk, 611), (64, 64, 64), jnp.float32))
        return (x, ctx_512)
    x, ctx_512 = _rec_inputs()

    def _L0_attn_setup():
        import jax, jax.numpy as jnp
        import numpy as np
        import math
        B, T, D_MODEL, N_HEADS, K_CONV = (2, 256, 256, 16, 4)
        HEAD_DIM = D_MODEL // N_HEADS
        EPS_GN = 1e-05

        def _group_norm(x2d, w, b, groups, eps):
            N, C = x2d.shape
            xg = x2d.reshape(N, groups, C // groups)
            mu = xg.mean(-1, keepdims=True)
            var = ((xg - mu) ** 2).mean(-1, keepdims=True)
            xn = ((xg - mu) * jax.lax.rsqrt(var + eps)).reshape(N, C)
            return xn * w + b

        def _causal_depthwise_conv(x, w, b):
            xt = jnp.transpose(x, (0, 2, 1))
            xp = jnp.pad(xt, ((0, 0), (0, 0), (K_CONV - 1, 0)))
            y = jax.lax.conv_general_dilated(xp, w[:, None, :], (1,), 'VALID', feature_group_count=D_MODEL, dimension_numbers=('NCH', 'OIH', 'NCH'))
            y = y + b[None, :, None]
            return jax.nn.silu(jnp.transpose(y, (0, 2, 1)))

        def _l2norm(t):
            n = jnp.sqrt(jnp.sum(t * t, axis=-1, keepdims=True))
            return t / jnp.maximum(n, 1e-12)

        def _reference_tuple_inner(x, Wq, Wk, Wv, Wo, conv_w, conv_b, Wig, b_ig, Wog, b_og, Wg, b_g, gn_w, gn_b, mn_w, mn_b):
            Bq, Tq, C = x.shape
            x_conv = _causal_depthwise_conv(x, conv_w, conv_b)
            q = _l2norm((x @ Wq.T).reshape(Bq, Tq, N_HEADS, HEAD_DIM))
            k = _l2norm((x @ Wk.T).reshape(Bq, Tq, N_HEADS, HEAD_DIM))
            v = (x @ Wv.T).reshape(Bq, Tq, N_HEADS, HEAD_DIM)
            input_gate = jax.nn.sigmoid(x_conv @ Wig.T + b_ig).reshape(Bq, Tq, N_HEADS, HEAD_DIM)
            gamma = jax.nn.sigmoid(x_conv @ Wg.T + b_g).reshape(Bq, Tq, N_HEADS, 1)
            bterm = input_gate * k * v
            aterm = jnp.broadcast_to(gamma, bterm.shape)

            def scan_op(c1, c2):
                a1, b1 = c1
                a2, b2 = c2
                return (a1 * a2, a2 * b1 + b2)
            _, mem = jax.lax.associative_scan(scan_op, (aterm, bterm), axis=1)
            next_rnn_state = mem[:, -1]
            mem_n = _group_norm(mem.reshape(Bq * Tq, D_MODEL), mn_w, mn_b, N_HEADS, EPS_GN)
            mem_n = mem_n.reshape(Bq, Tq, N_HEADS, HEAD_DIM)
            out = (mem_n * q).reshape(Bq * Tq, C)
            out = _group_norm(out, gn_w, gn_b, N_HEADS, EPS_GN).reshape(Bq, Tq, C)
            output_gate = jax.nn.sigmoid(x_conv @ Wog.T + b_og)
            out = out * output_gate @ Wo.T
            new_conv_cache = jnp.transpose(x, (0, 2, 1))[:, :, -(K_CONV - 1):]
            return (out, next_rnn_state, new_conv_cache)
        key = jax.random.key(seed)
        ks = jax.random.split(key, 16)
        s = 0.02
        min_d, max_d = (0.9, 0.9999)
        tgt = 1.0 - np.exp(np.linspace(math.log(1 - min_d), math.log(1 - max_d), N_HEADS))
        gamma_bias = np.log(tgt / (1 - tgt)).astype(np.float32)
        return {'x': jax.random.normal(ks[0], (B, T, D_MODEL), jnp.float32), 'Wq': jax.random.normal(ks[1], (D_MODEL, D_MODEL), jnp.float32) * s, 'Wk': jax.random.normal(ks[2], (D_MODEL, D_MODEL), jnp.float32) * s, 'Wv': jax.random.normal(ks[3], (D_MODEL, D_MODEL), jnp.float32) * s, 'Wo': jax.random.normal(ks[4], (D_MODEL, D_MODEL), jnp.float32) * s, 'conv_w': jax.random.normal(ks[5], (D_MODEL, K_CONV), jnp.float32) * 0.1, 'conv_b': jnp.zeros((D_MODEL,), jnp.float32), 'Wig': jax.random.normal(ks[6], (D_MODEL, D_MODEL), jnp.float32) * s, 'b_ig': jnp.zeros((D_MODEL,), jnp.float32), 'Wog': jax.random.normal(ks[7], (D_MODEL, D_MODEL), jnp.float32) * s, 'b_og': jnp.zeros((D_MODEL,), jnp.float32), 'Wg': jnp.zeros((N_HEADS, D_MODEL), jnp.float32), 'b_g': jnp.asarray(gamma_bias), 'gn_w': jnp.ones((D_MODEL,), jnp.float32), 'gn_b': jnp.zeros((D_MODEL,), jnp.float32), 'mn_w': jnp.ones((D_MODEL,), jnp.float32), 'mn_b': jnp.zeros((D_MODEL,), jnp.float32)}
    _L0_attn_all = _L0_attn_setup()
    _L0_attn_in = {k: v for k, v in _L0_attn_all.items() if k in ('Wq', 'Wk', 'Wv', 'Wo', 'conv_w', 'conv_b', 'Wig', 'b_ig', 'Wog', 'b_og', 'Wg', 'b_g', 'gn_w', 'gn_b', 'mn_w', 'mn_b')}
    del _L0_attn_all

    def _L0_xattn_setup():
        import jax, jax.numpy as jnp
        import numpy as np
        B, S, E = (2, 256, 256)
        QH, KVH = (32, 8)
        D = E // QH
        G = QH // KVH
        DROPOUT = 1.0
        key = jax.random.key(seed)
        k1, k2, k3 = jax.random.split(key, 3)
        q = jax.random.normal(k1, (B, S, E), dtype=jnp.float32)
        k = jax.random.normal(k2, (B, S, E // G), dtype=jnp.float32)
        v = jax.random.normal(k3, (B, S, E // G), dtype=jnp.float32)
        return {'q': q, 'k': k, 'v': v}
    _L0_xattn_all = _L0_xattn_setup()
    _L0_xattn_in = {k: v for k, v in _L0_xattn_all.items() if k in ()}
    del _L0_xattn_all

    def _L0_ffn_setup():
        import jax, jax.numpy as jnp
        import numpy as np
        N_EXPERTS = 8
        TOP_K = 2
        N_GROUP = 4
        TOPK_GROUP = 2
        ROUTED_SCALE = 1.0

        def _group_limited_topk(scores):
            T, N = scores.shape
            E = N // N_GROUP
            group_scores = scores.reshape(T, N_GROUP, E).max(axis=-1)
            _, gidx = jax.lax.top_k(group_scores, TOPK_GROUP)
            gmask = jax.nn.one_hot(gidx, N_GROUP, dtype=scores.dtype).sum(1)
            smask = jnp.repeat(gmask, E, axis=1)
            masked = jnp.where(smask > 0, scores, jnp.zeros((), scores.dtype))
            topk_w, topk_i = jax.lax.top_k(masked, TOP_K)
            return (topk_w, topk_i)
        key = jax.random.key(seed)
        ks = jax.random.split(key, 8)
        B, S, H, F, FS, N = (2, 128, 256, 176, 352, N_EXPERTS)
        std = jnp.float32(0.02)
        return {'hidden_states': jax.random.normal(ks[0], (B, S, H), jnp.float32), 'gate_weight': jax.random.normal(ks[1], (N, H), jnp.float32) * std, 'gate_w': jax.random.normal(ks[2], (N, F, H), jnp.float32) * std, 'up_w': jax.random.normal(ks[3], (N, F, H), jnp.float32) * std, 'down_w': jax.random.normal(ks[4], (N, H, F), jnp.float32) * std, 'sh_gate_w': jax.random.normal(ks[5], (FS, H), jnp.float32) * std, 'sh_up_w': jax.random.normal(ks[6], (FS, H), jnp.float32) * std, 'sh_down_w': jax.random.normal(ks[7], (H, FS), jnp.float32) * std}
    _L0_ffn_all = _L0_ffn_setup()
    _L0_ffn_in = {k: v for k, v in _L0_ffn_all.items() if k in ('gate_weight', 'gate_w', 'up_w', 'down_w', 'sh_gate_w', 'sh_up_w', 'sh_down_w')}
    del _L0_ffn_all
    return {'x': x, 'ctx_512': ctx_512, 'L0_attn_Wq': _L0_attn_in['Wq'], 'L0_attn_Wk': _L0_attn_in['Wk'], 'L0_attn_Wv': _L0_attn_in['Wv'], 'L0_attn_Wo': _L0_attn_in['Wo'], 'L0_attn_conv_w': _L0_attn_in['conv_w'], 'L0_attn_conv_b': _L0_attn_in['conv_b'], 'L0_attn_Wig': _L0_attn_in['Wig'], 'L0_attn_b_ig': _L0_attn_in['b_ig'], 'L0_attn_Wog': _L0_attn_in['Wog'], 'L0_attn_b_og': _L0_attn_in['b_og'], 'L0_attn_Wg': _L0_attn_in['Wg'], 'L0_attn_b_g': _L0_attn_in['b_g'], 'L0_attn_gn_w': _L0_attn_in['gn_w'], 'L0_attn_gn_b': _L0_attn_in['gn_b'], 'L0_attn_mn_w': _L0_attn_in['mn_w'], 'L0_attn_mn_b': _L0_attn_in['mn_b'], 'L0_ffn_gate_weight': _L0_ffn_in['gate_weight'], 'L0_ffn_gate_w': _L0_ffn_in['gate_w'], 'L0_ffn_up_w': _L0_ffn_in['up_w'], 'L0_ffn_down_w': _L0_ffn_in['down_w'], 'L0_ffn_sh_gate_w': _L0_ffn_in['sh_gate_w'], 'L0_ffn_sh_up_w': _L0_ffn_in['sh_up_w'], 'L0_ffn_sh_down_w': _L0_ffn_in['sh_down_w']}

def reference(x, ctx_512, L0_attn_Wq, L0_attn_Wk, L0_attn_Wv, L0_attn_Wo, L0_attn_conv_w, L0_attn_conv_b, L0_attn_Wig, L0_attn_b_ig, L0_attn_Wog, L0_attn_b_og, L0_attn_Wg, L0_attn_b_g, L0_attn_gn_w, L0_attn_gn_b, L0_attn_mn_w, L0_attn_mn_b, L0_ffn_gate_weight, L0_ffn_gate_w, L0_ffn_up_w, L0_ffn_down_w, L0_ffn_sh_gate_w, L0_ffn_sh_up_w, L0_ffn_sh_down_w):
    import jax
    import jax.numpy as jnp

    def _L0_attn_ref(x, Wq, Wk, Wv, Wo, conv_w, conv_b, Wig, b_ig, Wog, b_og, Wg, b_g, gn_w, gn_b, mn_w, mn_b):
        import jax, jax.numpy as jnp
        import numpy as np
        import math
        B, T, D_MODEL, N_HEADS, K_CONV = (2, 256, 256, 16, 4)
        HEAD_DIM = D_MODEL // N_HEADS
        EPS_GN = 1e-05

        def _group_norm(x2d, w, b, groups, eps):
            N, C = x2d.shape
            xg = x2d.reshape(N, groups, C // groups)
            mu = xg.mean(-1, keepdims=True)
            var = ((xg - mu) ** 2).mean(-1, keepdims=True)
            xn = ((xg - mu) * jax.lax.rsqrt(var + eps)).reshape(N, C)
            return xn * w + b

        def _causal_depthwise_conv(x, w, b):
            xt = jnp.transpose(x, (0, 2, 1))
            xp = jnp.pad(xt, ((0, 0), (0, 0), (K_CONV - 1, 0)))
            y = jax.lax.conv_general_dilated(xp, w[:, None, :], (1,), 'VALID', feature_group_count=D_MODEL, dimension_numbers=('NCH', 'OIH', 'NCH'))
            y = y + b[None, :, None]
            return jax.nn.silu(jnp.transpose(y, (0, 2, 1)))

        def _l2norm(t):
            n = jnp.sqrt(jnp.sum(t * t, axis=-1, keepdims=True))
            return t / jnp.maximum(n, 1e-12)

        def _reference_tuple_inner(x, Wq, Wk, Wv, Wo, conv_w, conv_b, Wig, b_ig, Wog, b_og, Wg, b_g, gn_w, gn_b, mn_w, mn_b):
            Bq, Tq, C = x.shape
            x_conv = _causal_depthwise_conv(x, conv_w, conv_b)
            q = _l2norm((x @ Wq.T).reshape(Bq, Tq, N_HEADS, HEAD_DIM))
            k = _l2norm((x @ Wk.T).reshape(Bq, Tq, N_HEADS, HEAD_DIM))
            v = (x @ Wv.T).reshape(Bq, Tq, N_HEADS, HEAD_DIM)
            input_gate = jax.nn.sigmoid(x_conv @ Wig.T + b_ig).reshape(Bq, Tq, N_HEADS, HEAD_DIM)
            gamma = jax.nn.sigmoid(x_conv @ Wg.T + b_g).reshape(Bq, Tq, N_HEADS, 1)
            bterm = input_gate * k * v
            aterm = jnp.broadcast_to(gamma, bterm.shape)

            def scan_op(c1, c2):
                a1, b1 = c1
                a2, b2 = c2
                return (a1 * a2, a2 * b1 + b2)
            _, mem = jax.lax.associative_scan(scan_op, (aterm, bterm), axis=1)
            next_rnn_state = mem[:, -1]
            mem_n = _group_norm(mem.reshape(Bq * Tq, D_MODEL), mn_w, mn_b, N_HEADS, EPS_GN)
            mem_n = mem_n.reshape(Bq, Tq, N_HEADS, HEAD_DIM)
            out = (mem_n * q).reshape(Bq * Tq, C)
            out = _group_norm(out, gn_w, gn_b, N_HEADS, EPS_GN).reshape(Bq, Tq, C)
            output_gate = jax.nn.sigmoid(x_conv @ Wog.T + b_og)
            out = out * output_gate @ Wo.T
            new_conv_cache = jnp.transpose(x, (0, 2, 1))[:, :, -(K_CONV - 1):]
            return (out, next_rnn_state, new_conv_cache)
        return _reference_tuple_inner(x, Wq, Wk, Wv, Wo, conv_w, conv_b, Wig, b_ig, Wog, b_og, Wg, b_g, gn_w, gn_b, mn_w, mn_b)[0]

    def _L0_xattn_ref(q, k, v):
        import jax, jax.numpy as jnp
        import numpy as np
        B, S, E = (2, 256, 256)
        QH, KVH = (32, 8)
        D = E // QH
        G = QH // KVH
        DROPOUT = 1.0
        b, s, _ = q.shape
        qh = q.reshape(b, s, KVH, G, D).transpose(0, 2, 3, 1, 4)
        kh = k.reshape(b, s, KVH, D).transpose(0, 2, 1, 3)
        vh = v.reshape(b, s, KVH, D).transpose(0, 2, 1, 3)
        scale = 1.0 / jnp.sqrt(jnp.float32(D))
        scores = jnp.einsum('bkgsd,bktd->bkgst', qh, kh) * scale
        attn = jax.nn.softmax(scores, axis=-1) / DROPOUT
        out = jnp.einsum('bkgst,bktd->bkgsd', attn, vh)
        return out.transpose(0, 3, 1, 2, 4).reshape(b, s, E)

    def _L0_ffn_ref(hidden_states, gate_weight, gate_w, up_w, down_w, sh_gate_w, sh_up_w, sh_down_w):
        import jax, jax.numpy as jnp
        import numpy as np
        N_EXPERTS = 8
        TOP_K = 2
        N_GROUP = 4
        TOPK_GROUP = 2
        ROUTED_SCALE = 1.0

        def _group_limited_topk(scores):
            T, N = scores.shape
            E = N // N_GROUP
            group_scores = scores.reshape(T, N_GROUP, E).max(axis=-1)
            _, gidx = jax.lax.top_k(group_scores, TOPK_GROUP)
            gmask = jax.nn.one_hot(gidx, N_GROUP, dtype=scores.dtype).sum(1)
            smask = jnp.repeat(gmask, E, axis=1)
            masked = jnp.where(smask > 0, scores, jnp.zeros((), scores.dtype))
            topk_w, topk_i = jax.lax.top_k(masked, TOP_K)
            return (topk_w, topk_i)
        B, S, H = hidden_states.shape
        h = hidden_states.reshape(-1, H)
        logits = h.astype(jnp.float32) @ gate_weight.astype(jnp.float32).T
        scores = jax.nn.softmax(logits, axis=-1)
        topk_w, topk_i = _group_limited_topk(scores)
        topk_w = (topk_w * ROUTED_SCALE).astype(h.dtype)
        wmat = (jax.nn.one_hot(topk_i, N_EXPERTS, dtype=topk_w.dtype) * topk_w[..., None]).sum(axis=1)
        g = jnp.einsum('th,nfh->ntf', h, gate_w)
        u = jnp.einsum('th,nfh->ntf', h, up_w)
        e = jnp.einsum('ntf,nhf->nth', jax.nn.silu(g) * u, down_w)
        routed = jnp.einsum('nth,tn->th', e, wmat)
        sg = h @ sh_gate_w.T
        su = h @ sh_up_w.T
        shared = jax.nn.silu(sg) * su @ sh_down_w.T
        return (routed + shared).reshape(B, S, H)
    x = x + _L0_attn_ref(_layernorm(x, axis=-1), L0_attn_Wq, L0_attn_Wk, L0_attn_Wv, L0_attn_Wo, L0_attn_conv_w, L0_attn_conv_b, L0_attn_Wig, L0_attn_b_ig, L0_attn_Wog, L0_attn_b_og, L0_attn_Wg, L0_attn_b_g, L0_attn_gn_w, L0_attn_gn_b, L0_attn_mn_w, L0_attn_mn_b)
    x = x + _L0_xattn_ref(_layernorm(x, axis=-1), ctx_512, ctx_512)
    x = x + _L0_ffn_ref(_layernorm(x, axis=-1), L0_ffn_gate_weight, L0_ffn_gate_w, L0_ffn_up_w, L0_ffn_down_w, L0_ffn_sh_gate_w, L0_ffn_sh_up_w, L0_ffn_sh_down_w)
    return x

_drawn_inputs = setup_inputs


def setup_inputs(seed=0):
    import zlib

    import numpy as np

    out = dict(_drawn_inputs(seed))
    spreads = {'L0_attn_conv_b': (0.0, 0.8),
     'L0_attn_b_ig': (0.0, 0.8),
     'L0_attn_b_og': (0.0, 0.8),
     'L0_attn_Wg': (0.0, 0.8),
     'L0_attn_gn_w': (1.0, 0.2),
     'L0_attn_gn_b': (0.0, 0.575),
     'L0_attn_mn_w': (1.0, 0.6),
     'L0_attn_mn_b': (0.0, 0.525)}
    factors = {'L0_attn_conv_w': 8.0,
     'L0_attn_Wig': 8.0,
     'L0_attn_Wog': 8.0,
     'L0_ffn_gate_weight': 8.0,
     'L0_ffn_gate_w': 8.0,
     'L0_ffn_up_w': 8.0,
     'L0_ffn_down_w': 8.0,
     'L0_ffn_sh_gate_w': 4.015,
     'L0_ffn_sh_up_w': 3.979,
     'L0_ffn_sh_down_w': 3.979}
    for name, (base, spread) in spreads.items():
        noise = np.random.default_rng([zlib.crc32(name.encode()), seed]).standard_normal(out[name].shape)
        drawn = base * np.exp(spread * noise) if base else spread * noise
        out[name] = jnp.asarray(drawn.astype(out[name].dtype))
    for name, factor in factors.items():
        out[name] = (out[name] * factor).astype(out[name].dtype)
    return out
```

```python
from contextlib import ExitStack

import concourse.bass as bass
from concourse import mybir
from concourse.alu_op_type import AluOpType as ALU

F32 = mybir.dt.float32
F16 = mybir.dt.float16
BF16 = mybir.dt.bfloat16
I32 = mybir.dt.int32
ACT = mybir.ActivationFunctionType
AX_X = mybir.AxisListType.X

P = 128
SEQ, DM, CTX = 64, 256, 64
KC = DM // P
TOK = 256
TT = TOK // P
NB = TOK // SEQ
HEADS, HD = 16, 16
KVH, G, HQ = 8, 4, 8
NPAIR = KVH // 2
EXPERTS, FEXP, FSHARED = 8, 176, 352
FT = 14
FTR = EXPERTS * FEXP // P
FPAD = FT * P
assert FTR * P == EXPERTS * FEXP and FPAD >= FTR * P + FSHARED
CONV = 4
EPS = 1e-5

SX = 16.0
SW = 64.0
SP_ = SX * SW
SS = 2.0 * SX
SG = SS * SW
SM = 2.0 * SP_
SN = 8.0
SK = 16.0
SH = 4.0
MAGIC = 1597463007.0
START = 16


class Signal:

    def __init__(self, sem, per):
        self.sem, self.per = sem, per

    def at(self, block, k):
        return block * self.per + (k + START)


def build(nc, a):
    ctx = ExitStack()
    with ctx:
        def sb(name, shape, dt=F32):
            return ctx.enter_context(nc.sbuf_tensor(name, shape, dt))

        def bank(name):
            return ctx.enter_context(nc.psum_tensor(name, [P, 512], F32))

        signals = []

        def signal(name, per=1):
            s = Signal(ctx.enter_context(nc.semaphore(name)), per)
            signals.append(s)
            return s

        bank_a = [bank("bank_a0"), bank("bank_a1")]
        bank_b = [bank("bank_b0"), bank("bank_b1")]
        bank_v = bank("bank_v")
        bank_gu = [bank("bank_gu0"), bank("bank_gu1")]
        bank_dn = bank("bank_dn")

        wqkv = [sb(f"wqkv_{p}", [P, KC, 768], F16) for p in "hl"]
        wgate = [sb(f"wgate_{p}", [P, KC, 528], F16) for p in "hl"]
        wo = [sb(f"wo_{p}", [P, KC, DM], F16) for p in "hl"]
        wrt = [sb(f"wrt_{p}", [P, KC, EXPERTS], F16) for p in "hl"]
        wfg = [sb(f"wfg_{p}", [P, KC, FPAD], F16) for p in "hl"]
        wfu = [sb(f"wfu_{p}", [P, KC, FPAD], F16) for p in "hl"]
        wfd = [sb(f"wfd_{p}", [P, FT, DM], F16) for p in "hl"]
        bias2 = sb("bias2", [33, 528], F16)
        ones2 = sb("ones2", [33, P], F16)
        stage = [sb(f"stage{n}", [P, FPAD]) for n in range(2)]
        bias_f = sb("bias_f", [33, 528])
        convw = sb("convw", [P, KC, CONV])
        convb = sb("convb", [P, KC])
        convb16 = sb("convb16", [P, KC])
        rows = sb("rows", [P, 4, DM])
        gn8 = sb("gn8", [P, 2, DM])
        ident = sb("ident", [P, P])
        ident16 = sb("ident16", [P, P], F16)
        center = sb("center", [P, P])
        kmask = sb("kmask", [P, KVH, SEQ], F16)
        maxsel = sb("maxsel", [NB * KVH, NB * NPAIR, P], BF16)
        wsel = sb("wsel", [2 * EXPERTS, FTR, P], F16)
        tri = sb("tri", [P, 80])
        tri4 = tri[:, 0:16].rearrange("p (a b) -> p a b", b=4)
        tri8 = tri[:, 16:80].rearrange("p (a b) -> p a b", b=8)
        power = sb("power", [P, TT])

        x_in = sb("x_in", [P, TT, DM])
        x_res = sb("x_res", [P, TT, DM])
        st1 = sb("st1", [P, TT, 6]); mv1 = sb("mv1", [P, TT, 2]); ve1 = sb("ve1", [P, TT]); rs1 = sb("rs1", [P, TT])
        xn = sb("xn", [P, TT, DM])
        xt_h = sb("xt_h", [P, KC, TOK], F16); xt_l = sb("xt_l", [P, KC, TOK], F16)
        cacc = sb("cacc", [P, KC, NB, SEQ])
        cth = sb("cth", [P, KC, TOK]); csil = sb("csil", [P, KC, TOK])
        ct_h = sb("ct_h", [P, KC, TOK], F16); ct_l = sb("ct_l", [P, KC, TOK], F16)
        qk = sb("qk", [P, TT, 512]); qk_sq = sb("qk_sq", [P, TT, 512])
        gate_t = sb("gate_t", [P, TT, 512])
        gam = sb("gam", [P, TT, DM])
        bv = sb("bv", [P, TT, DM]); bkn = sb("bkn", [P, TT, DM]); qn = sb("qn", [P, TT, DM])
        ss_qk = sb("ss_qk", [P, TT, 32]); r_qk = sb("r_qk", [P, TT, 32]); t_qk = sb("t_qk", [P, TT, 32])
        at = sb("at", [P, TT, KC, 2, SEQ])
        memt = sb("memt", [P, TT, KC, P])
        msq = qk_sq[:, 0, :].rearrange("p (t d) -> p t d", t=TT); ss_m = sb("ss_m", [P, TT, HEADS]); v_m = sb("v_m", [P, TT, HEADS])
        r_m = sb("r_m", [P, TT, HEADS]); t_m = sb("t_m", [P, TT, HEADS])
        m1 = sb("m1", [P, TT, DM]); o1 = sb("o1", [P, TT, DM])
        sum_o = sb("sum_o", [P, TT, HEADS]); oc = sb("oc", [P, TT, DM]); osq = qk_sq[:, 1, :].rearrange("p (t d) -> p t d", t=TT)
        ss_o = sb("ss_o", [P, TT, HEADS]); v_o = sb("v_o", [P, TT, HEADS])
        r_o = sb("r_o", [P, TT, HEADS]); t_o = sb("t_o", [P, TT, HEADS])
        o2 = sb("o2", [P, TT, DM]);  o5 = sb("o5", [P, TT, DM])
        ot_h = sb("ot_h", [P, KC, TOK], F16); ot_l = sb("ot_l", [P, KC, TOK], F16)
        x1 = sb("x1", [P, TT, DM])
        ctxs = sb("ctxs", [P, NB, CTX])
        k2 = sb("k2", [SEQ, NB, 3 * CTX], F16)
        kt = sb("kt", [P, NB, SEQ], F16); ktl = sb("ktl", [CTX, NB, SEQ], F16)
        kb = sb("kb", [P, NB, KVH, SEQ], F16)
        kl = sb("kl", [CTX, NB, KVH, SEQ], F16)
        vblk = sb("vblk", [P, NB, NPAIR, 32])
        st2 = sb("st2", [P, TT, 6]); mv2 = sb("mv2", [P, TT, 2]); ve2 = sb("ve2", [P, TT]); rs2 = sb("rs2", [P, TT])
        xq = sb("xq", [P, TT, DM])
        qs = sb("qs", [P, NB, G, SEQ], F16)
        mx = sb("mx", [P, 2, NB, KVH])
        mxt = sb("mxt", [NB * KVH, 2 * P], BF16)
        prob = [sb(f"prob{n}", [P, 512]) for n in range(2)]
        avs = sb("avs", [P, TT, G, 2, SEQ])
        orec = sb("orec", [P, TT, G, NPAIR, 2])
        oatt = sb("oatt", [P, TT, DM])
        x2 = sb("x2", [P, TT, DM])
        x3 = sb("x3", [P, TT, DM])
        st3 = sb("st3", [P, TT, 6]); mv3 = sb("mv3", [P, TT, 2]); ve3 = sb("ve3", [P, TT]); rs3 = sb("rs3", [P, TT])
        hn = sb("hn", [P, TT, DM])
        ht_h = sb("ht_h", [P, KC, TOK], F16); ht_l = sb("ht_l", [P, KC, TOK], F16)
        lmax = sb("lmax", [P, TT]); lneg = sb("lneg", [P, TT]); lexp = sb("lexp", [P, TT, EXPERTS])
        lsum = sb("lsum", [P, TT]); lrec = sb("lrec", [P, TT]); prb = sb("prb", [P, TT, EXPERTS])
        gs = sb("gs", [P, TT, 4]); ggt = sb("ggt", [P, TT, 4, 4]); geq = sb("geq", [P, TT, 4, 4])
        geq2 = sb("geq2", [P, TT, 4, 4]); gcnt = sb("gcnt", [P, TT, 4, 4]); grank = sb("grank", [P, TT * 4])
        pm = sb("pm", [P, TT, EXPERTS])
        egt = sb("egt", [P, TT, 8, 8]); eeq = sb("eeq", [P, TT, 8, 8]); eeq2 = sb("eeq2", [P, TT, 8, 8])
        ecnt = sb("ecnt", [P, TT, 8, 8]); erank = sb("erank", [P, TT * 8]); wts = sb("wts", [P, TT, EXPERTS])
        whl = sb("whl", [P, TT, 16], F16)
        wt = sb("wt", [16, TOK], F16)
        wx = sb("wx", [P, FTR, TOK])
        ff_tanh = [sb(f"ff_tanh{n}", [P, TOK]) for n in range(2)]
        ff_g = [sb(f"ff_g{n}", [P, TOK]) for n in range(2)]
        ff_u = [sb(f"ff_u{n}", [P, TOK]) for n in range(2)]
        ff_w = [sb(f"ff_w{n}", [P, TOK]) for n in range(2)]
        hid_h = [sb(f"hid_h{n}", [P, TOK], F16) for n in range(2)]
        hid_l = [sb(f"hid_l{n}", [P, TOK], F16) for n in range(2)]
        y_sb = sb("y_sb", [P, TT, DM])

        def plain(name):
            return ctx.enter_context(nc.semaphore(name))

        cst_loaded = plain("cst_loaded")
        stage_loaded = [plain(f"stage_loaded{n}") for n in range(2)]
        stage_split = plain("stage_split")
        stage_high = plain("stage_high")
        cst_act = plain("cst_act")
        cst_dve = plain("cst_dve")
        cst_pool = plain("cst_pool")
        primed = plain("primed")
        held = plain("held")

        x_loaded = signal("x_loaded", 16)
        x_kept = signal("x_kept")
        ln1_stat = signal("ln1_stat", 5)
        ln1_rstd = signal("ln1_rstd")
        xn_ready = signal("xn_ready", TT)
        xt_ps = signal("xt_ps")
        xt_high = signal("xt_high")
        xt_low = signal("xt_low")
        conv_first = signal("conv_first", KC)
        conv_taps = signal("conv_taps", KC * (CONV - 1))
        conv_tanh = signal("conv_tanh")
        conv_silu = signal("conv_silu")
        ct_high = signal("ct_high")
        ct_low = signal("ct_low")
        qk_ps = signal("qk_ps", TT)
        vg_ps = signal("vg_ps", TT)
        gate_ps = signal("gate_ps", TT)
        qk_kept = signal("qk_kept", TT)
        qk_square = signal("qk_square", TT)
        gate_tanh = signal("gate_tanh", TT)
        gam_tanh = signal("gam_tanh", TT)
        v_gated = signal("v_gated", TT)
        qk_sums = signal("qk_sums", TT)
        qk_norm = signal("qk_norm", 12)
        bk_ready = signal("bk_ready")
        bkn_ready = signal("bkn_ready")
        qn_ready = signal("qn_ready")
        bg_ps = signal("bg_ps", TT)
        decay_ready = signal("decay_ready", TT)
        mem_ready = signal("mem_ready", TT * KC)
        ctr_ps = signal("ctr_ps")
        mem_square = signal("mem_square")
        mem_norm = signal("mem_norm", 13)
        m1_ready = signal("m1_ready")
        m2_ready = signal("m2_ready")
        m3_ready = signal("m3_ready")
        o1_ready = signal("o1_ready")
        out_center = signal("out_center", 2)
        out_square = signal("out_square")
        out_norm = signal("out_norm", 13)
        o2_ready = signal("o2_ready")
        o3_ready = signal("o3_ready")
        o4_ready = signal("o4_ready")
        o5_ready = signal("o5_ready")
        ot_ps = signal("ot_ps")
        ot_high = signal("ot_high")
        ot_low = signal("ot_low")
        mix_ps = signal("mix_ps")
        x1_ready = signal("x1_ready")
        ctx_loaded = signal("ctx_loaded", 32)
        k_high = signal("k_high")
        k_low = signal("k_low")
        v_block = signal("v_block", 2)
        kt_ps = signal("kt_ps")
        kt_kept = signal("kt_kept", 2)
        k_masked = signal("k_masked", 2)
        ln2_stat = signal("ln2_stat", 5)
        ln2_rstd = signal("ln2_rstd")
        xq_ready = signal("xq_ready", TT)
        qt_ps = signal("qt_ps", TT)
        q_high = signal("q_high", TT)
        q_low = signal("q_low", TT)
        row_ps = signal("row_ps", 2 * NB)
        row_max = signal("row_max", 2 * NB)
        maxt_ps = signal("maxt_ps")
        maxt_kept = signal("maxt_kept")
        col_ps = signal("col_ps", 2 * NB)
        col_exp = signal("col_exp", 2 * NB)
        val_ps = signal("val_ps", 2 * NB)
        val_kept = signal("val_kept", NB)
        att_ps = signal("att_ps", TT)
        att_norm = signal("att_norm", 3 * TT)
        x2_ready = signal("x2_ready", TT)
        ln3_stat = signal("ln3_stat", 5)
        ln3_rstd = signal("ln3_rstd")
        hn_ready = signal("hn_ready", TT)
        x2_kept = signal("x2_kept")
        ht_ps = signal("ht_ps")
        ht_high = signal("ht_high")
        ht_low = signal("ht_low")
        logit_ps = signal("logit_ps")
        logit_exp = signal("logit_exp", TT)
        route = signal("route", 20)
        wt_ps = signal("wt_ps")
        wt_kept = signal("wt_kept")
        wx_ps = signal("wx_ps", 6)
        wx_kept = signal("wx_kept", 6)
        gu_ps = signal("gu_ps", FT)
        tanh_done = signal("tanh_done", FT)
        silu_done = signal("silu_done", FT)
        up_done = signal("up_done", FT)
        weighted = signal("weighted", FTR)
        hid_high = signal("hid_high", FT)
        hid_low = signal("hid_low", FT)
        down_ps = signal("down_ps", FT)
        y_based = signal("y_based")
        y_ready = signal("y_ready")
        y_stored = signal("y_stored", 16)

        def flat(t, lo=0, hi=None):
            return t[:, lo:hi, :].rearrange("p a b -> p (a b)")

        loads = [(a["wqkv"], flat(wqkv[0]), flat(wqkv[1]), SW), (a["wgate"], flat(wgate[0]), flat(wgate[1]), SW),
                 (a["wo"], flat(wo[0]), flat(wo[1]), SW), (a["wrt"], flat(wrt[0]), flat(wrt[1]), SW),
                 (a["kmask"], flat(kmask), None, 1.0), (a["wsel"], flat(wsel), None, 1.0)]
        loads += [(a["maxsel"][:, 1024 * n:1024 * n + 1024], flat(maxsel, 8 * n, 8 * n + 8), None, 1.0) for n in range(2)]
        loads += [(a[name][:, c * FPAD:(c + 1) * FPAD], flat(w[0], c, c + 1), flat(w[1], c, c + 1), SW)
                  for name, w in (("wfg", wfg), ("wfu", wfu)) for c in range(KC)]
        loads += [(a["wfd"][:, c * FPAD:(c + 1) * FPAD], flat(wfd[0], 7 * c, 7 * c + 7), flat(wfd[1], 7 * c, 7 * c + 7), SW)
                  for c in range(2)]

        def splits_before(n):
            return sum(low is not None for _, _, low, _ in loads[:n])

        consts = [
            (ident[:, :], a["ident"]), (center[:, :], a["center"]), (tri[:, :], a["tri"]),
            (convw[:, :, :], a["convw"]), (convb[:, :], a["convb"]),
            (bias_f[:, :], a["bias"]),
        ] + [(rows[:, n, :], a[name].partition_broadcast(P)) for n, name in enumerate(("mn_w", "mn_b", "gn_w", "gn_b"))]

        x_blocks = a["x"].rearrange("(n t p) d -> n p t d", p=P, t=TT)
        y_blocks = a["y"].rearrange("(n t p) d -> n p t d", p=P, t=TT)
        c_blocks = a["ctx"].rearrange("(n b) t d -> n t b d", b=NB)
        BLOCKS = x_blocks.shape[0]
        LAG_B, LAG_R, LAG_E = 1, 2, 3

        block = ctx.enter_context(nc.Block())

        @block.sync
        def _(sp):
            def load_x(i):
                sp.wait_ge(xn_ready.sem, xn_ready.at(i, 0))
                sp.sem_inc(held, 1)
                sp.wait_ge(x_kept.sem, x_kept.at(i, 0))
                sp.sem_inc(held, 1)
                sp.dma_start(x_in[:, :, :], x_blocks[i]).then_inc(x_loaded.sem, 16)

            def load_ctx(i):
                sp.wait_ge(k_low.sem, k_low.at(i, 0))
                sp.sem_inc(held, 1)
                sp.wait_ge(v_block.sem, v_block.at(i, 0))
                sp.sem_inc(held, 1)
                sp.wait_ge(k_high.sem, k_high.at(i, 0))
                sp.sem_inc(held, 1)
                for half in range(2):
                    sp.dma_start(ctxs[64 * half:64 * half + 64, :, :], c_blocks[i]).then_inc(ctx_loaded.sem, 16)

            def store_y(i):
                sp.wait_ge(y_ready.sem, y_ready.at(i, 1))
                sp.sem_inc(held, 1)
                sp.dma_start(y_blocks[i], y_sb[:, :, :]).then_inc(y_stored.sem, 16)

            sp.wait_ge(primed, 1)
            load_x(0)
            for dst, src in consts:
                sp.dma_start(dst, src).then_inc(cst_loaded, 16)
            for n, (src, _, _, _) in enumerate(loads):
                if n >= 2:
                    sp.wait_ge(stage_high, n - 1)
                    sp.wait_ge(stage_split, splits_before(n - 1))
                sp.dma_start(stage[n % 2][0:src.shape[0], 0:src.shape[1]], src).then_inc(stage_loaded[n % 2], 16)

            def turn(j):
                if not isinstance(j, int) or j + 1 < BLOCKS:
                    load_x(j + 1)
                if not isinstance(j, int) or j < BLOCKS:
                    load_ctx(j)
                if not isinstance(j, int) or j >= LAG_E:
                    store_y(j - LAG_E)

            for j in range(LAG_E):
                turn(j)
            with sp.Fori(LAG_E, BLOCKS - 1) as j:
                turn(j)
            for j in range(BLOCKS - 1, BLOCKS + LAG_E):
                turn(j)
            sp.wait_ge(y_stored.sem, y_stored.at(BLOCKS, 0))

        def stages(j):
            def has(lag):
                return j - lag if not isinstance(j, int) or 0 <= j - lag < BLOCKS else None
            return has(0), has(LAG_B), has(LAG_R), has(LAG_E)

        @block.gpsimd
        def _(pool):
            for s in signals:
                pool.sem_inc(s.sem, START)
            pool.sem_inc(primed, 1)
            pool.memset(power[:, :], -0.5).then_inc(cst_pool, 1)
            pool.memset(at[:, :, :, :, :], 0.0).then_inc(cst_pool, 1)
            pool.memset(vblk[:, :, :, :], 0.0).then_inc(cst_pool, 1)
            pool.memset(ones2[:, :], 0.0).then_inc(cst_pool, 1)
            pool.wait_ge(cst_pool, 4)
            pool.memset(vblk[0:64, :, :, 16:17], 1.0).then_inc(cst_pool, 1)
            pool.memset(vblk[64:128, :, :, 17:18], 1.0).then_inc(cst_pool, 1)
            pool.wait_ge(cst_pool, 6)
            pool.memset(ones2[0:1, :], SS).then_inc(cst_pool, 1)
            pool.memset(ones2[32:33, :], SS).then_inc(cst_pool, 1)

            def rstd(i, stat, done, ve, rs, free, free_k):
                pool.wait_ge(free.sem, free.at(i, free_k))
                pool.wait_ge(stat.sem, stat.at(i, 5))
                pool.tensor_tensor(rs[:, :], ve[:, :], power[:, :], ALU.pow).then_inc(done.sem, 1)

            def silu_low(i):
                pool.wait_ge(ct_high.sem, ct_high.at(i, 1))
                pool.wait_ge(conv_silu.sem, conv_silu.at(i, 1))
                pool.wait_ge(gate_ps.sem, gate_ps.at(i, 0))
                pool.tensor_tensor(ct_l[:, :, :], csil[:, :, :], ct_h[:, :, :], ALU.subtract).then_inc(ct_low.sem, 1)

            def keys_times_values(i):
                pool.wait_ge(v_gated.sem, v_gated.at(i, TT))
                pool.wait_ge(qk_kept.sem, qk_kept.at(i, TT))
                pool.tensor_tensor(bv[:, :, :], bv[:, :, :], qk[:, :, DM:2 * DM], ALU.mult).then_inc(bk_ready.sem, 1)

            def head_bcast(r, lo=0):
                return r[:, :, lo:lo + HEADS].unsqueeze(3).broadcast_to([P, TT, HEADS, HD])

            def by_head(t):
                return t.rearrange("p t (h d) -> p t h d", d=HD)

            def apply_qk_norm(i):
                pool.wait_ge(qk_norm.sem, qk_norm.at(i, 12))
                pool.wait_ge(bk_ready.sem, bk_ready.at(i, 1))
                pool.wait_ge(bg_ps.sem, bg_ps.at(i, 0))
                pool.tensor_tensor(by_head(bkn[:, :, :]), by_head(bv[:, :, :]), head_bcast(r_qk, HEADS),
                                   ALU.mult).then_inc(bkn_ready.sem, 1)
                pool.wait_ge(o1_ready.sem, o1_ready.at(i, 0))
                pool.tensor_tensor(by_head(qn[:, :, :]), by_head(qk[:, :, 0:DM]), head_bcast(r_qk, 0),
                                   ALU.mult).then_inc(qn_ready.sem, 1)

            def row(t, n):
                return t[:, n:n + 1, :].broadcast_to([P, TT, DM])

            def mem_affine(i):
                pool.wait_ge(m1_ready.sem, m1_ready.at(i, 1))
                pool.tensor_tensor(m1[:, :, :], m1[:, :, :], row(rows, 0), ALU.mult).then_inc(m2_ready.sem, 1)
                pool.wait_ge(m2_ready.sem, m2_ready.at(i, 1))
                pool.tensor_tensor(m1[:, :, :], m1[:, :, :], row(rows, 1), ALU.add).then_inc(m3_ready.sem, 1)
                pool.wait_ge(m3_ready.sem, m3_ready.at(i, 1))
                pool.wait_ge(qn_ready.sem, qn_ready.at(i, 1))
                pool.wait_ge(out_center.sem, out_center.at(i, 0))
                pool.tensor_tensor(o1[:, :, :], m1[:, :, :], qn[:, :, :], ALU.mult).then_inc(o1_ready.sem, 1)

            def out_affine(i):
                pool.wait_ge(o2_ready.sem, o2_ready.at(i, 1))
                pool.tensor_tensor(o2[:, :, :], o2[:, :, :], gn8[:, 0:1, :].broadcast_to([P, TT, DM]),
                                   ALU.mult).then_inc(o3_ready.sem, 1)
                pool.wait_ge(o3_ready.sem, o3_ready.at(i, 1))
                pool.tensor_tensor(o2[:, :, :], o2[:, :, :], gn8[:, 1:2, :].broadcast_to([P, TT, DM]),
                                   ALU.add).then_inc(o4_ready.sem, 1)

            def attention_residual(i, t):
                pool.wait_ge(att_norm.sem, att_norm.at(i, 3 * t + 3))
                pool.wait_ge(hn_ready.sem, hn_ready.at(i, 0))
                pool.wait_ge(x2_kept.sem, x2_kept.at(i, 0))
                pool.wait_ge(x1_ready.sem, x1_ready.at(i, 1))
                pool.tensor_tensor(x2[:, t, :], oatt[:, t, :], x1[:, t, :], ALU.add).then_inc(x2_ready.sem, 1)

            def weigh(i, k):
                pool.wait_ge(up_done.sem, up_done.at(i, k + 1))
                pool.wait_ge(wx_kept.sem, wx_kept.at(i, k // 2 + 1))
                b, n = (i, k - 1) if k >= 2 else (i - 1, FTR - k)
                pool.wait_ge(hid_high.sem, hid_high.at(b, n))
                pool.wait_ge(hid_low.sem, hid_low.at(b, n))
                pool.tensor_tensor(ff_w[k % 2][:, :], ff_u[k % 2][:, :], wx[:, k, :], ALU.mult).then_inc(weighted.sem, 1)

            def hidden_low(i, k):
                src = ff_w if k < FTR else ff_u
                pool.wait_ge(hid_high.sem, hid_high.at(i, k + 1))
                if k < FTR:
                    pool.wait_ge(weighted.sem, weighted.at(i, k + 1))
                pool.wait_ge(down_ps.sem, down_ps.at(i, k - 1))
                pool.tensor_tensor(hid_l[k % 2][:, :], src[k % 2][:, :], hid_h[k % 2][:, :],
                                   ALU.subtract).then_inc(hid_low.sem, 1)

            def turn(j):
                m, c, r, e = stages(j)
                if r is not None:
                    rstd(r, ln3_stat, ln3_rstd, ve3, rs3, hn_ready, 0)
                if m is not None:
                    rstd(m, ln1_stat, ln1_rstd, ve1, rs1, xn_ready, 0)
                    silu_low(m)
                    keys_times_values(m)
                    apply_qk_norm(m)
                    mem_affine(m)
                    out_affine(m)
                if c is not None:
                    rstd(c, ln2_stat, ln2_rstd, ve2, rs2, xq_ready, 0)
                    for t in range(TT):
                        attention_residual(c, t)
                if e is not None:
                    for k in range(FT):
                        if k < FTR:
                            weigh(e, k)
                        hidden_low(e, k)

            pool.wait_ge(cst_dve, 2)
            pool.wait_ge(cst_pool, 8)
            for j in range(LAG_E):
                turn(j)
            with pool.Fori(LAG_E, BLOCKS) as j:
                turn(j)
            for j in range(BLOCKS, BLOCKS + LAG_E):
                turn(j)

        @block.scalar
        def _(act):
            act.wait_ge(cst_loaded, 16 * len(consts))
            act.activation(ident16[:, :], ident[:, :], ACT.Copy).then_inc(cst_act, 1)
            act.activation(convb16[:, :], convb[:, :], ACT.Copy, scale=SX).then_inc(cst_act, 1)
            act.activation(bias2[:, :], bias_f[:, :], ACT.Copy, scale=SW).then_inc(cst_act, 1)
            for n, (src, high, _, scale) in enumerate(loads):
                act.wait_ge(stage_loaded[n % 2], 16 * (n // 2 + 1))
                act.activation(high, stage[n % 2][0:src.shape[0], 0:src.shape[1]], ACT.Copy, scale=scale).then_inc(stage_high, 1)

            def keep_x(i):
                act.wait_ge(x_loaded.sem, x_loaded.at(i, 16))
                act.wait_ge(x1_ready.sem, x1_ready.at(i, 0))
                act.activation(x_res[:, :, :], x_in[:, :, :], ACT.Copy).then_inc(x_kept.sem, 1)

            def x_transposed(i):
                act.wait_ge(xt_ps.sem, xt_ps.at(i, 1))
                act.wait_ge(vg_ps.sem, vg_ps.at(i, 0))
                psum = bank_a[0][:, :].rearrange("p (c t) -> p c t", c=KC)
                act.activation(xt_h[:, :, :], psum, ACT.Copy).then_inc(xt_high.sem, 1)
                act.wait_ge(conv_silu.sem, conv_silu.at(i, 0))
                for c in range(KC):
                    act.activation(cacc[:, c, :, :].rearrange("p b s -> p (b s)"), psum[:, c, :], ACT.Identity,
                                   scale=convw[:, c, CONV - 1:CONV], bias=convb16[:, c:c + 1]).then_inc(conv_first.sem, 1)

            def conv_activation(i):
                act.wait_ge(conv_taps.sem, conv_taps.at(i, KC * (CONV - 1)))
                act.wait_ge(conv_silu.sem, conv_silu.at(i, 0))
                act.activation(cth[:, :, :], cacc[:, :, :, :].rearrange("p c b s -> p c (b s)"), ACT.Tanh,
                               scale=0.5 / SX).then_inc(conv_tanh.sem, 1)

            def silu_high(i):
                act.wait_ge(conv_silu.sem, conv_silu.at(i, 1))
                act.wait_ge(gate_ps.sem, gate_ps.at(i, 0))
                act.activation(ct_h[:, :, :], csil[:, :, :], ACT.Copy).then_inc(ct_high.sem, 1)

            def qk_out(i, t):
                b = bank_a[(t + 1) % 2]
                act.wait_ge(qk_ps.sem, qk_ps.at(i, t + 1))
                act.wait_ge(qn_ready.sem, qn_ready.at(i, 0))
                act.activation(qk[:, t, :], b[:, :], ACT.Copy).then_inc(qk_kept.sem, 1)
                prior = out_norm if t else mem_norm
                act.wait_ge(prior.sem, prior.at(i, 0))
                act.activation(qk_sq[:, t, :], b[:, :], ACT.Square).then_inc(qk_square.sem, 1)

            def gamma_out(i, t):
                b = bank_a[t % 2]
                act.wait_ge(vg_ps.sem, vg_ps.at(i, t + 1))
                act.wait_ge(bg_ps.sem, bg_ps.at(i, 0))
                src = b[:, DM:DM + HEADS].unsqueeze(2).broadcast_to([P, HEADS, HD])
                act.activation(gam[:, t, :].rearrange("p (h d) -> p h d", d=HD), src, ACT.Tanh,
                               scale=0.5 / SG).then_inc(gam_tanh.sem, 1)

            def gates_out(i, t):
                b = bank_a[(t + 1) % 2]
                act.wait_ge(gate_ps.sem, gate_ps.at(i, t + 1))
                act.wait_ge(o5_ready.sem, o5_ready.at(i, 0))
                act.activation(gate_t[:, t, :], b[:, :], ACT.Tanh, scale=0.5 / SG).then_inc(gate_tanh.sem, 1)

            def decay(i, t):
                b = bank_a[(t + 1) % 2][:, DM:2 * DM].rearrange("p (c b s) -> p c b s", c=KC, b=2)
                act.wait_ge(bg_ps.sem, bg_ps.at(i, t + 1))
                act.wait_ge(mem_ready.sem, mem_ready.at(i, KC * (t + 1) - TT * KC))
                for c in range(KC):
                    ins = act.activation(at[:, t, c, :, 1:SEQ], b[:, c, :, 1:SEQ], ACT.Copy, scale=0.5, bias=0.5)
                ins.then_inc(decay_ready.sem, 1)

            def mem_squares(i):
                act.wait_ge(ctr_ps.sem, ctr_ps.at(i, 1))
                act.wait_ge(mem_norm.sem, mem_norm.at(i, 0))
                act.activation(msq[:, :, :], bank_a[1][:, :].rearrange("p (t d) -> p t d", t=TT),
                               ACT.Square).then_inc(mem_square.sem, 1)

            def out_squares(i):
                act.wait_ge(out_center.sem, out_center.at(i, 2))
                act.wait_ge(out_norm.sem, out_norm.at(i, 0))
                act.activation(osq[:, :, :], oc[:, :, :], ACT.Square).then_inc(out_square.sem, 1)

            def out_transposed(i):
                act.wait_ge(ot_ps.sem, ot_ps.at(i, 1))
                act.wait_ge(mix_ps.sem, mix_ps.at(i, 0))
                act.activation(ot_h[:, :, :], bank_a[0][:, :].rearrange("p (c t) -> p c t", c=KC),
                               ACT.Copy).then_inc(ot_high.sem, 1)

            def keys_values(i):
                act.wait_ge(ctx_loaded.sem, ctx_loaded.at(i, 32))
                act.wait_ge(kt_ps.sem, kt_ps.at(i, 0))
                act.activation(k2[:, :, 0:2 * CTX].rearrange("p b (r d) -> p b r d", r=2),
                               ctxs[0:SEQ, :, :].unsqueeze(2).broadcast_to([SEQ, NB, 2, CTX]),
                               ACT.Copy, scale=SK).then_inc(k_high.sem, 1)
                act.wait_ge(val_ps.sem, val_ps.at(i, 0))
                for half in range(2):
                    src = ctxs[64 * half:64 * half + 64, :, :].rearrange("p b (j h d) -> p b j h d", j=NPAIR, h=2)
                    act.activation(vblk[64 * half:64 * half + 64, :, :, 8 * half:8 * half + 8],
                                   src[:, :, :, half, :], ACT.Copy).then_inc(v_block.sem, 1)

            def keys_transposed(i):
                act.wait_ge(kt_ps.sem, kt_ps.at(i, 1))
                act.wait_ge(k_masked.sem, k_masked.at(i, 0))
                psum = bank_v[:, 0:256].bitcast(F16)
                act.activation(kt[:, :, :].rearrange("p b s -> p (b s)"), psum[:, 0:256], ACT.Copy).then_inc(kt_kept.sem, 1)
                act.activation(ktl[:, :, :].rearrange("p b s -> p (b s)"), psum[0:CTX, 256:512], ACT.Copy).then_inc(kt_kept.sem, 1)

            def queries_high(i, t):
                act.wait_ge(qt_ps.sem, qt_ps.at(i, t + 1))
                act.wait_ge(col_ps.sem, col_ps.at(i, 0))
                act.activation(qs[0:64, 2 * t:2 * t + 2, :, :],
                               bank_b[t][0:64, :].rearrange("p (g b s) -> p b g s", g=G, b=2),
                               ACT.Copy).then_inc(q_high.sem, 1)

            def maxima_transposed(i):
                act.wait_ge(maxt_ps.sem, maxt_ps.at(i, 1))
                act.wait_ge(col_ps.sem, col_ps.at(i, 0))
                act.activation(mxt[:, :], bank_v[0:NB * KVH, 0:256], ACT.Copy).then_inc(maxt_kept.sem, 1)

            def exps(i, n):
                act.wait_ge(col_ps.sem, col_ps.at(i, n + 1))
                act.wait_ge(val_ps.sem, val_ps.at(i, n - 1))
                act.activation(prob[n % 2][:, :], bank_b[n % 2][:, :], ACT.Exp,
                               scale=1.0 / (SX * SK * HQ ** 0.5)).then_inc(col_exp.sem, 1)

            def values_out(i, b):
                act.wait_ge(val_ps.sem, val_ps.at(i, 2 * b + 2))
                act.wait_ge(att_ps.sem, att_ps.at(i, b // 2 + 1 - TT))
                act.activation(avs[:, b // 2, :, b % 2, :],
                               bank_v[:, 256 * (b % 2):256 * (b % 2) + 256].rearrange("p (g s) -> p g s", g=G),
                               ACT.Copy).then_inc(val_kept.sem, 1)

            def keep_y(i):
                act.wait_ge(x2_kept.sem, x2_kept.at(i, 1))
                act.wait_ge(y_stored.sem, y_stored.at(i, 0))
                act.activation(y_sb[:, :, :], x3[:, :, :], ACT.Copy).then_inc(y_based.sem, 1)

            def keep_x2(i):
                act.wait_ge(x2_ready.sem, x2_ready.at(i, TT))
                act.wait_ge(y_based.sem, y_based.at(i, 0))
                act.activation(x3[:, :, :], x2[:, :, :], ACT.Copy).then_inc(x2_kept.sem, 1)

            def h_transposed(i):
                act.wait_ge(ht_ps.sem, ht_ps.at(i, 1))
                act.wait_ge(gu_ps.sem, gu_ps.at(i, 0))
                act.wait_ge(logit_ps.sem, logit_ps.at(i, 0))
                act.activation(ht_h[:, :, :], bank_a[0][:, :].rearrange("p (c t) -> p c t", c=KC),
                               ACT.Copy).then_inc(ht_high.sem, 1)

            def router_exp(i):
                act.wait_ge(route.sem, route.at(i, 2))
                for t in range(TT):
                    act.activation(lexp[:, t, :], bank_a[1][:, EXPERTS * t:EXPERTS * (t + 1)], ACT.Exp,
                                   scale=1.0 / SP_, bias=lneg[:, t:t + 1]).then_inc(logit_exp.sem, 1)

            def weights_transposed(i):
                act.wait_ge(wt_ps.sem, wt_ps.at(i, 1))
                act.wait_ge(wx_ps.sem, wx_ps.at(i, 0))
                act.activation(wt[:, :], bank_a[0][0:16, 0:128].bitcast(F16), ACT.Copy).then_inc(wt_kept.sem, 1)

            def weights_spread(i, n):
                act.wait_ge(wx_ps.sem, wx_ps.at(i, n + 1))
                w = min(2, FTR - 2 * n)
                act.wait_ge(weighted.sem, weighted.at(i - 1, 2 * n + w))
                act.activation(wx[:, 2 * n:2 * n + w, :].rearrange("p k t -> p (k t)"),
                               bank_a[(n + 1) % 2][:, 0:w * TOK], ACT.Copy).then_inc(wx_kept.sem, 1)

            def expert_tanh(i, k):
                act.wait_ge(gu_ps.sem, gu_ps.at(i, k + 1))
                act.wait_ge(silu_done.sem, silu_done.at(i, k - 1))
                act.activation(ff_tanh[k % 2][:, :], bank_gu[k % 2][:, 0:TOK], ACT.Tanh,
                               scale=0.5 / SP_).then_inc(tanh_done.sem, 1)

            def expert_high(i, k):
                if k < FTR:
                    act.wait_ge(weighted.sem, weighted.at(i, k + 1))
                else:
                    act.wait_ge(up_done.sem, up_done.at(i, k + 1))
                act.wait_ge(down_ps.sem, down_ps.at(i, k - 1))
                src = ff_w if k < FTR else ff_u
                act.activation(hid_h[k % 2][:, :], src[k % 2][:, :], ACT.Copy).then_inc(hid_high.sem, 1)

            def turn(j):
                m, c, r, e = stages(j)
                if e is not None:
                    keep_y(e)
                if r is not None:
                    keep_x2(r)
                if m is not None:
                    keep_x(m)
                    x_transposed(m)
                    conv_activation(m)
                    silu_high(m)
                    for t in range(TT):
                        qk_out(m, t)
                        gamma_out(m, t)
                        gates_out(m, t)
                    for t in range(TT):
                        decay(m, t)
                    mem_squares(m)
                    out_squares(m)
                    out_transposed(m)
                if c is not None:
                    keys_values(c)
                    keys_transposed(c)
                    for t in range(TT):
                        queries_high(c, t)
                    maxima_transposed(c)
                    for b in range(NB):
                        exps(c, 2 * b)
                        exps(c, 2 * b + 1)
                        values_out(c, b)
                if e is not None:
                    for k in range(FT):
                        expert_tanh(e, k)
                        expert_high(e, k)
                if r is not None:
                    h_transposed(r)
                    router_exp(r)
                    weights_transposed(r)
                    for n in range(6):
                        weights_spread(r, n)

            act.wait_ge(cst_pool, 8)
            act.wait_ge(primed, 1)
            for j in range(LAG_E):
                turn(j)
            with act.Fori(LAG_E, BLOCKS) as j:
                turn(j)
            for j in range(BLOCKS, BLOCKS + LAG_E):
                turn(j)

        @block.tensor
        def _(pe):
            pe.wait_ge(cst_loaded, 16 * len(consts))
            pe.wait_ge(cst_act, 3)
            pe.wait_ge(cst_dve, 2)
            pe.wait_ge(cst_pool, 8)

            def product(out, lhs, rhs, first=True, last=True):
                terms = [(l, r) for lp, rp in ((0, 0), (1, 0), (0, 1)) for l, r in zip(lhs[lp], rhs[rp])]
                for n, (l, r) in enumerate(terms):
                    ins = pe.matmul(out, l, r, start=first and n == 0, stop=last and n == len(terms) - 1,
                                    skip_group_check=True)
                return ins

            def chunks(pair, cols):
                return [[t[:, c, cols] for c in range(KC)] for t in pair]

            def turned(src, b):
                for t in range(TT):
                    for c in range(KC):
                        ins = pe.transpose(b[:, c * TOK + t * P:c * TOK + (t + 1) * P],
                                           src[:, t, c * P:(c + 1) * P], ident[:, :])
                return ins

            def turn_x(i, r_before):
                pe.wait_ge(xn_ready.sem, xn_ready.at(i, TT))
                pe.wait_ge(ot_low.sem, ot_low.at(i, 0))
                pe.wait_ge(ot_high.sem, ot_high.at(i, 0))
                if r_before is not None:
                    pe.wait_ge(wx_kept.sem, wx_kept.at(r_before, 6))
                turned(xn, bank_a[0]).then_inc(xt_ps.sem, 1)

            def project_qk(i, t, r_before):
                toks = slice(t * P, (t + 1) * P)
                pe.wait_ge(xt_high.sem, xt_high.at(i, 1))
                pe.wait_ge(xt_low.sem, xt_low.at(i, 1))
                if t == 0:
                    pe.wait_ge(x1_ready.sem, x1_ready.at(i, 0))
                    if r_before is not None:
                        pe.wait_ge(wx_kept.sem, wx_kept.at(r_before, 5))
                else:
                    pe.wait_ge(v_gated.sem, v_gated.at(i, t))
                    pe.wait_ge(gam_tanh.sem, gam_tanh.at(i, t))
                product(bank_a[(t + 1) % 2][:, 0:512], chunks((xt_h, xt_l), toks),
                        chunks(wqkv, slice(0, 512))).then_inc(qk_ps.sem, 1)

            def project_v_gamma(i, t):
                toks = slice(t * P, (t + 1) * P)
                b = bank_a[t % 2]
                if t == 0:
                    pe.wait_ge(conv_taps.sem, conv_taps.at(i, KC * (CONV - 1)))
                    pe.wait_ge(conv_first.sem, conv_first.at(i, KC))
                else:
                    pe.wait_ge(gate_tanh.sem, gate_tanh.at(i, t))
                product(b[:, 0:DM], chunks((xt_h, xt_l), toks), chunks(wqkv, slice(512, 768)))
                pe.wait_ge(ct_high.sem, ct_high.at(i, 1))
                pe.wait_ge(ct_low.sem, ct_low.at(i, 1))
                product(b[:, DM:DM + HEADS], chunks((ct_h, ct_l), toks), chunks(wgate, slice(512, 528)), last=False)
                pe.matmul(b[:, DM:DM + HEADS], ones2[:, :], bias2[:, 512:528], start=False, stop=True,
                          skip_group_check=True).then_inc(vg_ps.sem, 1)

            def project_gates(i, t):
                toks = slice(t * P, (t + 1) * P)
                b = bank_a[(t + 1) % 2]
                pe.wait_ge(qk_square.sem, qk_square.at(i, t + 1))
                product(b[:, 0:512], chunks((ct_h, ct_l), toks), chunks(wgate, slice(0, 512)), last=False)
                pe.matmul(b[:, 0:512], ones2[:, :], bias2[:, 0:512], start=False, stop=True,
                          skip_group_check=True).then_inc(gate_ps.sem, 1)

            def turn_b_gamma(i, t):
                b = bank_a[(t + 1) % 2]
                if t == 0:
                    pe.wait_ge(bkn_ready.sem, bkn_ready.at(i, 1))
                    pe.wait_ge(gam_tanh.sem, gam_tanh.at(i, TT))
                    pe.wait_ge(v_gated.sem, v_gated.at(i, TT))
                else:
                    pe.wait_ge(gate_tanh.sem, gate_tanh.at(i, TT))
                for n, src in enumerate((bkn, gam)):
                    for c in range(KC):
                        ins = pe.transpose(b[:, (KC * n + c) * P:(KC * n + c + 1) * P],
                                           src[:, t, c * P:(c + 1) * P], ident[:, :])
                ins.then_inc(bg_ps.sem, 1)

            def center_mem(i):
                pe.wait_ge(mem_ready.sem, mem_ready.at(i, TT * KC))
                for t in range(TT):
                    for c in range(KC):
                        ins = pe.matmul(bank_a[1][:, t * DM + c * P:t * DM + (c + 1) * P], memt[:, t, c, :],
                                        center[:, :], start=True, stop=True, skip_group_check=True)
                ins.then_inc(ctr_ps.sem, 1)

            def turn_out(i):
                pe.wait_ge(o5_ready.sem, o5_ready.at(i, 1))
                turned(o5, bank_a[0]).then_inc(ot_ps.sem, 1)

            def project_out(i):
                pe.wait_ge(ot_high.sem, ot_high.at(i, 1))
                pe.wait_ge(ot_low.sem, ot_low.at(i, 1))
                pe.wait_ge(m1_ready.sem, m1_ready.at(i, 1))
                for t in range(TT):
                    ins = product(bank_a[1][:, t * DM:(t + 1) * DM], chunks((ot_h, ot_l), slice(t * P, (t + 1) * P)),
                                  chunks(wo, slice(0, DM)))
                ins.then_inc(mix_ps.sem, 1)

            def turn_keys(i):
                pe.wait_ge(k_high.sem, k_high.at(i, 1))
                pe.wait_ge(k_low.sem, k_low.at(i, 1))
                pe.wait_ge(val_kept.sem, val_kept.at(i, 0))
                pe.sem_inc(held, 1)
                psum = bank_v[:, 0:256].bitcast(F16)
                for b in range(NB):
                    pe.transpose(psum[:, SEQ * b:SEQ * (b + 1)], k2[:, b, 0:2 * CTX], ident16[0:SEQ, 0:SEQ])
                    ins = pe.transpose(psum[0:CTX, 256 + SEQ * b:256 + SEQ * (b + 1)], k2[:, b, 2 * CTX:3 * CTX],
                                       ident16[0:SEQ, 0:SEQ])
                ins.then_inc(kt_ps.sem, 1)

            def turn_queries(i, t):
                pe.wait_ge(xq_ready.sem, xq_ready.at(i, t + 1))
                pe.wait_ge(att_norm.sem, att_norm.at(i, 3 * (t + 1) - 3 * TT))
                pe.sem_inc(held, 1)
                for g in range(G):
                    ins = pe.transpose(bank_b[t][0:64, g * P:(g + 1) * P], xq[:, t, g * CTX:(g + 1) * CTX], ident[:, :])
                ins.then_inc(qt_ps.sem, 1)

            def scores_by_row(i, n):
                b, gp = n // 2, n % 2
                if n == 0:
                    pe.wait_ge(k_masked.sem, k_masked.at(i, 2))
                    pe.wait_ge(q_low.sem, q_low.at(i, TT))
                elif n >= 2:
                    pe.wait_ge(row_max.sem, row_max.at(i, n - 1))
                pe.matmul(bank_b[n % 2][:, :], qs[0:64, b, 2 * gp:2 * gp + 2, :].rearrange("p g s -> p (g s)"),
                          kb[0:64, b, :, :].rearrange("p h s -> p (h s)"), start=True, stop=True,
                          skip_group_check=True).then_inc(row_ps.sem, 1)

            def turn_maxima(i):
                pe.wait_ge(row_max.sem, row_max.at(i, 2 * NB))
                pe.wait_ge(kt_kept.sem, kt_kept.at(i, 2))
                for gp in range(2):
                    ins = pe.transpose(bank_v[0:NB * KVH, gp * P:(gp + 1) * P],
                                       mx[:, gp, :, :].rearrange("p b h -> p (b h)"), ident[:, :])
                ins.then_inc(maxt_ps.sem, 1)

            def scores_by_column(i, n):
                b, jp = n // 2, n % 2
                if n == 0:
                    pe.wait_ge(maxt_kept.sem, maxt_kept.at(i, 1))
                if n >= 2:
                    pe.wait_ge(col_exp.sem, col_exp.at(i, n - 1))
                q = qs[:, b, :, :].rearrange("p g s -> p (g s)")
                for h in range(2):
                    j = 2 * jp + h
                    out = bank_b[n % 2][:, 256 * h:256 * h + 256]
                    pe.matmul(out, kb[:, b, 2 * j:2 * j + 2, :].rearrange("p h s -> p (h s)"), q,
                              start=True, stop=False, skip_group_check=True)
                    pe.matmul(out, kl[:, b, 2 * j:2 * j + 2, :].rearrange("p h s -> p (h s)"), q[0:64, :],
                              start=False, stop=False, skip_group_check=True)
                    ins = pe.matmul(out, maxsel[:, NPAIR * b + j, :], mxt[:, :], start=False, stop=True,
                                    skip_group_check=True)
                ins.then_inc(col_ps.sem, 1)

            def values(i, n):
                b, jp = n // 2, n % 2
                pe.wait_ge(col_exp.sem, col_exp.at(i, n + 1))
                if jp == 0:
                    pe.wait_ge(val_kept.sem, val_kept.at(i, b))
                    if b == 0:
                        pe.wait_ge(v_block.sem, v_block.at(i, 2))
                for h in range(2):
                    j = 2 * jp + h
                    ins = pe.matmul(bank_v[32 * j:32 * j + 32, 256 * (b % 2):256 * (b % 2) + 256], vblk[:, b, j, :],
                                    prob[n % 2][:, 256 * h:256 * h + 256], start=True, stop=True, skip_group_check=True)
                ins.then_inc(val_ps.sem, 1)

            def turn_values(i, t):
                pe.wait_ge(val_kept.sem, val_kept.at(i, 2 * t + 2))
                pe.wait_ge(col_exp.sem, col_exp.at(i, 2 * NB))
                for g in range(G):
                    ins = pe.transpose(bank_b[t][:, g * P:(g + 1) * P], avs[:, t, g, :, :].rearrange("p b s -> p (b s)"), ident[:, :])
                ins.then_inc(att_ps.sem, 1)

            def turn_h(i):
                pe.wait_ge(hn_ready.sem, hn_ready.at(i, TT))
                turned(hn, bank_a[0]).then_inc(ht_ps.sem, 1)

            def router_logits(i):
                pe.wait_ge(ht_high.sem, ht_high.at(i, 1))
                pe.wait_ge(ht_low.sem, ht_low.at(i, 1))
                for t in range(TT):
                    ins = product(bank_a[1][:, EXPERTS * t:EXPERTS * (t + 1)],
                                  chunks((ht_h, ht_l), slice(t * P, (t + 1) * P)), chunks(wrt, slice(0, EXPERTS)))
                ins.then_inc(logit_ps.sem, 1)

            def turn_weights(i):
                pe.wait_ge(route.sem, route.at(i, 20))
                psum = bank_a[0][0:16, 0:128].bitcast(F16)
                for t in range(TT):
                    ins = pe.transpose(psum[:, t * P:(t + 1) * P], whl[:, t, :], ident16[:, :])
                ins.then_inc(wt_ps.sem, 1)

            def spread_weights(i, n):
                if n == 0:
                    pe.wait_ge(wt_kept.sem, wt_kept.at(i, 1))
                    pe.wait_ge(logit_exp.sem, logit_exp.at(i, TT))
                if n >= 2:
                    pe.wait_ge(wx_kept.sem, wx_kept.at(i, n - 1))
                for k in range(2 * n, min(2 * n + 2, FTR)):
                    ins = pe.matmul(bank_a[(n + 1) % 2][:, (k % 2) * TOK:(k % 2 + 1) * TOK], wsel[:, k, :], wt[:, :],
                                    start=True, stop=True, skip_group_check=True)
                ins.then_inc(wx_ps.sem, 1)

            def gate_up(i, k):
                cols = slice(k * P, (k + 1) * P)
                if k == 0:
                    pe.wait_ge(ht_high.sem, ht_high.at(i, 1))
                    pe.wait_ge(ht_low.sem, ht_low.at(i, 1))
                pe.wait_ge(up_done.sem, up_done.at(i, k - 1))
                h = chunks((ht_h, ht_l), slice(0, TOK))
                product(bank_gu[k % 2][:, 0:TOK], chunks(wfg, cols), h)
                product(bank_gu[k % 2][:, TOK:2 * TOK], chunks(wfu, cols), h).then_inc(gu_ps.sem, 1)

            def down(i, k):
                pe.wait_ge(hid_high.sem, hid_high.at(i, k + 1))
                pe.wait_ge(hid_low.sem, hid_low.at(i, k + 1))
                if k == 0:
                    pe.wait_ge(y_ready.sem, y_ready.at(i, 0))
                for t in range(TT):
                    toks = slice(t * P, (t + 1) * P)
                    hh, hl = hid_h[k % 2], hid_l[k % 2]
                    for n, (l, r) in enumerate(((hh, wfd[0]), (hl, wfd[0]), (hh, wfd[1]))):
                        ins = pe.matmul(bank_dn[:, t * DM:(t + 1) * DM], l[:, toks], r[:, k, :],
                                        start=k == 0 and t == 0 and n == 0, stop=k == FT - 1 and n == 2,
                                        skip_group_check=True)
                ins.then_inc(down_ps.sem, 1)

            def turn(j):
                m, c, r, e = stages(j)
                r_before = stages(j - 1)[2]
                if m is not None:
                    turn_x(m, r_before)
                    for t in range(TT):
                        project_qk(m, t, r_before)
                        project_v_gamma(m, t)
                        project_gates(m, t)
                    for t in range(TT):
                        turn_b_gamma(m, t)
                    center_mem(m)
                    turn_out(m)
                    project_out(m)
                if c is not None:
                    turn_keys(c)
                    for t in range(TT):
                        turn_queries(c, t)
                    for n in range(2 * NB):
                        scores_by_row(c, n)
                    turn_maxima(c)
                    for n in range(2 * NB):
                        scores_by_column(c, n)
                        if n >= 1:
                            values(c, n - 1)
                    values(c, 2 * NB - 1)
                    for t in range(TT):
                        turn_values(c, t)
                if e is not None:
                    for k in range(FT):
                        gate_up(e, k)
                        if k >= 1:
                            down(e, k - 1)
                    down(e, FT - 1)
                if r is not None:
                    if m is not None:
                        pe.wait_ge(x1_ready.sem, x1_ready.at(m, 1))
                        pe.wait_ge(ot_low.sem, ot_low.at(m, 1))
                    elif r_before is not None:
                        pe.wait_ge(wx_kept.sem, wx_kept.at(r_before, 6))
                    turn_h(r)
                    router_logits(r)
                    turn_weights(r)
                    for n in range(6):
                        spread_weights(r, n)

            pe.wait_ge(stage_split, splits_before(len(loads)))
            pe.wait_ge(stage_high, len(loads))
            pe.wait_ge(primed, 1)
            for j in range(LAG_E):
                turn(j)
            with pe.Fori(LAG_E, BLOCKS) as j:
                turn(j)
            for j in range(BLOCKS, BLOCKS + LAG_E):
                turn(j)

        @block.vector
        def _(dve):
            dve.wait_ge(cst_loaded, 16 * len(consts))
            dve.tensor_scalar(gn8[:, :, :], rows[:, 2:4, :], SN, None, ALU.mult).then_inc(cst_dve, 1)
            dve.wait_ge(cst_act, 3)
            dve.scalar_tensor_tensor(bias2[32:33, :], bias_f[32:33, :], SW, bias2[32:33, :], ALU.mult,
                                     ALU.subtract).then_inc(cst_dve, 1)
            for n, (src, high, low, scale) in enumerate(loads):
                if low is not None:
                    dve.wait_ge(stage_high, n + 1)
                    dve.scalar_tensor_tensor(low, stage[n % 2][:, 0:src.shape[1]], scale, high, ALU.mult,
                                             ALU.subtract).then_inc(stage_split, 1)

            def inverse_root(i, chain, k, y, t, v, scale):
                def step(ins):
                    ins.then_inc(chain.sem, 1)

                dve.wait_ge(chain.sem, chain.at(i, k))
                step(dve.tensor_scalar(y.bitcast(I32), v.bitcast(I32), -0.5, MAGIC, ALU.mult, ALU.add))
                for n, s in enumerate((1.0, 0.25, 0.0625)):
                    dve.wait_ge(chain.sem, chain.at(i, k + 3 * n + 1))
                    step(dve.scalar_tensor_tensor(t, y, s, y, ALU.mult, ALU.mult))
                    dve.wait_ge(chain.sem, chain.at(i, k + 3 * n + 2))
                    step(dve.tensor_tensor(t, t, v, ALU.mult))
                    dve.wait_ge(chain.sem, chain.at(i, k + 3 * n + 3))
                    step(dve.scalar_tensor_tensor(y, t, -3.0, y, ALU.add, ALU.mult))
                dve.wait_ge(chain.sem, chain.at(i, k + 10))
                step(dve.tensor_scalar(y, y, -0.125 * scale, None, ALU.mult))

            def norm_stats(i, x, st, mv, ve, stat, ready, ready_k, rstd):
                dve.wait_ge(ready.sem, ready.at(i, ready_k))
                for t in range(TT):
                    dve.bn_stats(st[:, t, :], x[:, t, :]).then_inc(stat.sem, 1)
                for t in range(TT):
                    dve.wait_ge(stat.sem, stat.at(i, t + 1))
                    dve.sem_inc(held, 1)
                    dve.bn_aggr(mv[:, t, :], st[:, t, :]).then_inc(stat.sem, 1)
                dve.wait_ge(stat.sem, stat.at(i, 4))
                dve.wait_ge(rstd.sem, rstd.at(i, 0))
                dve.tensor_scalar(ve[:, :], mv[:, :, 1], 1.0 / SX ** 2, EPS / SX ** 2, ALU.mult,
                                  ALU.add).then_inc(stat.sem, 1)

            def norm_apply(i, x, mv, rs, out, rstd, done, free, free_k, view=lambda z: z, out_view=lambda z: z):
                dve.wait_ge(rstd.sem, rstd.at(i, 1))
                dve.wait_ge(free.sem, free.at(i, free_k))
                for t in range(TT):
                    dve.tensor_scalar(out_view(out[:, t, :]), view(x[:, t, :]), mv[:, t, 0:1], rs[:, t:t + 1], ALU.subtract,
                                      ALU.mult).then_inc(done.sem, 1)

            def x_low(i):
                dve.wait_ge(conv_first.sem, conv_first.at(i, KC))
                dve.wait_ge(xt_high.sem, xt_high.at(i, 1))
                psum = bank_a[0][:, :].rearrange("p (c t) -> p c t", c=KC)
                dve.wait_ge(vg_ps.sem, vg_ps.at(i, 0))
                dve.tensor_tensor(xt_l[:, :, :], psum, xt_h[:, :, :], ALU.subtract).then_inc(xt_low.sem, 1)

            def conv(i):
                psum = bank_a[0][:, :].rearrange("p (c b s) -> p c b s", c=KC, b=NB)
                n = 0
                for tap in range(1, CONV):
                    for c in range(KC):
                        if tap == 1:
                            dve.wait_ge(conv_first.sem, conv_first.at(i, c + 1))
                        else:
                            dve.wait_ge(conv_taps.sem, conv_taps.at(i, n - 1))
                        dve.scalar_tensor_tensor(cacc[:, c, :, tap:SEQ], psum[:, c, :, 0:SEQ - tap],
                                                 convw[:, c, CONV - 1 - tap:CONV - tap], cacc[:, c, :, tap:SEQ],
                                                 ALU.mult, ALU.add).then_inc(conv_taps.sem, 1)
                        n += 1

            def silu(i):
                dve.wait_ge(conv_tanh.sem, conv_tanh.at(i, 1))
                dve.wait_ge(ct_low.sem, ct_low.at(i, 0))
                dve.wait_ge(ct_high.sem, ct_high.at(i, 0))
                dve.scalar_tensor_tensor(csil[:, :, :], cth[:, :, :], 1.0, cacc[:, :, :, :].rearrange("p c b s -> p c (b s)"),
                                         ALU.add, ALU.mult).then_inc(conv_silu.sem, 1)

            def gate_values(i, t):
                dve.wait_ge(gate_tanh.sem, gate_tanh.at(i, t + 1))
                dve.wait_ge(vg_ps.sem, vg_ps.at(i, t + 1))
                dve.wait_ge(gam_tanh.sem, gam_tanh.at(i, t + 1))
                dve.wait_ge(bkn_ready.sem, bkn_ready.at(i, 0))
                dve.scalar_tensor_tensor(bv[:, t, :], gate_t[:, t, 0:DM], 1.0, bank_a[t % 2][:, 0:DM],
                                         ALU.add, ALU.mult).then_inc(v_gated.sem, 1)

            def qk_sum(i, t):
                dve.wait_ge(qk_square.sem, qk_square.at(i, t + 1))
                dve.wait_ge(qk_norm.sem, qk_norm.at(i, 0))
                dve.tensor_reduce(ss_qk[:, t, :], qk_sq[:, t, :].rearrange("p (h d) -> p h d", d=HD), AX_X,
                                  ALU.add).then_inc(qk_sums.sem, 1)

            def qk_lengths(i):
                dve.wait_ge(qk_sums.sem, qk_sums.at(i, TT))
                dve.wait_ge(qn_ready.sem, qn_ready.at(i, 0))
                ss = ss_qk[:, :, :].rearrange("p t h -> p (t h)")
                dve.tensor_scalar(ss, ss, SP_ ** 2 * 1e-24, None, ALU.max).then_inc(qk_norm.sem, 1)
                inverse_root(i, qk_norm, 1, r_qk[:, :, :].rearrange("p t h -> p (t h)"),
                             t_qk[:, :, :].rearrange("p t h -> p (t h)"), ss, 1.0)

            def scan(i, t):
                b = bank_a[(t + 1) % 2]
                dve.wait_ge(decay_ready.sem, decay_ready.at(i, t + 1))
                dve.wait_ge(ctr_ps.sem, ctr_ps.at(i, 0))
                for c in range(KC):
                    dve.tensor_tensor_scan(memt[:, t, c, :], at[:, t, c, :, :].rearrange("p b s -> p (b s)"),
                                           b[:, c * P:(c + 1) * P], 0.0, ALU.mult, ALU.add).then_inc(mem_ready.sem, 1)

            def head_norm(i, sq, ss, v, r, t, norm, squared, scale):
                dve.wait_ge(squared.sem, squared.at(i, 1))
                f = lambda z: z[:, :, :].rearrange("p t h -> p (t h)")
                dve.tensor_reduce(f(ss), sq[:, :, :].rearrange("p t (h d) -> p (t h) d", d=HD), AX_X,
                                  ALU.add).then_inc(norm.sem, 1)
                dve.wait_ge(norm.sem, norm.at(i, 1))
                dve.tensor_scalar(f(v), f(ss), 1.0 / HD, EPS * scale ** 2, ALU.mult, ALU.add).then_inc(norm.sem, 1)
                inverse_root(i, norm, 2, f(r), f(t), f(v), 1.0)

            def heads(t):
                return t.rearrange("p t (h d) -> p (t h) d", d=HD)

            def per_head(r):
                return r[:, :, :].rearrange("p t h -> p (t h)").unsqueeze(2).broadcast_to([P, TT * HEADS, HD])

            def mem_scaled(i):
                dve.wait_ge(mem_norm.sem, mem_norm.at(i, 13))
                dve.wait_ge(o1_ready.sem, o1_ready.at(i, 0))
                dve.tensor_tensor(heads(m1[:, :, :]), bank_a[1][:, :].rearrange("p (h d) -> p h d", d=HD), per_head(r_m),
                                  ALU.mult).then_inc(m1_ready.sem, 1)

            def center_out(i):
                dve.wait_ge(o1_ready.sem, o1_ready.at(i, 1))
                dve.tensor_reduce(sum_o[:, :, :].rearrange("p t h -> p (t h)"), heads(o1[:, :, :]), AX_X,
                                  ALU.add).then_inc(out_center.sem, 1)
                dve.wait_ge(out_center.sem, out_center.at(i, 1))
                dve.scalar_tensor_tensor(heads(oc[:, :, :]), per_head(sum_o), -1.0 / HD, heads(o1[:, :, :]), ALU.mult,
                                         ALU.add).then_inc(out_center.sem, 1)

            def out_scaled(i):
                dve.wait_ge(out_norm.sem, out_norm.at(i, 13))
                dve.wait_ge(o5_ready.sem, o5_ready.at(i, 0))
                dve.tensor_tensor(heads(o2[:, :, :]), heads(oc[:, :, :]), per_head(r_o), ALU.mult).then_inc(o2_ready.sem, 1)

            def gate_out(i):
                dve.wait_ge(o4_ready.sem, o4_ready.at(i, 1))
                dve.wait_ge(ot_ps.sem, ot_ps.at(i, 0))
                dve.scalar_tensor_tensor(o5[:, :, :], gate_t[:, :, DM:2 * DM], 1.0, o2[:, :, :], ALU.add,
                                         ALU.mult).then_inc(o5_ready.sem, 1)

            def out_low(i):
                dve.wait_ge(ot_high.sem, ot_high.at(i, 1))
                dve.wait_ge(mix_ps.sem, mix_ps.at(i, 0))
                dve.tensor_tensor(ot_l[:, :, :], bank_a[0][:, :].rearrange("p (c t) -> p c t", c=KC), ot_h[:, :, :],
                                  ALU.subtract).then_inc(ot_low.sem, 1)

            def mixer_residual(i):
                dve.wait_ge(mix_ps.sem, mix_ps.at(i, 1))
                dve.wait_ge(x_kept.sem, x_kept.at(i, 1))
                dve.wait_ge(x2_ready.sem, x2_ready.at(i, 0))
                dve.scalar_tensor_tensor(x1[:, :, :], bank_a[1][:, :].rearrange("p (t d) -> p t d", t=TT),
                                         1.0 / (2.0 * SN * SW), x_res[:, :, :], ALU.mult, ALU.add).then_inc(x1_ready.sem, 1)

            def keys_low(i):
                dve.wait_ge(k_high.sem, k_high.at(i, 1))
                dve.scalar_tensor_tensor(k2[:, :, 2 * CTX:3 * CTX], ctxs[0:SEQ, :, :], SK, k2[:, :, 0:CTX], ALU.mult,
                                         ALU.subtract).then_inc(k_low.sem, 1)

            def mask_keys(i):
                dve.wait_ge(kt_kept.sem, kt_kept.at(i, 2))
                dve.wait_ge(col_ps.sem, col_ps.at(i, 0))
                for src, dst, rows_ in ((kt, kb, P), (ktl, kl, CTX)):
                    dve.tensor_tensor(dst[:, :, :, :], src[:, :, :].unsqueeze(2).broadcast_to([rows_, NB, KVH, SEQ]),
                                      kmask[0:rows_, :, :].unsqueeze(1).broadcast_to([rows_, NB, KVH, SEQ]),
                                      ALU.mult).then_inc(k_masked.sem, 1)

            def queries_low(i, t):
                dve.wait_ge(q_high.sem, q_high.at(i, t + 1))
                dve.tensor_tensor(qs[64:128, 2 * t:2 * t + 2, :, :].rearrange("p b g s -> p g b s"),
                                  bank_b[t][0:64, :].rearrange("p (g b s) -> p g b s", g=G, b=2),
                                  qs[0:64, 2 * t:2 * t + 2, :, :].rearrange("p b g s -> p g b s"),
                                  ALU.subtract).then_inc(q_low.sem, 1)

            def maxima(i, n):
                b, gp = n // 2, n % 2
                dve.wait_ge(row_ps.sem, row_ps.at(i, n + 1))
                if n == 0:
                    dve.wait_ge(maxt_ps.sem, maxt_ps.at(i, 0))
                dve.tensor_reduce(mx[:, gp, b, :], bank_b[n % 2][:, :].rearrange("p (h s) -> p h s", s=SEQ), AX_X,
                                  ALU.max).then_inc(row_max.sem, 1)

            def attention_norm(i, t):
                cols = bank_b[t][:, :].rearrange("p (g j m) -> p g j m", g=G, j=NPAIR)
                dve.wait_ge(att_ps.sem, att_ps.at(i, t + 1))
                dve.wait_ge(x2_ready.sem, x2_ready.at(i, t + 1 - TT))
                dve.reciprocal(orec[:, t, :, :, :], cols[:, :, :, 16:18]).then_inc(att_norm.sem, 1)
                dve.wait_ge(att_norm.sem, att_norm.at(i, 3 * t + 1))
                out = oatt[:, t, :].rearrange("p (j h g d) -> p g j h d", j=NPAIR, h=2, g=G)
                for h in range(2):
                    dve.tensor_tensor(out[:, :, :, h, :], cols[:, :, :, 8 * h:8 * h + 8],
                                      orec[:, t, :, :, h:h + 1].broadcast_to([P, G, NPAIR, HQ]),
                                      ALU.mult).then_inc(att_norm.sem, 1)

            def h_low(i):
                dve.wait_ge(ht_high.sem, ht_high.at(i, 1))
                dve.wait_ge(gu_ps.sem, gu_ps.at(i, 0))
                dve.tensor_tensor(ht_l[:, :, :], bank_a[0][:, :].rearrange("p (c t) -> p c t", c=KC), ht_h[:, :, :],
                                  ALU.subtract).then_inc(ht_low.sem, 1)

            def routing(i):
                done = [0]

                def after(ins):
                    ins.then_inc(route.sem, 1)
                    done[0] += 1
                    dve.wait_ge(route.sem, route.at(i, done[0]))

                logits = bank_a[1][:, 0:TT * EXPERTS].rearrange("p (t e) -> p t e", e=EXPERTS)
                dve.wait_ge(logit_ps.sem, logit_ps.at(i, 1))
                after(dve.tensor_reduce(lmax[:, :], logits, AX_X, ALU.max))
                after(dve.tensor_scalar(lneg[:, :], lmax[:, :], -1.0 / SP_, None, ALU.mult))
                dve.wait_ge(logit_exp.sem, logit_exp.at(i, TT))
                after(dve.tensor_reduce(lsum[:, :], lexp[:, :, :], AX_X, ALU.add))
                after(dve.reciprocal(lrec[:, :], lsum[:, :]))
                after(dve.tensor_tensor(prb[:, :, :], lexp[:, :, :], lrec[:, :].unsqueeze(2).broadcast_to([P, TT, EXPERTS]),
                                        ALU.mult))
                after(dve.tensor_reduce(gs[:, :, :].rearrange("p t g -> p (t g)"),
                                        prb[:, :, :].rearrange("p t (g e) -> p (t g) e", e=2), AX_X, ALU.max))

                def rank(v, gt, eq, eq2, cnt, out, tri_n, n):
                    shape = [P, TT, n, n]
                    other, own = v.unsqueeze(2).broadcast_to(shape), v.unsqueeze(3).broadcast_to(shape)
                    after(dve.tensor_tensor(gt[:, :, :, :], other, own, ALU.is_gt))
                    after(dve.tensor_tensor(eq[:, :, :, :], other, own, ALU.is_equal))
                    after(dve.tensor_tensor(eq2[:, :, :, :], eq[:, :, :, :], tri_n.unsqueeze(1).broadcast_to(shape), ALU.mult))
                    after(dve.tensor_tensor(cnt[:, :, :, :], gt[:, :, :, :], eq2[:, :, :, :], ALU.add))
                    after(dve.tensor_reduce(out[:, :], cnt[:, :, :, :].rearrange("p t a b -> p (t a) b"), AX_X, ALU.add))

                rank(gs[:, :, :], ggt, geq, geq2, gcnt, grank, tri4, 4)
                after(dve.scalar_tensor_tensor(pm[:, :, :].rearrange("p t (g e) -> p (t g) e", e=2),
                                               grank[:, :].unsqueeze(2).broadcast_to([P, TT * 4, 2]), 2.0,
                                               prb[:, :, :].rearrange("p t (g e) -> p (t g) e", e=2), ALU.is_lt, ALU.mult))
                rank(pm[:, :, :], egt, eeq, eeq2, ecnt, erank, tri8, 8)
                after(dve.scalar_tensor_tensor(wts[:, :, :].rearrange("p t e -> p (t e)"), erank[:, :], 2.0,
                                               pm[:, :, :].rearrange("p t e -> p (t e)"), ALU.is_lt, ALU.mult))
                dve.wait_ge(wt_ps.sem, wt_ps.at(i, 0))
                after(dve.tensor_scalar(whl[:, :, 0:8], wts[:, :, :], SW, None, ALU.mult))
                dve.scalar_tensor_tensor(whl[:, :, 8:16], wts[:, :, :], SW, whl[:, :, 0:8], ALU.mult,
                                         ALU.subtract).then_inc(route.sem, 1)

            def expert_silu(i, k):
                dve.wait_ge(tanh_done.sem, tanh_done.at(i, k + 1))
                dve.scalar_tensor_tensor(ff_g[k % 2][:, :], ff_tanh[k % 2][:, :], 1.0, bank_gu[k % 2][:, 0:TOK], ALU.add,
                                         ALU.mult).then_inc(silu_done.sem, 1)

            def expert_up(i, k):
                scale = SH / (2.0 * SP_ ** 2) * (4.0 if k < FTR else 1.0)
                dve.wait_ge(silu_done.sem, silu_done.at(i, k + 1))
                b, n = (i, k - 2) if k >= 2 else (i - 1, k - 2 + FT)
                if n < FTR:
                    dve.wait_ge(weighted.sem, weighted.at(b, n + 1))
                else:
                    dve.wait_ge(hid_low.sem, hid_low.at(b, n + 1))
                dve.scalar_tensor_tensor(ff_u[k % 2][:, :], ff_g[k % 2][:, :], scale, bank_gu[k % 2][:, TOK:2 * TOK],
                                         ALU.mult, ALU.mult).then_inc(up_done.sem, 1)

            def expert_residual(i):
                dve.wait_ge(down_ps.sem, down_ps.at(i, FT))
                dve.wait_ge(y_based.sem, y_based.at(i, 1))
                dve.scalar_tensor_tensor(y_sb[:, :, :], bank_dn[:, :].rearrange("p (t d) -> p t d", t=TT),
                                         1.0 / (SH * SW), y_sb[:, :, :], ALU.mult, ALU.add).then_inc(y_ready.sem, 1)

            def turn(j):
                m, c, r, e = stages(j)
                if r is not None:
                    norm_stats(r, x2, st3, mv3, ve3, ln3_stat, x2_ready, TT, ln3_rstd)
                    norm_apply(r, x2, mv3, rs3, hn, ln3_rstd, hn_ready, ht_ps, 0)
                if m is not None:
                    norm_stats(m, x_in, st1, mv1, ve1, ln1_stat, x_loaded, 16, ln1_rstd)
                    norm_apply(m, x_in, mv1, rs1, xn, ln1_rstd, xn_ready, xt_ps, 0)
                    x_low(m)
                    conv(m)
                    silu(m)
                    for t in range(TT):
                        qk_sum(m, t)
                        gate_values(m, t)
                    qk_lengths(m)
                    for t in range(TT):
                        scan(m, t)
                    head_norm(m, msq, ss_m, v_m, r_m, t_m, mem_norm, mem_square, SM)
                    mem_scaled(m)
                    center_out(m)
                    head_norm(m, osq, ss_o, v_o, r_o, t_o, out_norm, out_square, 1.0)
                    out_scaled(m)
                    gate_out(m)
                    out_low(m)
                if c is not None:
                    keys_low(c)
                    mask_keys(c)
                    norm_stats(c, x1, st2, mv2, ve2, ln2_stat, x1_ready, 1, ln2_rstd)
                    norm_apply(c, x1, mv2, rs2, xq, ln2_rstd, xq_ready, qt_ps, 0,
                               view=lambda z: z.rearrange("p (h g d) -> p h g d", h=KVH, g=G),
                               out_view=lambda z: z.rearrange("p (g h d) -> p h g d", h=KVH, g=G))
                    for t in range(TT):
                        queries_low(c, t)
                    for n in range(2 * NB):
                        maxima(c, n)
                    for t in range(TT):
                        attention_norm(c, t)
                if m is not None:
                    mixer_residual(m)
                if e is not None:
                    for k in range(FT):
                        expert_silu(e, k)
                        expert_up(e, k)
                    expert_residual(e)
                if r is not None:
                    h_low(r)
                    routing(r)

            dve.wait_ge(stage_high, len(loads))
            dve.wait_ge(primed, 1)
            for j in range(LAG_E):
                turn(j)
            with dve.Fori(LAG_E, BLOCKS) as j:
                turn(j)
            for j in range(BLOCKS, BLOCKS + LAG_E):
                turn(j)


def kernel(x, ctx_512, L0_attn_Wq, L0_attn_Wk, L0_attn_Wv, L0_attn_Wo, L0_attn_conv_w, L0_attn_conv_b,
           L0_attn_Wig, L0_attn_b_ig, L0_attn_Wog, L0_attn_b_og, L0_attn_Wg, L0_attn_b_g, L0_attn_gn_w,
           L0_attn_gn_b, L0_attn_mn_w, L0_attn_mn_b, L0_ffn_gate_weight, L0_ffn_gate_w, L0_ffn_up_w,
           L0_ffn_down_w, L0_ffn_sh_gate_w, L0_ffn_sh_up_w, L0_ffn_sh_down_w):
    import numpy as np
    import concourse.bacc as bacc
    from concourse.bass_utils import run_bass_kernel_spmd

    arr = np.asarray

    def by_partition(w):
        return np.ascontiguousarray(w.reshape(-1, P, w.shape[1]).transpose(1, 0, 2).reshape(P, -1))

    def padded(w, n):
        return np.concatenate([w, np.zeros((n - w.shape[0], w.shape[1]), w.dtype)], 0)

    def hidden_rows(routed, shared):
        return padded(np.concatenate([routed.reshape(-1, DM), shared], 0), FPAD)

    down = padded(np.concatenate([arr(L0_ffn_down_w).transpose(0, 2, 1).reshape(-1, DM), arr(L0_ffn_sh_down_w).T], 0), FPAD)

    eye = np.eye(P, dtype=np.float32)
    same_head = np.kron(np.eye(P // HD, dtype=np.float32), np.ones((HD, HD), np.float32))
    kmask = np.zeros((P, KVH, SEQ), np.float32)
    for p in range(P):
        kmask[p, (p % CTX) // HQ] = 1.0
    maxsel = np.zeros((NB, KVH, NB, NPAIR, 2, SEQ), np.float32)
    for b in range(NB):
        for h in range(KVH):
            maxsel[b, h, b, h // 2, h % 2] = -1.0
    wsel = np.zeros((2, EXPERTS, FTR * P), np.float32)
    for e in range(EXPERTS):
        wsel[:, e, e * FEXP:(e + 1) * FEXP] = 1.0 / (4.0 * SW)
    tri = np.concatenate([np.tril(np.ones((n, n), np.float32), -1).reshape(-1) for n in (4, 8)])

    b = np.concatenate([arr(L0_attn_b_ig), arr(L0_attn_b_og), arr(L0_attn_b_g)])[None, :]
    zeros = np.zeros((31, b.shape[1]), b.dtype)
    bias = np.concatenate([b, zeros, b], 0)

    ins = {
        "x": arr(x).reshape(-1, DM), "ctx": arr(ctx_512),
        "wqkv": by_partition(np.concatenate([arr(w).T for w in (L0_attn_Wq, L0_attn_Wk, L0_attn_Wv)], 1)),
        "wgate": by_partition(np.concatenate([arr(w).T for w in (L0_attn_Wig, L0_attn_Wog, L0_attn_Wg)], 1)),
        "bias": bias,
        "wo": by_partition(arr(L0_attn_Wo).T), "wrt": by_partition(arr(L0_ffn_gate_weight).T),
        "wfg": by_partition(hidden_rows(arr(L0_ffn_gate_w), arr(L0_ffn_sh_gate_w)).T),
        "wfu": by_partition(hidden_rows(arr(L0_ffn_up_w), arr(L0_ffn_sh_up_w)).T),
        "wfd": by_partition(down),
        "convw": np.ascontiguousarray(arr(L0_attn_conv_w).reshape(KC, P, CONV).transpose(1, 0, 2)),
        "convb": np.ascontiguousarray(arr(L0_attn_conv_b).reshape(KC, P).T),
        "mn_w": arr(L0_attn_mn_w), "mn_b": arr(L0_attn_mn_b), "gn_w": arr(L0_attn_gn_w), "gn_b": arr(L0_attn_gn_b),
        "ident": eye, "center": eye - same_head / HD, "kmask": kmask.reshape(P, -1),
        "maxsel": maxsel.reshape(NB * KVH, -1), "wsel": wsel.reshape(2 * EXPERTS, -1),
        "tri": np.ascontiguousarray(np.broadcast_to(tri, (P, tri.size))),
    }
    nc = bacc.Bacc("TRN2", target_bir_lowering=False, num_devices=1)
    arrays, a = {}, {}
    for name, v in ins.items():
        arrays[f"in_{name}"] = np.ascontiguousarray(v)
        a[name] = nc.dram_tensor(f"in_{name}", v.shape, mybir.dt.from_np(v.dtype), kind="ExternalInput").ap()
    a["y"] = nc.dram_tensor("out_y", ins["x"].shape, F32, kind="ExternalOutput").ap()
    build(nc, a)
    r = run_bass_kernel_spmd(nc, [arrays], core_ids=[0])
    return r.results[0]["out_y"].reshape(arr(x).shape)
```

```python
from contextlib import ExitStack

import concourse.bass as bass
from concourse import mybir
from concourse.alu_op_type import AluOpType as ALU

F32 = mybir.dt.float32
F16 = mybir.dt.float16
BF16 = mybir.dt.bfloat16
I32 = mybir.dt.int32
ACT = mybir.ActivationFunctionType
AX_X = mybir.AxisListType.X

P = 128
SEQ, DM, CTX = 64, 256, 64
KC = DM // P
TOK = 256
TT = TOK // P
NB = TOK // SEQ
HEADS, HD = 16, 16
KVH, G, HQ = 8, 4, 8
NPAIR = KVH // 2
EXPERTS, FEXP, FSHARED = 8, 176, 352
FT = 14
FTR = EXPERTS * FEXP // P
FTS = FT - FTR
FPAD = FT * P
assert FTR * P == EXPERTS * FEXP and FTS * P >= FSHARED
CONV = 4
EPS = 1e-5

SX = 16.0
SW = 64.0
SP_ = SX * SW
SS = 2.0 * SX
SG = SS * SW
SM = 2.0 * SP_
SN = 8.0
SK = 16.0
SH = 4.0
MAGIC = 1597463007.0
START = 64


class Signal:

    def __init__(self, sem, per):
        self.sem, self.per = sem, per

    def at(self, block, k):
        return block * self.per + (k + START)


def build(nc, a):
    ctx = ExitStack()
    with ctx:
        def sb(name, shape, dt=F32):
            return ctx.enter_context(nc.sbuf_tensor(name, shape, dt))

        def bank(name):
            return ctx.enter_context(nc.psum_tensor(name, [P, 512], F32))

        signals = []

        def signal(name, per=1):
            s = Signal(ctx.enter_context(nc.semaphore(name)), per)
            signals.append(s)
            return s

        bank_a = [bank("bank_a0"), bank("bank_a1")]
        bank_b = [bank("bank_b0"), bank("bank_b1")]
        bank_v = bank("bank_v")
        bank_gu = [bank("bank_gu0"), bank("bank_gu1")]
        bank_dn = bank("bank_dn")

        wqkv = [sb(f"wqkv_{p}", [P, KC, 768], F16) for p in "hl"]
        wgate = [sb(f"wgate_{p}", [P, KC, 528], F16) for p in "hl"]
        wo = [sb(f"wo_{p}", [P, KC, DM], F16) for p in "hl"]
        wrt = [sb(f"wrt_{p}", [P, KC, EXPERTS], F16) for p in "hl"]
        wfg = [sb(f"wfg_{p}", [P, KC, FPAD], F16) for p in "hl"]
        wfu = [sb(f"wfu_{p}", [P, KC, FPAD], F16) for p in "hl"]
        wfd = [sb(f"wfd_{p}", [P, FT, DM], F16) for p in "hl"]
        bias2 = sb("bias2", [33, 528], F16)
        ones2 = sb("ones2", [33, P], F16)
        stage = [sb(f"stage{n}", [P, FPAD]) for n in range(2)]
        bias_f = sb("bias_f", [33, 528])
        convw = sb("convw", [P, KC, CONV])
        convb = sb("convb", [P, KC])
        convb16 = sb("convb16", [P, KC])
        rows = sb("rows", [P, 4, DM])
        gn8 = sb("gn8", [P, 2, DM])
        ident = sb("ident", [P, P])
        ident16 = sb("ident16", [P, P], F16)
        center = sb("center", [P, P])
        kmask = sb("kmask", [P, KVH, SEQ], F16)
        maxsel = sb("maxsel", [NB * KVH, NB * NPAIR, P], BF16)
        wsel = sb("wsel", [2 * EXPERTS, FTR, P], F16)
        tri = sb("tri", [P, 80])
        tri4 = tri[:, 0:16].rearrange("p (a b) -> p a b", b=4)
        tri8 = tri[:, 16:80].rearrange("p (a b) -> p a b", b=8)
        power = sb("power", [P, TT])

        x_in = sb("x_in", [P, TT, DM])
        x_res = sb("x_res", [P, TT, DM])
        st1 = sb("st1", [P, TT, 6]); mv1 = sb("mv1", [P, TT, 2]); ve1 = sb("ve1", [P, TT]); rs1 = sb("rs1", [P, TT])
        xn = sb("xn", [P, TT, DM])
        xt_h = sb("xt_h", [P, KC, TOK], F16); xt_l = sb("xt_l", [P, KC, TOK], F16)
        cacc = sb("cacc", [P, KC, NB, SEQ])
        cth = sb("cth", [P, KC, TOK]); csil = sb("csil", [P, KC, TOK])
        ct_h = sb("ct_h", [P, KC, TOK], F16); ct_l = sb("ct_l", [P, KC, TOK], F16)
        qk = sb("qk", [P, TT, 512]); qk_sq = sb("qk_sq", [P, TT, 512])
        gate_t = sb("gate_t", [P, TT, 512])
        gam = sb("gam", [P, TT, DM])
        bv = sb("bv", [P, TT, DM]); bkn = sb("bkn", [P, TT, DM]); qn = sb("qn", [P, TT, DM])
        ss_qk = sb("ss_qk", [P, TT, 32]); r_qk = sb("r_qk", [P, TT, 32]); t_qk = sb("t_qk", [P, TT, 32])
        at = sb("at", [P, TT, KC, 2, SEQ])
        memt = sb("memt", [P, TT, KC, P])
        msq = qk_sq[:, 0, :].rearrange("p (t d) -> p t d", t=TT); ss_m = sb("ss_m", [P, TT, HEADS]); v_m = sb("v_m", [P, TT, HEADS])
        r_m = sb("r_m", [P, TT, HEADS]); t_m = sb("t_m", [P, TT, HEADS])
        m1 = sb("m1", [P, TT, DM]); o1 = sb("o1", [P, TT, DM])
        sum_o = sb("sum_o", [P, TT, HEADS]); oc = sb("oc", [P, TT, DM]); osq = qk_sq[:, 1, :].rearrange("p (t d) -> p t d", t=TT)
        ss_o = sb("ss_o", [P, TT, HEADS]); v_o = sb("v_o", [P, TT, HEADS])
        r_o = sb("r_o", [P, TT, HEADS]); t_o = sb("t_o", [P, TT, HEADS])
        o2 = sb("o2", [P, TT, DM]);  o5 = sb("o5", [P, TT, DM])
        ot_h = sb("ot_h", [P, KC, TOK], F16); ot_l = sb("ot_l", [P, KC, TOK], F16)
        x1 = sb("x1", [P, TT, DM])
        ctxs = sb("ctxs", [P, NB, CTX])
        k2 = sb("k2", [SEQ, NB, 3 * CTX], F16)
        kt = sb("kt", [P, NB, SEQ], F16); ktl = sb("ktl", [CTX, NB, SEQ], F16)
        kb = sb("kb", [P, NB, KVH, SEQ], F16)
        kl = sb("kl", [CTX, NB, KVH, SEQ], F16)
        vblk = sb("vblk", [P, NB, NPAIR, 32])
        st2 = sb("st2", [P, TT, 6]); mv2 = sb("mv2", [P, TT, 2]); ve2 = sb("ve2", [P, TT]); rs2 = sb("rs2", [P, TT])
        xq = sb("xq", [P, TT, DM])
        qs = sb("qs", [P, NB, G, SEQ], F16)
        mx = sb("mx", [P, 2, NB, KVH])
        mxt = sb("mxt", [NB * KVH, 2 * P], BF16)
        prob = [sb(f"prob{n}", [P, 512]) for n in range(2)]
        avs = sb("avs", [P, TT, G, 2, SEQ])
        orec = sb("orec", [P, TT, G, NPAIR, 2])
        oatt = sb("oatt", [P, TT, DM])
        x2 = sb("x2", [P, TT, DM])
        x3 = sb("x3", [P, TT, DM])
        st3 = sb("st3", [P, TT, 6]); mv3 = sb("mv3", [P, TT, 2]); ve3 = sb("ve3", [P, TT]); rs3 = sb("rs3", [P, TT])
        hn = sb("hn", [P, TT, DM])
        ht_h = sb("ht_h", [P, KC, TOK], F16); ht_l = sb("ht_l", [P, KC, TOK], F16)
        lmax = sb("lmax", [P, TT]); lneg = sb("lneg", [P, TT]); lexp = sb("lexp", [P, TT, EXPERTS])
        lsum = sb("lsum", [P, TT]); lrec = sb("lrec", [P, TT]); prb = sb("prb", [P, TT, EXPERTS])
        gs = sb("gs", [P, TT, 4]); ggt = sb("ggt", [P, TT, 4, 4]); geq = sb("geq", [P, TT, 4, 4])
        gcnt = sb("gcnt", [P, TT, 4, 4]); grank = sb("grank", [P, TT * 4])
        pm = sb("pm", [P, TT, EXPERTS])
        egt = sb("egt", [P, TT, 8, 8]); eeq = sb("eeq", [P, TT, 8, 8]);
        ecnt = sb("ecnt", [P, TT, 8, 8]); erank = sb("erank", [P, TT * 8]); wts = sb("wts", [P, TT, EXPERTS])
        whl = sb("whl", [P, TT, 16], F16)
        wt = sb("wt", [16, TOK], F16)
        wx = sb("wx", [P, FTR, TOK])
        ff_tanh = [sb(f"ff_tanh{n}", [P, TOK]) for n in range(2)]
        ff_g = [sb(f"ff_g{n}", [P, TOK]) for n in range(2)]
        ff_u = [sb(f"ff_u{n}", [P, TOK]) for n in range(2)]
        ff_w = [sb(f"ff_w{n}", [P, TOK]) for n in range(2)]
        hid_h = [sb(f"hid_h{n}", [P, TOK], F16) for n in range(2)]
        hid_l = [sb(f"hid_l{n}", [P, TOK], F16) for n in range(2)]
        y_sb = sb("y_sb", [P, TT, DM])

        def plain(name):
            return ctx.enter_context(nc.semaphore(name))

        cst_loaded = plain("cst_loaded")
        stage_loaded = [plain(f"stage_loaded{n}") for n in range(2)]
        stage_split = plain("stage_split")
        stage_high = plain("stage_high")
        cst_act = plain("cst_act")
        cst_dve = plain("cst_dve")
        cst_pool = plain("cst_pool")
        primed = plain("primed")
        held = plain("held")

        x_loaded = signal("x_loaded", 16)
        x_kept = signal("x_kept")
        ln1_stat = signal("ln1_stat", 5)
        ln1_rstd = signal("ln1_rstd")
        xn_ready = signal("xn_ready", TT)
        xt_ps = signal("xt_ps")
        xt_high = signal("xt_high")
        xt_low = signal("xt_low")
        conv_first = signal("conv_first", KC)
        conv_taps = signal("conv_taps", KC * (CONV - 1))
        conv_tanh = signal("conv_tanh")
        conv_silu = signal("conv_silu")
        ct_high = signal("ct_high")
        ct_low = signal("ct_low")
        qk_ps = signal("qk_ps", TT)
        vg_ps = signal("vg_ps", TT)
        gate_ps = signal("gate_ps", TT)
        qk_kept = signal("qk_kept", TT)
        qk_square = signal("qk_square", TT)
        gate_tanh = signal("gate_tanh", TT)
        gam_tanh = signal("gam_tanh", TT)
        v_gated = signal("v_gated", TT)
        qk_sums = signal("qk_sums", TT)
        qk_norm = signal("qk_norm", 12)
        bk_ready = signal("bk_ready")
        bkn_ready = signal("bkn_ready")
        qn_ready = signal("qn_ready")
        bg_ps = signal("bg_ps", TT)
        decay_ready = signal("decay_ready", TT)
        mem_ready = signal("mem_ready", TT * KC)
        ctr_ps = signal("ctr_ps")
        mem_square = signal("mem_square")
        mem_norm = signal("mem_norm", 13)
        m1_ready = signal("m1_ready")
        m2_ready = signal("m2_ready")
        m3_ready = signal("m3_ready")
        o1_ready = signal("o1_ready")
        out_center = signal("out_center", 2)
        out_square = signal("out_square")
        out_norm = signal("out_norm", 13)
        o2_ready = signal("o2_ready")
        o3_ready = signal("o3_ready")
        o4_ready = signal("o4_ready")
        o5_ready = signal("o5_ready")
        ot_ps = signal("ot_ps")
        ot_high = signal("ot_high")
        ot_low = signal("ot_low")
        mix_ps = signal("mix_ps")
        x1_ready = signal("x1_ready")
        ctx_loaded = signal("ctx_loaded", 32)
        k_high = signal("k_high")
        k_low = signal("k_low")
        v_block = signal("v_block", 2)
        kt_ps = signal("kt_ps")
        kt_kept = signal("kt_kept", 2)
        k_masked = signal("k_masked", 2)
        ln2_stat = signal("ln2_stat", 5)
        ln2_rstd = signal("ln2_rstd")
        xq_ready = signal("xq_ready", TT)
        qt_ps = signal("qt_ps", TT)
        q_high = signal("q_high", TT)
        q_low = signal("q_low", TT)
        row_ps = signal("row_ps", 2 * NB)
        row_max = signal("row_max", 2 * NB)
        maxt_ps = signal("maxt_ps")
        maxt_kept = signal("maxt_kept")
        col_ps = signal("col_ps", 2 * NB)
        col_exp = signal("col_exp", 2 * NB)
        val_ps = signal("val_ps", 2 * NB)
        val_kept = signal("val_kept", NB)
        att_ps = signal("att_ps", TT)
        att_norm = signal("att_norm", 3 * TT)
        x2_ready = signal("x2_ready", TT)
        ln3_stat = signal("ln3_stat", 5)
        ln3_rstd = signal("ln3_rstd")
        hn_ready = signal("hn_ready", TT)
        x2_kept = signal("x2_kept")
        ht_ps = signal("ht_ps")
        ht_high = signal("ht_high")
        ht_low = signal("ht_low")
        logit_ps = signal("logit_ps")
        logit_exp = signal("logit_exp", TT)
        route = signal("route", 20)
        wt_ps = signal("wt_ps")
        wt_kept = signal("wt_kept")
        wx_ps = signal("wx_ps", 6)
        wx_kept = signal("wx_kept", 6)
        gu_ps = signal("gu_ps", FT)
        tanh_done = signal("tanh_done", FT)
        silu_done = signal("silu_done", FT)
        up_done = signal("up_done", FT)
        weighted = signal("weighted", FTR)
        hid_high = signal("hid_high", FT)
        hid_low = signal("hid_low", FT)
        down_ps = signal("down_ps", FT)
        y_based = signal("y_based")
        y_ready = signal("y_ready")
        y_stored = signal("y_stored", 16)

        def flat(t, lo=0, hi=None):
            return t[:, lo:hi, :].rearrange("p a b -> p (a b)")

        loads = [(a["wqkv"], flat(wqkv[0]), flat(wqkv[1]), SW), (a["wgate"], flat(wgate[0]), flat(wgate[1]), SW),
                 (a["wo"], flat(wo[0]), flat(wo[1]), SW), (a["kmask"], flat(kmask), None, 1.0)]
        loads += [(a["maxsel"][:, 1024 * n:1024 * n + 1024], flat(maxsel, 8 * n, 8 * n + 8), None, 1.0) for n in range(2)]
        loads += [(a["wrt"], flat(wrt[0]), flat(wrt[1]), SW), (a["wsel"], flat(wsel), None, 1.0)]
        loads += [(a[name][:, c * FPAD:(c + 1) * FPAD], flat(w[0], c, c + 1), flat(w[1], c, c + 1), SW)
                  for name, w in (("wfg", wfg), ("wfu", wfu)) for c in range(KC)]
        loads += [(a["wfd"][:, c * FPAD:(c + 1) * FPAD], flat(wfd[0], 7 * c, 7 * c + 7), flat(wfd[1], 7 * c, 7 * c + 7), SW)
                  for c in range(2)]

        WQKV, WGATE, WO, KMASK, MAXSEL, WRT, WSEL, WFG, WFU, WFD = 0, 1, 2, 3, 5, 6, 7, 9, 11, 13

        def splits_before(n):
            return sum(low is not None for _, _, low, _ in loads[:n])

        consts = [
            (ident[:, :], a["ident"]), (center[:, :], a["center"]), (tri[:, :], a["tri"]),
            (convw[:, :, :], a["convw"]), (convb[:, :], a["convb"]),
            (bias_f[:, :], a["bias"]),
        ] + [(rows[:, n, :], a[name].partition_broadcast(P)) for n, name in enumerate(("mn_w", "mn_b", "gn_w", "gn_b"))]

        x_blocks = a["x"].rearrange("(n t p) d -> n p t d", p=P, t=TT)
        y_blocks = a["y"].rearrange("(n t p) d -> n p t d", p=P, t=TT)
        c_blocks = a["ctx"].rearrange("(n b) t d -> n t b d", b=NB)
        BLOCKS = x_blocks.shape[0]
        LAGS = 8
        ROUTER_BEHIND = 2

        block = ctx.enter_context(nc.Block())

        def blocks(j):
            return [j - n if not isinstance(j, int) or 0 <= j - n < BLOCKS else None for n in range(LAGS + 1)]

        def on(i, step, *args):
            if i is not None:
                step(i, *args)

        def once(i, step, n):
            if isinstance(i, int) and i == 0:
                step(i, n)

        def need(engine, i, n):
            if isinstance(i, int) and i == 0:
                engine.wait_ge(stage_high, n + 1)
                engine.wait_ge(stage_split, splits_before(n + 1))

        @block.sync
        def _(sp):
            def load_x(i):
                sp.wait_ge(xn_ready.sem, xn_ready.at(i, 0))
                sp.sem_inc(held, 1)
                sp.wait_ge(x_kept.sem, x_kept.at(i, 0))
                sp.sem_inc(held, 1)
                sp.dma_start(x_in[:, :, :], x_blocks[i]).then_inc(x_loaded.sem, 16)

            def load_next_x(i):
                if not isinstance(i, int) or i + 1 < BLOCKS:
                    load_x(i + 1)

            def load_ctx(i):
                sp.wait_ge(k_low.sem, k_low.at(i, 0))
                sp.sem_inc(held, 1)
                sp.wait_ge(v_block.sem, v_block.at(i, 0))
                sp.sem_inc(held, 1)
                sp.wait_ge(k_high.sem, k_high.at(i, 0))
                sp.sem_inc(held, 1)
                for half in range(2):
                    sp.dma_start(ctxs[64 * half:64 * half + 64, :, :], c_blocks[i]).then_inc(ctx_loaded.sem, 16)

            def store_y(i):
                sp.wait_ge(y_ready.sem, y_ready.at(i, 1))
                sp.sem_inc(held, 1)
                sp.dma_start(y_blocks[i], y_sb[:, :, :]).then_inc(y_stored.sem, 16)

            sp.wait_ge(primed, 1)
            load_x(0)
            for dst, src in consts:
                sp.dma_start(dst, src).then_inc(cst_loaded, 16)

            def load_weight(i, n):
                src = loads[n][0]
                if n >= 2:
                    sp.wait_ge(stage_high, n - 1)
                    if splits_before(n - 1):
                        sp.wait_ge(stage_split, splits_before(n - 1))
                sp.dma_start(stage[n % 2][0:src.shape[0], 0:src.shape[1]], src).then_inc(stage_loaded[n % 2], 16)

            def turn(j):
                b = blocks(j)
                for n in range(10, 13):
                    once(b[2], load_weight, n)
                once(b[1], load_weight, 0)
                on(b[5], load_next_x)
                once(b[2], load_weight, 13)
                for n in range(1, 5):
                    once(b[1], load_weight, n)
                on(b[8], store_y)
                for n in range(5, 8):
                    once(b[1], load_weight, n)
                on(b[4], load_ctx)
                once(b[1], load_weight, 8)
                once(b[1], load_weight, 9)

            for j in range(LAGS):
                turn(j)
            with sp.Fori(LAGS, BLOCKS - 1) as j:
                turn(j)
            for j in range(BLOCKS - 1, BLOCKS + LAGS):
                turn(j)
            sp.wait_ge(y_stored.sem, y_stored.at(BLOCKS, 0))

        @block.gpsimd
        def _(pool):
            for s in signals:
                pool.sem_inc(s.sem, START)
            pool.sem_inc(primed, 1)
            pool.memset(power[:, :], -0.5).then_inc(cst_pool, 1)
            pool.memset(at[:, :, :, :, :], 0.0).then_inc(cst_pool, 1)
            pool.memset(vblk[:, :, :, :], 0.0).then_inc(cst_pool, 1)
            pool.memset(ones2[:, :], 0.0).then_inc(cst_pool, 1)
            pool.wait_ge(cst_pool, 4)
            pool.memset(vblk[0:64, :, :, 16:17], 1.0).then_inc(cst_pool, 1)
            pool.memset(vblk[64:128, :, :, 17:18], 1.0).then_inc(cst_pool, 1)
            pool.wait_ge(cst_pool, 6)
            pool.memset(ones2[0:1, :], SS).then_inc(cst_pool, 1)
            pool.memset(ones2[32:33, :], SS).then_inc(cst_pool, 1)

            def rstd(i, stat, done, ve, rs, free):
                pool.wait_ge(free.sem, free.at(i, 0))
                pool.wait_ge(stat.sem, stat.at(i, 5))
                pool.tensor_tensor(rs[:, :], ve[:, :], power[:, :], ALU.pow).then_inc(done.sem, 1)

            def norm1_rstd(i):
                rstd(i, ln1_stat, ln1_rstd, ve1, rs1, xn_ready)

            def norm2_rstd(i):
                rstd(i, ln2_stat, ln2_rstd, ve2, rs2, xq_ready)

            def norm3_rstd(i):
                rstd(i, ln3_stat, ln3_rstd, ve3, rs3, hn_ready)

            def silu_low(i):
                pool.wait_ge(ct_high.sem, ct_high.at(i, 1))
                pool.wait_ge(conv_silu.sem, conv_silu.at(i, 1))
                pool.wait_ge(gate_ps.sem, gate_ps.at(i, 0))
                pool.tensor_tensor(ct_l[:, :, :], csil[:, :, :], ct_h[:, :, :], ALU.subtract).then_inc(ct_low.sem, 1)

            def keys_times_values(i):
                pool.wait_ge(v_gated.sem, v_gated.at(i, TT))
                pool.wait_ge(qk_kept.sem, qk_kept.at(i, TT))
                pool.tensor_tensor(bv[:, :, :], bv[:, :, :], qk[:, :, DM:2 * DM], ALU.mult).then_inc(bk_ready.sem, 1)

            def head_bcast(r, lo=0):
                return r[:, :, lo:lo + HEADS].unsqueeze(3).broadcast_to([P, TT, HEADS, HD])

            def by_head(t):
                return t.rearrange("p t (h d) -> p t h d", d=HD)

            def keys_normed(i):
                pool.wait_ge(qk_norm.sem, qk_norm.at(i, 12))
                pool.wait_ge(bk_ready.sem, bk_ready.at(i, 1))
                pool.wait_ge(bg_ps.sem, bg_ps.at(i, 0))
                pool.tensor_tensor(by_head(bkn[:, :, :]), by_head(bv[:, :, :]), head_bcast(r_qk, HEADS),
                                   ALU.mult).then_inc(bkn_ready.sem, 1)

            def queries_normed(i):
                pool.wait_ge(qk_norm.sem, qk_norm.at(i, 12))
                pool.wait_ge(qk_kept.sem, qk_kept.at(i, TT))
                pool.wait_ge(o1_ready.sem, o1_ready.at(i, 0))
                pool.tensor_tensor(by_head(qn[:, :, :]), by_head(qk[:, :, 0:DM]), head_bcast(r_qk, 0),
                                   ALU.mult).then_inc(qn_ready.sem, 1)

            def row(t, n):
                return t[:, n:n + 1, :].broadcast_to([P, TT, DM])

            def mem_weight(i):
                pool.wait_ge(m1_ready.sem, m1_ready.at(i, 1))
                pool.tensor_tensor(m1[:, :, :], m1[:, :, :], row(rows, 0), ALU.mult).then_inc(m2_ready.sem, 1)

            def mem_bias(i):
                pool.wait_ge(m2_ready.sem, m2_ready.at(i, 1))
                pool.tensor_tensor(m1[:, :, :], m1[:, :, :], row(rows, 1), ALU.add).then_inc(m3_ready.sem, 1)

            def mem_times_queries(i):
                pool.wait_ge(m3_ready.sem, m3_ready.at(i, 1))
                pool.wait_ge(qn_ready.sem, qn_ready.at(i, 1))
                pool.wait_ge(out_center.sem, out_center.at(i, 0))
                pool.tensor_tensor(o1[:, :, :], m1[:, :, :], qn[:, :, :], ALU.mult).then_inc(o1_ready.sem, 1)

            def out_weight(i):
                pool.wait_ge(o2_ready.sem, o2_ready.at(i, 1))
                pool.tensor_tensor(o2[:, :, :], o2[:, :, :], row(gn8, 0), ALU.mult).then_inc(o3_ready.sem, 1)

            def out_bias(i):
                pool.wait_ge(o3_ready.sem, o3_ready.at(i, 1))
                pool.tensor_tensor(o2[:, :, :], o2[:, :, :], row(gn8, 1), ALU.add).then_inc(o4_ready.sem, 1)

            def attention_residual(i, t):
                pool.wait_ge(att_norm.sem, att_norm.at(i, 3 * t + 3))
                pool.wait_ge(hn_ready.sem, hn_ready.at(i, 0))
                pool.wait_ge(x2_kept.sem, x2_kept.at(i, 0))
                pool.wait_ge(x1_ready.sem, x1_ready.at(i, 1))
                pool.tensor_tensor(x2[:, t, :], oatt[:, t, :], x1[:, t, :], ALU.add).then_inc(x2_ready.sem, 1)

            def weigh(i, k):
                pool.wait_ge(up_done.sem, up_done.at(i, k + 1))
                pool.wait_ge(wx_kept.sem, wx_kept.at(i, (k - FTS) // 2 + 1))
                b, n = (i, k - 1) if k >= FTS + 2 else (i - 1, FT - (k - FTS))
                pool.wait_ge(hid_high.sem, hid_high.at(b, n))
                pool.wait_ge(hid_low.sem, hid_low.at(b, n))
                pool.tensor_tensor(ff_w[k % 2][:, :], ff_u[k % 2][:, :], wx[:, k - FTS, :], ALU.mult).then_inc(weighted.sem, 1)

            def hidden_low(i, k):
                src = ff_u if k < FTS else ff_w
                pool.wait_ge(hid_high.sem, hid_high.at(i, k + 1))
                if k >= FTS:
                    pool.wait_ge(weighted.sem, weighted.at(i, k - FTS + 1))
                pool.wait_ge(down_ps.sem, down_ps.at(i, k - 1))
                pool.tensor_tensor(hid_l[k % 2][:, :], src[k % 2][:, :], hid_h[k % 2][:, :],
                                   ALU.subtract).then_inc(hid_low.sem, 1)

            def turn(j):
                b = blocks(j)
                on(b[4], hidden_low, 2)
                on(b[4], weigh, 3)
                on(b[2], norm2_rstd)
                on(b[4], hidden_low, 3)
                on(b[4], weigh, 4)
                on(b[1], silu_low)
                on(b[4], hidden_low, 4)
                on(b[4], weigh, 5)
                on(b[4], hidden_low, 5)
                on(b[4], weigh, 6)
                on(b[4], weigh, 7)
                on(b[1], keys_times_values)
                on(b[1], keys_normed)
                on(b[4], hidden_low, 6)
                on(b[4], hidden_low, 7)
                on(b[4], weigh, 8)
                on(b[4], weigh, 9)
                on(b[4], hidden_low, 8)
                on(b[4], weigh, 10)
                on(b[3], norm3_rstd)
                on(b[4], hidden_low, 9)
                on(b[1], queries_normed)
                on(b[1], mem_weight)
                on(b[4], weigh, 11)
                on(b[1], mem_bias)
                on(b[4], hidden_low, 10)
                on(b[4], weigh, 12)
                on(b[1], mem_times_queries)
                on(b[4], hidden_low, 11)
                on(b[4], weigh, 13)
                on(b[0], norm1_rstd)
                on(b[4], hidden_low, 12)
                on(b[4], hidden_low, 13)
                on(b[1], out_weight)
                on(b[1], out_bias)
                on(b[3], hidden_low, 0)
                on(b[3], hidden_low, 1)
                on(b[2], attention_residual, 0)
                on(b[2], attention_residual, 1)

            pool.wait_ge(cst_dve, 2)
            pool.wait_ge(cst_pool, 8)
            for j in range(LAGS):
                turn(j)
            with pool.Fori(LAGS, BLOCKS) as j:
                turn(j)
            for j in range(BLOCKS, BLOCKS + LAGS):
                turn(j)

        @block.scalar
        def _(act):
            act.wait_ge(cst_loaded, 16 * len(consts))
            act.activation(ident16[:, :], ident[:, :], ACT.Copy).then_inc(cst_act, 1)
            act.activation(convb16[:, :], convb[:, :], ACT.Copy, scale=SX).then_inc(cst_act, 1)
            act.activation(bias2[:, :], bias_f[:, :], ACT.Copy, scale=SW).then_inc(cst_act, 1)

            def weight_high(i, n):
                src, high, _, scale = loads[n]
                act.wait_ge(stage_loaded[n % 2], 16 * (n // 2 + 1))
                act.activation(high, stage[n % 2][0:src.shape[0], 0:src.shape[1]], ACT.Copy,
                               scale=scale).then_inc(stage_high, 1)

            def keep_x(i):
                act.wait_ge(x_loaded.sem, x_loaded.at(i, 16))
                act.wait_ge(x1_ready.sem, x1_ready.at(i, 0))
                act.activation(x_res[:, :, :], x_in[:, :, :], ACT.Copy).then_inc(x_kept.sem, 1)

            def x_transposed(i):
                act.wait_ge(xt_ps.sem, xt_ps.at(i, 1))
                act.wait_ge(vg_ps.sem, vg_ps.at(i, 0))
                psum = bank_a[0][:, :].rearrange("p (c t) -> p c t", c=KC)
                act.activation(xt_h[:, :, :], psum, ACT.Copy).then_inc(xt_high.sem, 1)

            def conv_start(i):
                act.wait_ge(xt_ps.sem, xt_ps.at(i, 1))
                act.wait_ge(conv_silu.sem, conv_silu.at(i, 0))
                psum = bank_a[0][:, :].rearrange("p (c t) -> p c t", c=KC)
                for c in range(KC):
                    act.activation(cacc[:, c, :, :].rearrange("p b s -> p (b s)"), psum[:, c, :], ACT.Identity,
                                   scale=convw[:, c, CONV - 1:CONV], bias=convb16[:, c:c + 1]).then_inc(conv_first.sem, 1)

            def conv_activation(i):
                act.wait_ge(conv_taps.sem, conv_taps.at(i, KC * (CONV - 1)))
                act.wait_ge(conv_silu.sem, conv_silu.at(i, 0))
                act.activation(cth[:, :, :], cacc[:, :, :, :].rearrange("p c b s -> p c (b s)"), ACT.Tanh,
                               scale=0.5 / SX).then_inc(conv_tanh.sem, 1)

            def silu_high(i):
                act.wait_ge(conv_silu.sem, conv_silu.at(i, 1))
                act.wait_ge(gate_ps.sem, gate_ps.at(i, 0))
                act.activation(ct_h[:, :, :], csil[:, :, :], ACT.Copy).then_inc(ct_high.sem, 1)

            def qk_out(i, t):
                b = bank_a[(t + 1) % 2]
                act.wait_ge(qk_ps.sem, qk_ps.at(i, t + 1))
                act.wait_ge(qn_ready.sem, qn_ready.at(i, 0))
                act.activation(qk[:, t, :], b[:, :], ACT.Copy).then_inc(qk_kept.sem, 1)
                prior = out_norm if t else mem_norm
                act.wait_ge(prior.sem, prior.at(i, 0))
                act.activation(qk_sq[:, t, :], b[:, :], ACT.Square).then_inc(qk_square.sem, 1)

            def gamma_out(i, t):
                b = bank_a[t % 2]
                act.wait_ge(vg_ps.sem, vg_ps.at(i, t + 1))
                act.wait_ge(bg_ps.sem, bg_ps.at(i, 0))
                src = b[:, DM:DM + HEADS].unsqueeze(2).broadcast_to([P, HEADS, HD])
                act.activation(gam[:, t, :].rearrange("p (h d) -> p h d", d=HD), src, ACT.Tanh,
                               scale=0.5 / SG).then_inc(gam_tanh.sem, 1)

            def gates_out(i, t):
                b = bank_a[(t + 1) % 2]
                act.wait_ge(gate_ps.sem, gate_ps.at(i, t + 1))
                act.wait_ge(o5_ready.sem, o5_ready.at(i, 0))
                act.activation(gate_t[:, t, :], b[:, :], ACT.Tanh, scale=0.5 / SG).then_inc(gate_tanh.sem, 1)

            def decay(i, t):
                b = bank_a[(t + 1) % 2][:, DM:2 * DM].rearrange("p (c b s) -> p c b s", c=KC, b=2)
                act.wait_ge(bg_ps.sem, bg_ps.at(i, t + 1))
                act.wait_ge(mem_ready.sem, mem_ready.at(i, KC * (t + 1) - TT * KC))
                for c in range(KC):
                    ins = act.activation(at[:, t, c, :, 1:SEQ], b[:, c, :, 1:SEQ], ACT.Copy, scale=0.5, bias=0.5)
                ins.then_inc(decay_ready.sem, 1)

            def mem_squares(i):
                act.wait_ge(ctr_ps.sem, ctr_ps.at(i, 1))
                act.wait_ge(mem_norm.sem, mem_norm.at(i, 0))
                act.activation(msq[:, :, :], bank_a[1][:, :].rearrange("p (t d) -> p t d", t=TT),
                               ACT.Square).then_inc(mem_square.sem, 1)

            def out_squares(i):
                act.wait_ge(out_center.sem, out_center.at(i, 2))
                act.wait_ge(out_norm.sem, out_norm.at(i, 0))
                act.activation(osq[:, :, :], oc[:, :, :], ACT.Square).then_inc(out_square.sem, 1)

            def out_transposed(i):
                act.wait_ge(ot_ps.sem, ot_ps.at(i, 1))
                act.wait_ge(mix_ps.sem, mix_ps.at(i, 0))
                act.activation(ot_h[:, :, :], bank_a[0][:, :].rearrange("p (c t) -> p c t", c=KC),
                               ACT.Copy).then_inc(ot_high.sem, 1)

            def keys_values(i):
                act.wait_ge(ctx_loaded.sem, ctx_loaded.at(i, 32))
                act.wait_ge(kt_ps.sem, kt_ps.at(i, 0))
                act.activation(k2[:, :, 0:2 * CTX].rearrange("p b (r d) -> p b r d", r=2),
                               ctxs[0:SEQ, :, :].unsqueeze(2).broadcast_to([SEQ, NB, 2, CTX]),
                               ACT.Copy, scale=SK).then_inc(k_high.sem, 1)
                act.wait_ge(val_ps.sem, val_ps.at(i, 0))
                for half in range(2):
                    src = ctxs[64 * half:64 * half + 64, :, :].rearrange("p b (j h d) -> p b j h d", j=NPAIR, h=2)
                    act.activation(vblk[64 * half:64 * half + 64, :, :, 8 * half:8 * half + 8],
                                   src[:, :, :, half, :], ACT.Copy).then_inc(v_block.sem, 1)

            def keys_transposed(i):
                act.wait_ge(kt_ps.sem, kt_ps.at(i, 1))
                act.wait_ge(k_masked.sem, k_masked.at(i, 0))
                psum = bank_v[:, 0:256].bitcast(F16)
                act.activation(kt[:, :, :].rearrange("p b s -> p (b s)"), psum[:, 0:256], ACT.Copy).then_inc(kt_kept.sem, 1)
                act.activation(ktl[:, :, :].rearrange("p b s -> p (b s)"), psum[0:CTX, 256:512], ACT.Copy).then_inc(kt_kept.sem, 1)

            def queries_high(i, t):
                act.wait_ge(qt_ps.sem, qt_ps.at(i, t + 1))
                act.wait_ge(col_ps.sem, col_ps.at(i, 0))
                act.activation(qs[0:64, 2 * t:2 * t + 2, :, :],
                               bank_b[t][0:64, :].rearrange("p (g b s) -> p b g s", g=G, b=2),
                               ACT.Copy).then_inc(q_high.sem, 1)

            def maxima_transposed(i):
                act.wait_ge(maxt_ps.sem, maxt_ps.at(i, 1))
                act.wait_ge(col_ps.sem, col_ps.at(i, 0))
                act.activation(mxt[:, :], bank_v[0:NB * KVH, 0:256], ACT.Copy).then_inc(maxt_kept.sem, 1)

            def exps(i, n):
                act.wait_ge(col_ps.sem, col_ps.at(i, n + 1))
                act.wait_ge(val_ps.sem, val_ps.at(i, n - 1))
                act.activation(prob[n % 2][:, :], bank_b[n % 2][:, :], ACT.Exp,
                               scale=1.0 / (SX * SK * HQ ** 0.5)).then_inc(col_exp.sem, 1)

            def values_out(i, b):
                act.wait_ge(val_ps.sem, val_ps.at(i, 2 * b + 2))
                act.wait_ge(att_ps.sem, att_ps.at(i, b // 2 + 1 - TT))
                act.activation(avs[:, b // 2, :, b % 2, :],
                               bank_v[:, 256 * (b % 2):256 * (b % 2) + 256].rearrange("p (g s) -> p g s", g=G),
                               ACT.Copy).then_inc(val_kept.sem, 1)

            def keep_y(i):
                act.wait_ge(x2_kept.sem, x2_kept.at(i, 1))
                act.wait_ge(y_stored.sem, y_stored.at(i, 0))
                act.activation(y_sb[:, :, :], x3[:, :, :], ACT.Copy).then_inc(y_based.sem, 1)

            def keep_x2(i):
                act.wait_ge(x2_ready.sem, x2_ready.at(i, TT))
                act.wait_ge(y_based.sem, y_based.at(i, 0))
                act.activation(x3[:, :, :], x2[:, :, :], ACT.Copy).then_inc(x2_kept.sem, 1)

            def h_transposed(i):
                act.wait_ge(ht_ps.sem, ht_ps.at(i, 1))
                act.wait_ge(gu_ps.sem, gu_ps.at(i, 0))
                act.wait_ge(logit_ps.sem, logit_ps.at(i, 0))
                act.activation(ht_h[:, :, :], bank_a[0][:, :].rearrange("p (c t) -> p c t", c=KC),
                               ACT.Copy).then_inc(ht_high.sem, 1)

            def router_exp(i):
                act.wait_ge(route.sem, route.at(i, 2))
                for t in range(TT):
                    act.activation(lexp[:, t, :], bank_a[1][:, EXPERTS * t:EXPERTS * (t + 1)], ACT.Exp,
                                   scale=1.0 / SP_, bias=lneg[:, t:t + 1]).then_inc(logit_exp.sem, 1)

            def weights_transposed(i):
                act.wait_ge(wt_ps.sem, wt_ps.at(i, 1))
                act.wait_ge(wx_ps.sem, wx_ps.at(i, 0))
                act.activation(wt[:, :], bank_a[0][0:16, 0:128].bitcast(F16), ACT.Copy).then_inc(wt_kept.sem, 1)

            def weights_spread(i, n):
                act.wait_ge(wx_ps.sem, wx_ps.at(i, n + 1))
                w = min(2, FTR - 2 * n)
                act.wait_ge(weighted.sem, weighted.at(i - 1, 2 * n + w))
                act.activation(wx[:, 2 * n:2 * n + w, :].rearrange("p k t -> p (k t)"),
                               bank_a[(n + 1) % 2][:, 0:w * TOK], ACT.Copy).then_inc(wx_kept.sem, 1)

            def expert_tanh(i, k):
                act.wait_ge(gu_ps.sem, gu_ps.at(i, k + 1))
                act.wait_ge(silu_done.sem, silu_done.at(i, k - 1))
                act.activation(ff_tanh[k % 2][:, :], bank_gu[k % 2][:, 0:TOK], ACT.Tanh,
                               scale=0.5 / SP_).then_inc(tanh_done.sem, 1)

            def expert_high(i, k):
                if k >= FTS:
                    act.wait_ge(weighted.sem, weighted.at(i, k - FTS + 1))
                else:
                    act.wait_ge(up_done.sem, up_done.at(i, k + 1))
                act.wait_ge(down_ps.sem, down_ps.at(i, k - 1))
                src = ff_u if k < FTS else ff_w
                act.activation(hid_h[k % 2][:, :], src[k % 2][:, :], ACT.Copy).then_inc(hid_high.sem, 1)

            def turn(j):
                b = blocks(j)
                on(b[7], router_exp)
                once(b[3], weight_high, 5)
                on(b[8], expert_high, 11)
                on(b[6], values_out, 1)
                on(b[6], exps, 4)
                on(b[6], exps, 5)
                on(b[5], out_squares)
                once(b[3], weight_high, 6)
                on(b[6], values_out, 2)
                on(b[8], expert_high, 12)
                on(b[8], expert_high, 13)
                once(b[3], weight_high, 7)
                on(b[7], expert_tanh, 0)
                on(b[6], exps, 6)
                on(b[7], weights_transposed)
                on(b[6], exps, 7)
                on(b[7], weights_spread, 0)
                on(b[7], weights_spread, 1)
                once(b[3], weight_high, 8)
                on(b[7], expert_tanh, 1)
                on(b[7], weights_spread, 2)
                on(b[7], weights_spread, 3)
                on(b[6], values_out, 3)
                on(b[7], expert_high, 0)
                on(b[7], weights_spread, 4)
                on(b[7], weights_spread, 5)
                on(b[7], expert_tanh, 2)
                on(b[7], expert_high, 1)
                on(b[5], out_transposed)
                on(b[5], keys_values)
                on(b[7], expert_tanh, 3)
                once(b[3], weight_high, 9)
                on(b[7], expert_high, 2)
                on(b[4], x_transposed)
                on(b[4], conv_start)
                on(b[7], expert_tanh, 4)
                once(b[3], weight_high, 10)
                on(b[4], qk_out, 0)
                on(b[4], conv_activation)
                on(b[5], keys_transposed)
                on(b[7], expert_high, 3)
                once(b[3], weight_high, 11)
                on(b[4], silu_high)
                on(b[7], expert_tanh, 5)
                on(b[4], gates_out, 0)
                once(b[3], weight_high, 12)
                on(b[5], queries_high, 0)
                once(b[3], weight_high, 13)
                on(b[5], queries_high, 1)
                on(b[4], gamma_out, 0)
                on(b[7], expert_high, 4)
                on(b[7], expert_tanh, 6)
                on(b[4], qk_out, 1)
                on(b[4], gamma_out, 1)
                on(b[7], expert_tanh, 7)
                on(b[7], expert_high, 5)
                on(b[4], gates_out, 1)
                on(b[4], keep_x)
                on(b[7], expert_high, 6)
                on(b[7], expert_tanh, 8)
                on(b[7], expert_tanh, 9)
                on(b[4], decay, 0)
                on(b[7], expert_high, 7)
                on(b[4], decay, 1)
                on(b[7], expert_tanh, 10)
                on(b[4], mem_squares)
                on(b[7], expert_high, 8)
                on(b[5], maxima_transposed)
                on(b[7], expert_tanh, 11)
                on(b[5], exps, 0)
                on(b[7], expert_high, 9)
                once(b[2], weight_high, 0)
                on(b[5], exps, 1)
                on(b[7], keep_y)
                on(b[7], expert_tanh, 12)
                on(b[7], expert_high, 10)
                on(b[6], keep_x2)
                once(b[2], weight_high, 1)
                on(b[7], expert_tanh, 13)
                on(b[5], exps, 2)
                once(b[2], weight_high, 2)
                once(b[2], weight_high, 3)
                on(b[6], h_transposed)
                on(b[5], values_out, 0)
                once(b[2], weight_high, 4)
                on(b[5], exps, 3)

            act.wait_ge(cst_pool, 8)
            act.wait_ge(primed, 1)
            for j in range(LAGS):
                turn(j)
            with act.Fori(LAGS, BLOCKS) as j:
                turn(j)
            for j in range(BLOCKS, BLOCKS + LAGS):
                turn(j)

        @block.tensor
        def _(pe):
            pe.wait_ge(cst_loaded, 16 * len(consts))
            pe.wait_ge(cst_act, 3)
            pe.wait_ge(cst_dve, 2)
            pe.wait_ge(cst_pool, 8)

            def product(out, lhs, rhs, first=True, last=True):
                terms = [(l, r) for lp, rp in ((0, 0), (1, 0), (0, 1)) for l, r in zip(lhs[lp], rhs[rp])]
                for n, (l, r) in enumerate(terms):
                    ins = pe.matmul(out, l, r, start=first and n == 0, stop=last and n == len(terms) - 1,
                                    skip_group_check=True)
                return ins

            def chunks(pair, cols):
                return [[t[:, c, cols] for c in range(KC)] for t in pair]

            def turned(src, b):
                for t in range(TT):
                    for c in range(KC):
                        ins = pe.transpose(b[:, c * TOK + t * P:c * TOK + (t + 1) * P],
                                           src[:, t, c * P:(c + 1) * P], ident[:, :])
                return ins

            def turn_x(i):
                pe.wait_ge(xn_ready.sem, xn_ready.at(i, TT))
                pe.wait_ge(ot_low.sem, ot_low.at(i, 0))
                pe.wait_ge(ot_high.sem, ot_high.at(i, 0))
                turned(xn, bank_a[0]).then_inc(xt_ps.sem, 1)

            def project_qk(i, t):
                toks = slice(t * P, (t + 1) * P)
                need(pe, i, WQKV)
                pe.wait_ge(xt_high.sem, xt_high.at(i, 1))
                pe.wait_ge(xt_low.sem, xt_low.at(i, 1))
                if t == 0:
                    pe.wait_ge(x1_ready.sem, x1_ready.at(i, 0))
                else:
                    pe.wait_ge(v_gated.sem, v_gated.at(i, t))
                    pe.wait_ge(gam_tanh.sem, gam_tanh.at(i, t))
                product(bank_a[(t + 1) % 2][:, 0:512], chunks((xt_h, xt_l), toks),
                        chunks(wqkv, slice(0, 512))).then_inc(qk_ps.sem, 1)

            def project_v_gamma(i, t):
                toks = slice(t * P, (t + 1) * P)
                b = bank_a[t % 2]
                if t == 0:
                    pe.wait_ge(conv_taps.sem, conv_taps.at(i, KC * (CONV - 1)))
                    pe.wait_ge(conv_first.sem, conv_first.at(i, KC))
                else:
                    pe.wait_ge(gate_tanh.sem, gate_tanh.at(i, t))
                need(pe, i, WQKV)
                pe.wait_ge(xt_high.sem, xt_high.at(i, 1))
                pe.wait_ge(xt_low.sem, xt_low.at(i, 1))
                product(b[:, 0:DM], chunks((xt_h, xt_l), toks), chunks(wqkv, slice(512, 768)))
                need(pe, i, WGATE)
                pe.wait_ge(ct_high.sem, ct_high.at(i, 1))
                pe.wait_ge(ct_low.sem, ct_low.at(i, 1))
                product(b[:, DM:DM + HEADS], chunks((ct_h, ct_l), toks), chunks(wgate, slice(512, 528)), last=False)
                pe.matmul(b[:, DM:DM + HEADS], ones2[:, :], bias2[:, 512:528], start=False, stop=True,
                          skip_group_check=True).then_inc(vg_ps.sem, 1)

            def project_gates(i, t):
                toks = slice(t * P, (t + 1) * P)
                b = bank_a[(t + 1) % 2]
                need(pe, i, WGATE)
                pe.wait_ge(qk_square.sem, qk_square.at(i, t + 1))
                pe.wait_ge(ct_high.sem, ct_high.at(i, 1))
                pe.wait_ge(ct_low.sem, ct_low.at(i, 1))
                product(b[:, 0:512], chunks((ct_h, ct_l), toks), chunks(wgate, slice(0, 512)), last=False)
                pe.matmul(b[:, 0:512], ones2[:, :], bias2[:, 0:512], start=False, stop=True,
                          skip_group_check=True).then_inc(gate_ps.sem, 1)

            def turn_b_gamma(i, t):
                b = bank_a[(t + 1) % 2]
                pe.wait_ge(bkn_ready.sem, bkn_ready.at(i, 1))
                pe.wait_ge(gam_tanh.sem, gam_tanh.at(i, TT))
                if t == 0:
                    pe.wait_ge(v_gated.sem, v_gated.at(i, TT))
                else:
                    pe.wait_ge(gate_tanh.sem, gate_tanh.at(i, TT))
                for n, src in enumerate((bkn, gam)):
                    for c in range(KC):
                        ins = pe.transpose(b[:, (KC * n + c) * P:(KC * n + c + 1) * P],
                                           src[:, t, c * P:(c + 1) * P], ident[:, :])
                ins.then_inc(bg_ps.sem, 1)

            def center_mem(i):
                pe.wait_ge(mem_ready.sem, mem_ready.at(i, TT * KC))
                for t in range(TT):
                    for c in range(KC):
                        ins = pe.matmul(bank_a[1][:, t * DM + c * P:t * DM + (c + 1) * P], memt[:, t, c, :],
                                        center[:, :], start=True, stop=True, skip_group_check=True)
                ins.then_inc(ctr_ps.sem, 1)

            def turn_out(i):
                pe.wait_ge(o5_ready.sem, o5_ready.at(i, 1))
                pe.wait_ge(wx_kept.sem, wx_kept.at(i - ROUTER_BEHIND, 6))
                turned(o5, bank_a[0]).then_inc(ot_ps.sem, 1)

            def project_out(i):
                need(pe, i, WO)
                pe.wait_ge(ot_high.sem, ot_high.at(i, 1))
                pe.wait_ge(ot_low.sem, ot_low.at(i, 1))
                pe.wait_ge(m1_ready.sem, m1_ready.at(i, 1))
                for t in range(TT):
                    ins = product(bank_a[1][:, t * DM:(t + 1) * DM], chunks((ot_h, ot_l), slice(t * P, (t + 1) * P)),
                                  chunks(wo, slice(0, DM)))
                ins.then_inc(mix_ps.sem, 1)

            def turn_keys(i):
                pe.wait_ge(k_high.sem, k_high.at(i, 1))
                pe.wait_ge(k_low.sem, k_low.at(i, 1))
                pe.wait_ge(val_kept.sem, val_kept.at(i, 0))
                pe.sem_inc(held, 1)
                psum = bank_v[:, 0:256].bitcast(F16)
                for b in range(NB):
                    pe.transpose(psum[:, SEQ * b:SEQ * (b + 1)], k2[:, b, 0:2 * CTX], ident16[0:SEQ, 0:SEQ])
                    ins = pe.transpose(psum[0:CTX, 256 + SEQ * b:256 + SEQ * (b + 1)], k2[:, b, 2 * CTX:3 * CTX],
                                       ident16[0:SEQ, 0:SEQ])
                ins.then_inc(kt_ps.sem, 1)

            def turn_queries(i, t):
                pe.wait_ge(xq_ready.sem, xq_ready.at(i, t + 1))
                pe.wait_ge(att_norm.sem, att_norm.at(i, 3 * (t + 1) - 3 * TT))
                pe.sem_inc(held, 1)
                for g in range(G):
                    ins = pe.transpose(bank_b[t][0:64, g * P:(g + 1) * P], xq[:, t, g * CTX:(g + 1) * CTX], ident[:, :])
                ins.then_inc(qt_ps.sem, 1)

            def scores_by_row(i, n):
                b, gp = n // 2, n % 2
                if n == 0:
                    pe.wait_ge(k_masked.sem, k_masked.at(i, 2))
                    pe.wait_ge(q_low.sem, q_low.at(i, TT))
                elif n >= 2:
                    pe.wait_ge(row_max.sem, row_max.at(i, n - 1))
                pe.matmul(bank_b[n % 2][:, :], qs[0:64, b, 2 * gp:2 * gp + 2, :].rearrange("p g s -> p (g s)"),
                          kb[0:64, b, :, :].rearrange("p h s -> p (h s)"), start=True, stop=True,
                          skip_group_check=True).then_inc(row_ps.sem, 1)

            def turn_maxima(i):
                pe.wait_ge(row_max.sem, row_max.at(i, 2 * NB))
                pe.wait_ge(kt_kept.sem, kt_kept.at(i, 2))
                for gp in range(2):
                    ins = pe.transpose(bank_v[0:NB * KVH, gp * P:(gp + 1) * P],
                                       mx[:, gp, :, :].rearrange("p b h -> p (b h)"), ident[:, :])
                ins.then_inc(maxt_ps.sem, 1)

            def scores_by_column(i, n):
                b, jp = n // 2, n % 2
                need(pe, i, MAXSEL)
                if n == 0:
                    pe.wait_ge(maxt_kept.sem, maxt_kept.at(i, 1))
                if n >= 2:
                    pe.wait_ge(col_exp.sem, col_exp.at(i, n - 1))
                q = qs[:, b, :, :].rearrange("p g s -> p (g s)")
                for h in range(2):
                    j = 2 * jp + h
                    out = bank_b[n % 2][:, 256 * h:256 * h + 256]
                    pe.matmul(out, kb[:, b, 2 * j:2 * j + 2, :].rearrange("p h s -> p (h s)"), q,
                              start=True, stop=False, skip_group_check=True)
                    pe.matmul(out, kl[:, b, 2 * j:2 * j + 2, :].rearrange("p h s -> p (h s)"), q[0:64, :],
                              start=False, stop=False, skip_group_check=True)
                    ins = pe.matmul(out, maxsel[:, NPAIR * b + j, :], mxt[:, :], start=False, stop=True,
                                    skip_group_check=True)
                ins.then_inc(col_ps.sem, 1)

            def values(i, n):
                b, jp = n // 2, n % 2
                pe.wait_ge(col_exp.sem, col_exp.at(i, n + 1))
                if jp == 0:
                    pe.wait_ge(val_kept.sem, val_kept.at(i, b))
                    if b == 0:
                        pe.wait_ge(v_block.sem, v_block.at(i, 2))
                for h in range(2):
                    j = 2 * jp + h
                    ins = pe.matmul(bank_v[32 * j:32 * j + 32, 256 * (b % 2):256 * (b % 2) + 256], vblk[:, b, j, :],
                                    prob[n % 2][:, 256 * h:256 * h + 256], start=True, stop=True, skip_group_check=True)
                ins.then_inc(val_ps.sem, 1)

            def turn_values(i, t):
                pe.wait_ge(val_kept.sem, val_kept.at(i, 2 * t + 2))
                pe.wait_ge(col_exp.sem, col_exp.at(i, 2 * NB))
                for g in range(G):
                    ins = pe.transpose(bank_b[t][:, g * P:(g + 1) * P], avs[:, t, g, :, :].rearrange("p b s -> p (b s)"), ident[:, :])
                ins.then_inc(att_ps.sem, 1)

            def turn_h(i):
                pe.wait_ge(hn_ready.sem, hn_ready.at(i, TT))
                if not isinstance(i, int) or i + ROUTER_BEHIND < BLOCKS:
                    pe.wait_ge(mem_ready.sem, mem_ready.at(i + ROUTER_BEHIND, TT * KC))
                    pe.wait_ge(m1_ready.sem, m1_ready.at(i + ROUTER_BEHIND, 1))
                else:
                    pe.wait_ge(wx_kept.sem, wx_kept.at(i, 0))
                turned(hn, bank_a[0]).then_inc(ht_ps.sem, 1)

            def router_logits(i):
                need(pe, i, WRT)
                pe.wait_ge(ht_high.sem, ht_high.at(i, 1))
                pe.wait_ge(ht_low.sem, ht_low.at(i, 1))
                for t in range(TT):
                    ins = product(bank_a[1][:, EXPERTS * t:EXPERTS * (t + 1)],
                                  chunks((ht_h, ht_l), slice(t * P, (t + 1) * P)), chunks(wrt, slice(0, EXPERTS)))
                ins.then_inc(logit_ps.sem, 1)

            def turn_weights(i):
                pe.wait_ge(route.sem, route.at(i, 20))
                psum = bank_a[0][0:16, 0:128].bitcast(F16)
                for t in range(TT):
                    ins = pe.transpose(psum[:, t * P:(t + 1) * P], whl[:, t, :], ident16[:, :])
                ins.then_inc(wt_ps.sem, 1)

            def spread_weights(i, n):
                need(pe, i, WSEL)
                if n == 0:
                    pe.wait_ge(wt_kept.sem, wt_kept.at(i, 1))
                    pe.wait_ge(logit_exp.sem, logit_exp.at(i, TT))
                if n >= 2:
                    pe.wait_ge(wx_kept.sem, wx_kept.at(i, n - 1))
                for k in range(2 * n, min(2 * n + 2, FTR)):
                    ins = pe.matmul(bank_a[(n + 1) % 2][:, (k % 2) * TOK:(k % 2 + 1) * TOK], wsel[:, k, :], wt[:, :],
                                    start=True, stop=True, skip_group_check=True)
                ins.then_inc(wx_ps.sem, 1)

            def gate_up(i, k):
                cols = slice(k * P, (k + 1) * P)
                need(pe, i, WFU)
                if k == 0:
                    pe.wait_ge(ht_high.sem, ht_high.at(i, 1))
                    pe.wait_ge(ht_low.sem, ht_low.at(i, 1))
                pe.wait_ge(up_done.sem, up_done.at(i, k - 1))
                h = chunks((ht_h, ht_l), slice(0, TOK))
                product(bank_gu[k % 2][:, 0:TOK], chunks(wfg, cols), h)
                product(bank_gu[k % 2][:, TOK:2 * TOK], chunks(wfu, cols), h).then_inc(gu_ps.sem, 1)

            def down(i, k):
                need(pe, i, WFD)
                pe.wait_ge(hid_high.sem, hid_high.at(i, k + 1))
                pe.wait_ge(hid_low.sem, hid_low.at(i, k + 1))
                if k == 0:
                    pe.wait_ge(y_ready.sem, y_ready.at(i, 0))
                for t in range(TT):
                    toks = slice(t * P, (t + 1) * P)
                    hh, hl = hid_h[k % 2], hid_l[k % 2]
                    for n, (l, r) in enumerate(((hh, wfd[0]), (hl, wfd[0]), (hh, wfd[1]))):
                        ins = pe.matmul(bank_dn[:, t * DM:(t + 1) * DM], l[:, toks], r[:, k, :],
                                        start=k == 0 and t == 0 and n == 0, stop=k == FT - 1 and n == 2,
                                        skip_group_check=True)
                ins.then_inc(down_ps.sem, 1)

            def turn(j):
                b = blocks(j)
                on(b[1], project_gates, 1)
                on(b[4], down, 4)
                on(b[2], scores_by_row, 2)
                on(b[2], scores_by_row, 3)
                on(b[4], gate_up, 8)
                on(b[4], gate_up, 9)
                on(b[2], scores_by_row, 4)
                on(b[4], down, 5)
                on(b[1], turn_b_gamma, 0)
                on(b[4], down, 6)
                on(b[1], turn_b_gamma, 1)
                on(b[2], scores_by_row, 5)
                on(b[4], gate_up, 10)
                on(b[2], scores_by_row, 6)
                on(b[1], center_mem)
                on(b[2], scores_by_row, 7)
                on(b[4], gate_up, 11)
                on(b[4], down, 7)
                on(b[2], turn_maxima)
                on(b[4], down, 8)
                on(b[2], scores_by_column, 0)
                on(b[4], gate_up, 12)
                on(b[2], scores_by_column, 1)
                on(b[2], values, 0)
                on(b[4], gate_up, 13)
                on(b[2], values, 1)
                on(b[2], scores_by_column, 2)
                on(b[3], turn_h)
                on(b[4], down, 9)
                on(b[2], scores_by_column, 3)
                on(b[2], values, 2)
                on(b[3], router_logits)
                on(b[4], down, 10)
                on(b[2], scores_by_column, 4)
                on(b[2], values, 3)
                on(b[2], scores_by_column, 5)
                on(b[3], gate_up, 0)
                on(b[2], scores_by_column, 6)
                on(b[2], values, 4)
                on(b[2], values, 5)
                on(b[4], down, 11)
                on(b[2], scores_by_column, 7)
                on(b[3], gate_up, 1)
                on(b[3], turn_weights)
                on(b[4], down, 12)
                on(b[3], spread_weights, 0)
                on(b[2], values, 6)
                on(b[3], spread_weights, 1)
                on(b[2], values, 7)
                on(b[2], turn_values, 0)
                on(b[3], spread_weights, 2)
                on(b[3], spread_weights, 3)
                on(b[3], gate_up, 2)
                on(b[3], spread_weights, 4)
                on(b[3], spread_weights, 5)
                on(b[2], turn_values, 1)
                on(b[4], down, 13)
                on(b[1], turn_out)
                on(b[3], gate_up, 3)
                on(b[3], down, 0)
                on(b[0], turn_x)
                on(b[1], project_out)
                on(b[3], gate_up, 4)
                on(b[1], turn_keys)
                on(b[3], down, 1)
                on(b[0], project_qk, 0)
                on(b[3], gate_up, 5)
                on(b[3], down, 2)
                on(b[0], project_gates, 0)
                on(b[1], turn_queries, 0)
                on(b[3], down, 3)
                on(b[1], turn_queries, 1)
                on(b[0], project_v_gamma, 0)
                on(b[3], gate_up, 6)
                on(b[0], project_qk, 1)
                on(b[1], scores_by_row, 0)
                on(b[1], scores_by_row, 1)
                on(b[0], project_v_gamma, 1)
                on(b[3], gate_up, 7)

            pe.wait_ge(primed, 1)
            for j in range(LAGS):
                turn(j)
            with pe.Fori(LAGS, BLOCKS) as j:
                turn(j)
            for j in range(BLOCKS, BLOCKS + LAGS):
                turn(j)

        @block.vector
        def _(dve):
            dve.wait_ge(cst_loaded, 16 * len(consts))
            dve.tensor_scalar(gn8[:, :, :], rows[:, 2:4, :], SN, None, ALU.mult).then_inc(cst_dve, 1)
            dve.wait_ge(cst_act, 3)
            dve.scalar_tensor_tensor(bias2[32:33, :], bias_f[32:33, :], SW, bias2[32:33, :], ALU.mult,
                                     ALU.subtract).then_inc(cst_dve, 1)

            def weight_low(i, n):
                src, high, low, scale = loads[n]
                dve.wait_ge(stage_high, n + 1)
                dve.scalar_tensor_tensor(low, stage[n % 2][:, 0:src.shape[1]], scale, high, ALU.mult,
                                         ALU.subtract).then_inc(stage_split, 1)

            def inverse_root(i, chain, k, n, y, t, v):
                dve.wait_ge(chain.sem, chain.at(i, k + n))
                if n == 0:
                    ins = dve.tensor_scalar(y.bitcast(I32), v.bitcast(I32), -0.5, MAGIC, ALU.mult, ALU.add)
                elif n == 10:
                    ins = dve.tensor_scalar(y, y, -0.125, None, ALU.mult)
                elif n % 3 == 1:
                    ins = dve.scalar_tensor_tensor(t, y, 0.25 ** (n // 3), y, ALU.mult, ALU.mult)
                elif n % 3 == 2:
                    ins = dve.tensor_tensor(t, t, v, ALU.mult)
                else:
                    ins = dve.scalar_tensor_tensor(y, t, -3.0, y, ALU.add, ALU.mult)
                ins.then_inc(chain.sem, 1)

            def norm_stats(i, x, st, mv, ve, stat, ready, ready_k, rstd):
                dve.wait_ge(ready.sem, ready.at(i, ready_k))
                for t in range(TT):
                    dve.bn_stats(st[:, t, :], x[:, t, :]).then_inc(stat.sem, 1)
                for t in range(TT):
                    dve.wait_ge(stat.sem, stat.at(i, t + 1))
                    dve.sem_inc(held, 1)
                    dve.bn_aggr(mv[:, t, :], st[:, t, :]).then_inc(stat.sem, 1)
                dve.wait_ge(stat.sem, stat.at(i, 4))
                dve.wait_ge(rstd.sem, rstd.at(i, 0))
                dve.tensor_scalar(ve[:, :], mv[:, :, 1], 1.0 / SX ** 2, EPS / SX ** 2, ALU.mult,
                                  ALU.add).then_inc(stat.sem, 1)

            def norm_apply(i, x, mv, rs, out, rstd, done, free, view=lambda z: z, out_view=lambda z: z):
                dve.wait_ge(rstd.sem, rstd.at(i, 1))
                dve.wait_ge(free.sem, free.at(i, 0))
                for t in range(TT):
                    dve.tensor_scalar(out_view(out[:, t, :]), view(x[:, t, :]), mv[:, t, 0:1], rs[:, t:t + 1], ALU.subtract,
                                      ALU.mult).then_inc(done.sem, 1)

            def norm1_stats(i):
                norm_stats(i, x_in, st1, mv1, ve1, ln1_stat, x_loaded, 16, ln1_rstd)

            def norm1_apply(i):
                norm_apply(i, x_in, mv1, rs1, xn, ln1_rstd, xn_ready, xt_ps)

            def norm2_stats(i):
                norm_stats(i, x1, st2, mv2, ve2, ln2_stat, x1_ready, 1, ln2_rstd)

            def norm2_apply(i):
                norm_apply(i, x1, mv2, rs2, xq, ln2_rstd, xq_ready, qt_ps,
                           view=lambda z: z.rearrange("p (h g d) -> p h g d", h=KVH, g=G),
                           out_view=lambda z: z.rearrange("p (g h d) -> p h g d", h=KVH, g=G))

            def norm3_stats(i):
                norm_stats(i, x2, st3, mv3, ve3, ln3_stat, x2_ready, TT, ln3_rstd)

            def norm3_apply(i):
                norm_apply(i, x2, mv3, rs3, hn, ln3_rstd, hn_ready, ht_ps)

            def x_low(i):
                dve.wait_ge(conv_first.sem, conv_first.at(i, KC))
                dve.wait_ge(xt_high.sem, xt_high.at(i, 1))
                psum = bank_a[0][:, :].rearrange("p (c t) -> p c t", c=KC)
                dve.wait_ge(vg_ps.sem, vg_ps.at(i, 0))
                dve.tensor_tensor(xt_l[:, :, :], psum, xt_h[:, :, :], ALU.subtract).then_inc(xt_low.sem, 1)

            def conv(i, tap):
                psum = bank_a[0][:, :].rearrange("p (c b s) -> p c b s", c=KC, b=NB)
                for c in range(KC):
                    if tap == 1:
                        dve.wait_ge(conv_first.sem, conv_first.at(i, c + 1))
                        if c == 0:
                            dve.wait_ge(xt_high.sem, xt_high.at(i, 1))
                    else:
                        dve.wait_ge(conv_taps.sem, conv_taps.at(i, KC * (tap - 2) + c + 1))
                    dve.scalar_tensor_tensor(cacc[:, c, :, tap:SEQ], psum[:, c, :, 0:SEQ - tap],
                                             convw[:, c, CONV - 1 - tap:CONV - tap], cacc[:, c, :, tap:SEQ],
                                             ALU.mult, ALU.add).then_inc(conv_taps.sem, 1)

            def silu(i):
                dve.wait_ge(conv_tanh.sem, conv_tanh.at(i, 1))
                dve.wait_ge(ct_low.sem, ct_low.at(i, 0))
                dve.wait_ge(ct_high.sem, ct_high.at(i, 0))
                dve.scalar_tensor_tensor(csil[:, :, :], cth[:, :, :], 1.0, cacc[:, :, :, :].rearrange("p c b s -> p c (b s)"),
                                         ALU.add, ALU.mult).then_inc(conv_silu.sem, 1)

            def gate_values(i, t):
                dve.wait_ge(gate_tanh.sem, gate_tanh.at(i, t + 1))
                dve.wait_ge(vg_ps.sem, vg_ps.at(i, t + 1))
                dve.wait_ge(gam_tanh.sem, gam_tanh.at(i, t + 1))
                dve.wait_ge(bkn_ready.sem, bkn_ready.at(i, 0))
                dve.scalar_tensor_tensor(bv[:, t, :], gate_t[:, t, 0:DM], 1.0, bank_a[t % 2][:, 0:DM],
                                         ALU.add, ALU.mult).then_inc(v_gated.sem, 1)

            def qk_sum(i, t):
                dve.wait_ge(qk_square.sem, qk_square.at(i, t + 1))
                dve.wait_ge(qk_norm.sem, qk_norm.at(i, 0))
                dve.tensor_reduce(ss_qk[:, t, :], qk_sq[:, t, :].rearrange("p (h d) -> p h d", d=HD), AX_X,
                                  ALU.add).then_inc(qk_sums.sem, 1)

            def flat_heads(t):
                return t[:, :, :].rearrange("p t h -> p (t h)")

            def qk_root(i, n):
                if n == 0:
                    dve.wait_ge(qk_sums.sem, qk_sums.at(i, TT))
                    dve.wait_ge(qn_ready.sem, qn_ready.at(i, 0))
                    dve.wait_ge(bkn_ready.sem, bkn_ready.at(i, 0))
                    dve.tensor_scalar(flat_heads(ss_qk), flat_heads(ss_qk), SP_ ** 2 * 1e-24, None,
                                      ALU.max).then_inc(qk_norm.sem, 1)
                else:
                    inverse_root(i, qk_norm, 1, n - 1, flat_heads(r_qk), flat_heads(t_qk), flat_heads(ss_qk))

            def scan(i, t):
                b = bank_a[(t + 1) % 2]
                dve.wait_ge(decay_ready.sem, decay_ready.at(i, t + 1))
                dve.wait_ge(ctr_ps.sem, ctr_ps.at(i, 0))
                for c in range(KC):
                    dve.tensor_tensor_scan(memt[:, t, c, :], at[:, t, c, :, :].rearrange("p b s -> p (b s)"),
                                           b[:, c * P:(c + 1) * P], 0.0, ALU.mult, ALU.add).then_inc(mem_ready.sem, 1)

            def head_root(i, n, sq, ss, v, r, t, norm, squared, scale):
                if n == 0:
                    dve.wait_ge(squared.sem, squared.at(i, 1))
                    dve.tensor_reduce(flat_heads(ss), sq[:, :, :].rearrange("p t (h d) -> p (t h) d", d=HD), AX_X,
                                      ALU.add).then_inc(norm.sem, 1)
                elif n == 1:
                    dve.wait_ge(norm.sem, norm.at(i, 1))
                    dve.tensor_scalar(flat_heads(v), flat_heads(ss), 1.0 / HD, EPS * scale ** 2, ALU.mult,
                                      ALU.add).then_inc(norm.sem, 1)
                else:
                    inverse_root(i, norm, 2, n - 2, flat_heads(r), flat_heads(t), flat_heads(v))

            def mem_root(i, n):
                head_root(i, n, msq, ss_m, v_m, r_m, t_m, mem_norm, mem_square, SM)

            def out_root(i, n):
                head_root(i, n, osq, ss_o, v_o, r_o, t_o, out_norm, out_square, 1.0)

            def heads(t):
                return t.rearrange("p t (h d) -> p (t h) d", d=HD)

            def per_head(r):
                return r[:, :, :].rearrange("p t h -> p (t h)").unsqueeze(2).broadcast_to([P, TT * HEADS, HD])

            def mem_scaled(i):
                dve.wait_ge(mem_norm.sem, mem_norm.at(i, 13))
                dve.wait_ge(o1_ready.sem, o1_ready.at(i, 0))
                dve.tensor_tensor(heads(m1[:, :, :]), bank_a[1][:, :].rearrange("p (h d) -> p h d", d=HD), per_head(r_m),
                                  ALU.mult).then_inc(m1_ready.sem, 1)

            def out_sums(i):
                dve.wait_ge(o1_ready.sem, o1_ready.at(i, 1))
                dve.tensor_reduce(sum_o[:, :, :].rearrange("p t h -> p (t h)"), heads(o1[:, :, :]), AX_X,
                                  ALU.add).then_inc(out_center.sem, 1)

            def center_out(i):
                dve.wait_ge(out_center.sem, out_center.at(i, 1))
                dve.scalar_tensor_tensor(heads(oc[:, :, :]), per_head(sum_o), -1.0 / HD, heads(o1[:, :, :]), ALU.mult,
                                         ALU.add).then_inc(out_center.sem, 1)

            def out_scaled(i):
                dve.wait_ge(out_norm.sem, out_norm.at(i, 13))
                dve.wait_ge(o5_ready.sem, o5_ready.at(i, 0))
                dve.tensor_tensor(heads(o2[:, :, :]), heads(oc[:, :, :]), per_head(r_o), ALU.mult).then_inc(o2_ready.sem, 1)

            def gate_out(i):
                dve.wait_ge(o4_ready.sem, o4_ready.at(i, 1))
                dve.wait_ge(ot_ps.sem, ot_ps.at(i, 0))
                dve.scalar_tensor_tensor(o5[:, :, :], gate_t[:, :, DM:2 * DM], 1.0, o2[:, :, :], ALU.add,
                                         ALU.mult).then_inc(o5_ready.sem, 1)

            def out_low(i):
                dve.wait_ge(ot_high.sem, ot_high.at(i, 1))
                dve.wait_ge(mix_ps.sem, mix_ps.at(i, 0))
                dve.tensor_tensor(ot_l[:, :, :], bank_a[0][:, :].rearrange("p (c t) -> p c t", c=KC), ot_h[:, :, :],
                                  ALU.subtract).then_inc(ot_low.sem, 1)

            def mixer_residual(i):
                dve.wait_ge(mix_ps.sem, mix_ps.at(i, 1))
                dve.wait_ge(x_kept.sem, x_kept.at(i, 1))
                dve.wait_ge(x2_ready.sem, x2_ready.at(i, 0))
                dve.scalar_tensor_tensor(x1[:, :, :], bank_a[1][:, :].rearrange("p (t d) -> p t d", t=TT),
                                         1.0 / (2.0 * SN * SW), x_res[:, :, :], ALU.mult, ALU.add).then_inc(x1_ready.sem, 1)

            def keys_low(i):
                dve.wait_ge(k_high.sem, k_high.at(i, 1))
                dve.scalar_tensor_tensor(k2[:, :, 2 * CTX:3 * CTX], ctxs[0:SEQ, :, :], SK, k2[:, :, 0:CTX], ALU.mult,
                                         ALU.subtract).then_inc(k_low.sem, 1)

            def mask_keys(i):
                need(dve, i, KMASK)
                dve.wait_ge(kt_kept.sem, kt_kept.at(i, 2))
                dve.wait_ge(col_ps.sem, col_ps.at(i, 0))
                for src, dst, rows_ in ((kt, kb, P), (ktl, kl, CTX)):
                    dve.tensor_tensor(dst[:, :, :, :], src[:, :, :].unsqueeze(2).broadcast_to([rows_, NB, KVH, SEQ]),
                                      kmask[0:rows_, :, :].unsqueeze(1).broadcast_to([rows_, NB, KVH, SEQ]),
                                      ALU.mult).then_inc(k_masked.sem, 1)

            def queries_low(i, t):
                dve.wait_ge(q_high.sem, q_high.at(i, t + 1))
                dve.tensor_tensor(qs[64:128, 2 * t:2 * t + 2, :, :].rearrange("p b g s -> p g b s"),
                                  bank_b[t][0:64, :].rearrange("p (g b s) -> p g b s", g=G, b=2),
                                  qs[0:64, 2 * t:2 * t + 2, :, :].rearrange("p b g s -> p g b s"),
                                  ALU.subtract).then_inc(q_low.sem, 1)

            def maxima(i, n):
                b, gp = n // 2, n % 2
                dve.wait_ge(row_ps.sem, row_ps.at(i, n + 1))
                if n == 0:
                    dve.wait_ge(maxt_ps.sem, maxt_ps.at(i, 0))
                dve.tensor_reduce(mx[:, gp, b, :], bank_b[n % 2][:, :].rearrange("p (h s) -> p h s", s=SEQ), AX_X,
                                  ALU.max).then_inc(row_max.sem, 1)

            def attention_norm(i, t):
                cols = bank_b[t][:, :].rearrange("p (g j m) -> p g j m", g=G, j=NPAIR)
                dve.wait_ge(att_ps.sem, att_ps.at(i, t + 1))
                dve.wait_ge(x2_ready.sem, x2_ready.at(i, t + 1 - TT))
                dve.reciprocal(orec[:, t, :, :, :], cols[:, :, :, 16:18]).then_inc(att_norm.sem, 1)
                dve.wait_ge(att_norm.sem, att_norm.at(i, 3 * t + 1))
                out = oatt[:, t, :].rearrange("p (j h g d) -> p g j h d", j=NPAIR, h=2, g=G)
                for h in range(2):
                    dve.tensor_tensor(out[:, :, :, h, :], cols[:, :, :, 8 * h:8 * h + 8],
                                      orec[:, t, :, :, h:h + 1].broadcast_to([P, G, NPAIR, HQ]),
                                      ALU.mult).then_inc(att_norm.sem, 1)

            def h_low(i):
                dve.wait_ge(ht_high.sem, ht_high.at(i, 1))
                dve.wait_ge(gu_ps.sem, gu_ps.at(i, 0))
                dve.tensor_tensor(ht_l[:, :, :], bank_a[0][:, :].rearrange("p (c t) -> p c t", c=KC), ht_h[:, :, :],
                                  ALU.subtract).then_inc(ht_low.sem, 1)

            def per_group(t):
                return t[:, :, :].rearrange("p t (g e) -> p (t g) e", e=2)

            def softmax(i, n):
                logits = bank_a[1][:, 0:TT * EXPERTS].rearrange("p (t e) -> p t e", e=EXPERTS)
                if n == 0:
                    dve.wait_ge(logit_ps.sem, logit_ps.at(i, 1))
                    ins = dve.tensor_reduce(lmax[:, :], logits, AX_X, ALU.max)
                else:
                    dve.wait_ge(route.sem, route.at(i, n))
                if n == 1:
                    ins = dve.tensor_scalar(lneg[:, :], lmax[:, :], -1.0 / SP_, None, ALU.mult)
                elif n == 2:
                    dve.wait_ge(logit_exp.sem, logit_exp.at(i, TT))
                    ins = dve.tensor_reduce(lsum[:, :], lexp[:, :, :], AX_X, ALU.add)
                elif n == 3:
                    ins = dve.reciprocal(lrec[:, :], lsum[:, :])
                elif n == 4:
                    ins = dve.tensor_tensor(prb[:, :, :], lexp[:, :, :],
                                            lrec[:, :].unsqueeze(2).broadcast_to([P, TT, EXPERTS]), ALU.mult)
                elif n == 5:
                    ins = dve.tensor_reduce(gs[:, :, :].rearrange("p t g -> p (t g)"), per_group(prb), AX_X, ALU.max)
                ins.then_inc(route.sem, 1)

            def rank(i, n, k, v, gt, eq, cnt, out, before, size):
                shape = [P, TT, size, size]
                other, own = v[:, :, :].unsqueeze(2).broadcast_to(shape), v[:, :, :].unsqueeze(3).broadcast_to(shape)
                dve.wait_ge(route.sem, route.at(i, k if n < 2 else k + n))
                if n == 0:
                    ins = dve.tensor_tensor(gt[:, :, :, :], other, own, ALU.is_gt)
                elif n == 1:
                    ins = dve.tensor_tensor(eq[:, :, :, :], other, own, ALU.is_equal)
                elif n == 2:
                    ins = dve.tensor_tensor(eq[:, :, :, :], eq[:, :, :, :], before.unsqueeze(1).broadcast_to(shape), ALU.mult)
                elif n == 3:
                    ins = dve.tensor_tensor(cnt[:, :, :, :], gt[:, :, :, :], eq[:, :, :, :], ALU.add)
                else:
                    ins = dve.tensor_reduce(out[:, :], cnt[:, :, :, :].rearrange("p t a b -> p (t a) b"), AX_X, ALU.add)
                ins.then_inc(route.sem, 1)

            def group_rank(i, n):
                rank(i, n, 6, gs, ggt, geq, gcnt, grank, tri4, 4)

            def keep_groups(i):
                dve.wait_ge(route.sem, route.at(i, 11))
                dve.scalar_tensor_tensor(per_group(pm), grank[:, :].unsqueeze(2).broadcast_to([P, TT * 4, 2]), 2.0,
                                         per_group(prb), ALU.is_lt, ALU.mult).then_inc(route.sem, 1)

            def expert_rank(i, n):
                rank(i, n, 12, pm, egt, eeq, ecnt, erank, tri8, 8)

            def keep_experts(i):
                dve.wait_ge(route.sem, route.at(i, 17))
                dve.scalar_tensor_tensor(wts[:, :, :].rearrange("p t e -> p (t e)"), erank[:, :], 2.0,
                                         pm[:, :, :].rearrange("p t e -> p (t e)"), ALU.is_lt,
                                         ALU.mult).then_inc(route.sem, 1)

            def weights_high(i):
                dve.wait_ge(route.sem, route.at(i, 18))
                dve.wait_ge(wt_ps.sem, wt_ps.at(i, 0))
                dve.tensor_scalar(whl[:, :, 0:8], wts[:, :, :], SW, None, ALU.mult).then_inc(route.sem, 1)

            def weights_low(i):
                dve.wait_ge(route.sem, route.at(i, 19))
                dve.scalar_tensor_tensor(whl[:, :, 8:16], wts[:, :, :], SW, whl[:, :, 0:8], ALU.mult,
                                         ALU.subtract).then_inc(route.sem, 1)

            def expert_silu(i, k):
                dve.wait_ge(tanh_done.sem, tanh_done.at(i, k + 1))
                dve.scalar_tensor_tensor(ff_g[k % 2][:, :], ff_tanh[k % 2][:, :], 1.0, bank_gu[k % 2][:, 0:TOK], ALU.add,
                                         ALU.mult).then_inc(silu_done.sem, 1)

            def expert_up(i, k):
                scale = SH / (2.0 * SP_ ** 2) * (1.0 if k < FTS else 4.0)
                dve.wait_ge(silu_done.sem, silu_done.at(i, k + 1))
                b, n = (i, k - 2) if k >= 2 else (i - 1, k - 2 + FT)
                if n >= FTS:
                    dve.wait_ge(weighted.sem, weighted.at(b, n - FTS + 1))
                else:
                    dve.wait_ge(hid_low.sem, hid_low.at(b, n + 1))
                dve.scalar_tensor_tensor(ff_u[k % 2][:, :], ff_g[k % 2][:, :], scale, bank_gu[k % 2][:, TOK:2 * TOK],
                                         ALU.mult, ALU.mult).then_inc(up_done.sem, 1)

            def expert_residual(i):
                dve.wait_ge(down_ps.sem, down_ps.at(i, FT))
                dve.wait_ge(y_based.sem, y_based.at(i, 1))
                dve.scalar_tensor_tensor(y_sb[:, :, :], bank_dn[:, :].rearrange("p (t d) -> p t d", t=TT),
                                         1.0 / (SH * SW), y_sb[:, :, :], ALU.mult, ALU.add).then_inc(y_ready.sem, 1)

            def turn(j):
                b = blocks(j)
                on(b[2], qk_root, 4)
                on(b[2], qk_root, 5)
                once(b[1], weight_low, 2)
                on(b[2], gate_values, 1)
                for n in range(6, 12):
                    on(b[2], qk_root, n)
                on(b[3], maxima, 2)
                on(b[4], norm3_stats)
                on(b[5], expert_silu, 8)
                on(b[3], maxima, 3)
                on(b[5], expert_up, 8)
                on(b[3], maxima, 4)
                on(b[2], scan, 0)
                once(b[1], weight_low, 6)
                on(b[5], expert_silu, 9)
                on(b[2], scan, 1)
                on(b[5], expert_up, 9)
                for n in range(5, 8):
                    on(b[3], maxima, n)
                on(b[5], expert_silu, 10)
                on(b[2], mem_root, 0)
                on(b[2], mem_root, 1)
                once(b[1], weight_low, 8)
                on(b[2], mem_root, 2)
                on(b[2], mem_root, 3)
                on(b[5], expert_up, 10)
                for n in range(4, 9):
                    on(b[2], mem_root, n)
                on(b[5], expert_silu, 11)
                for n in range(9, 12):
                    on(b[2], mem_root, n)
                on(b[5], expert_up, 11)
                on(b[2], mem_root, 12)
                on(b[2], mem_scaled)
                on(b[4], norm3_apply)
                on(b[1], norm1_stats)
                on(b[5], expert_silu, 12)
                on(b[5], expert_up, 12)
                on(b[5], expert_silu, 13)
                on(b[4], h_low)
                on(b[4], softmax, 0)
                on(b[4], softmax, 1)
                on(b[5], expert_up, 13)
                on(b[4], softmax, 2)
                on(b[4], softmax, 3)
                once(b[1], weight_low, 9)
                on(b[2], out_sums)
                on(b[4], softmax, 4)
                on(b[4], softmax, 5)
                once(b[1], weight_low, 10)
                on(b[2], center_out)
                for n in range(0, 5):
                    on(b[4], group_rank, n)
                on(b[2], out_root, 0)
                on(b[4], keep_groups)
                once(b[1], weight_low, 11)
                on(b[2], out_root, 1)
                on(b[4], expert_rank, 0)
                on(b[4], expert_rank, 1)
                on(b[2], out_root, 2)
                on(b[4], expert_rank, 2)
                on(b[2], out_root, 3)
                on(b[4], expert_rank, 3)
                on(b[2], out_root, 4)
                on(b[4], expert_rank, 4)
                on(b[2], out_root, 5)
                on(b[4], keep_experts)
                on(b[2], out_root, 6)
                on(b[4], weights_high)
                on(b[4], weights_low)
                for n in range(7, 13):
                    on(b[2], out_root, n)
                on(b[2], out_scaled)
                on(b[4], expert_silu, 0)
                once(b[1], weight_low, 12)
                on(b[4], expert_up, 0)
                on(b[3], attention_norm, 0)
                on(b[1], norm1_apply)
                on(b[4], expert_silu, 1)
                on(b[2], gate_out)
                on(b[4], expert_up, 1)
                on(b[3], attention_norm, 1)
                on(b[5], expert_residual)
                on(b[2], out_low)
                on(b[4], expert_silu, 2)
                on(b[4], expert_up, 2)
                on(b[4], expert_silu, 3)
                on(b[2], keys_low)
                on(b[4], expert_up, 3)
                on(b[2], mixer_residual)
                on(b[1], x_low)
                for n in range(1, 4):
                    on(b[1], conv, n)
                on(b[2], norm2_stats)
                on(b[4], expert_silu, 4)
                on(b[4], expert_up, 4)
                on(b[1], silu)
                on(b[2], norm2_apply)
                on(b[2], mask_keys)
                on(b[4], expert_silu, 5)
                on(b[1], gate_values, 0)
                on(b[2], queries_low, 0)
                on(b[2], queries_low, 1)
                on(b[1], qk_sum, 0)
                once(b[1], weight_low, 13)
                on(b[4], expert_up, 5)
                on(b[2], maxima, 0)
                on(b[2], maxima, 1)
                on(b[1], qk_sum, 1)
                on(b[4], expert_silu, 6)
                once(b[0], weight_low, 0)
                on(b[1], qk_root, 0)
                on(b[4], expert_up, 6)
                once(b[0], weight_low, 1)
                on(b[1], qk_root, 1)
                on(b[4], expert_silu, 7)
                on(b[1], qk_root, 2)
                on(b[4], expert_up, 7)
                on(b[1], qk_root, 3)

            dve.wait_ge(primed, 1)
            for j in range(LAGS):
                turn(j)
            with dve.Fori(LAGS, BLOCKS) as j:
                turn(j)
            for j in range(BLOCKS, BLOCKS + LAGS):
                turn(j)


def kernel(x, ctx_512, L0_attn_Wq, L0_attn_Wk, L0_attn_Wv, L0_attn_Wo, L0_attn_conv_w, L0_attn_conv_b,
           L0_attn_Wig, L0_attn_b_ig, L0_attn_Wog, L0_attn_b_og, L0_attn_Wg, L0_attn_b_g, L0_attn_gn_w,
           L0_attn_gn_b, L0_attn_mn_w, L0_attn_mn_b, L0_ffn_gate_weight, L0_ffn_gate_w, L0_ffn_up_w,
           L0_ffn_down_w, L0_ffn_sh_gate_w, L0_ffn_sh_up_w, L0_ffn_sh_down_w):
    import numpy as np
    import concourse.bacc as bacc
    from concourse.bass_utils import run_bass_kernel_spmd

    arr = np.asarray

    def by_partition(w):
        return np.ascontiguousarray(w.reshape(-1, P, w.shape[1]).transpose(1, 0, 2).reshape(P, -1))

    def padded(w, n):
        return np.concatenate([w, np.zeros((n - w.shape[0], w.shape[1]), w.dtype)], 0)

    def hidden_rows(routed, shared):
        return np.concatenate([padded(shared, FTS * P), routed.reshape(-1, DM)], 0)

    eye = np.eye(P, dtype=np.float32)
    same_head = np.kron(np.eye(P // HD, dtype=np.float32), np.ones((HD, HD), np.float32))
    kmask = np.zeros((P, KVH, SEQ), np.float32)
    for p in range(P):
        kmask[p, (p % CTX) // HQ] = 1.0
    maxsel = np.zeros((NB, KVH, NB, NPAIR, 2, SEQ), np.float32)
    for b in range(NB):
        for h in range(KVH):
            maxsel[b, h, b, h // 2, h % 2] = -1.0
    wsel = np.zeros((2, EXPERTS, FTR * P), np.float32)
    for e in range(EXPERTS):
        wsel[:, e, e * FEXP:(e + 1) * FEXP] = 1.0 / (4.0 * SW)
    tri = np.concatenate([np.tril(np.ones((n, n), np.float32), -1).reshape(-1) for n in (4, 8)])

    b = np.concatenate([arr(L0_attn_b_ig), arr(L0_attn_b_og), arr(L0_attn_b_g)])[None, :]
    zeros = np.zeros((31, b.shape[1]), b.dtype)
    bias = np.concatenate([b, zeros, b], 0)

    ins = {
        "x": arr(x).reshape(-1, DM), "ctx": arr(ctx_512),
        "wqkv": by_partition(np.concatenate([arr(w).T for w in (L0_attn_Wq, L0_attn_Wk, L0_attn_Wv)], 1)),
        "wgate": by_partition(np.concatenate([arr(w).T for w in (L0_attn_Wig, L0_attn_Wog, L0_attn_Wg)], 1)),
        "bias": bias,
        "wo": by_partition(arr(L0_attn_Wo).T), "wrt": by_partition(arr(L0_ffn_gate_weight).T),
        "wfg": by_partition(hidden_rows(arr(L0_ffn_gate_w), arr(L0_ffn_sh_gate_w)).T),
        "wfu": by_partition(hidden_rows(arr(L0_ffn_up_w), arr(L0_ffn_sh_up_w)).T),
        "wfd": by_partition(hidden_rows(arr(L0_ffn_down_w).transpose(0, 2, 1), arr(L0_ffn_sh_down_w).T)),
        "convw": np.ascontiguousarray(arr(L0_attn_conv_w).reshape(KC, P, CONV).transpose(1, 0, 2)),
        "convb": np.ascontiguousarray(arr(L0_attn_conv_b).reshape(KC, P).T),
        "mn_w": arr(L0_attn_mn_w), "mn_b": arr(L0_attn_mn_b), "gn_w": arr(L0_attn_gn_w), "gn_b": arr(L0_attn_gn_b),
        "ident": eye, "center": eye - same_head / HD, "kmask": kmask.reshape(P, -1),
        "maxsel": maxsel.reshape(NB * KVH, -1), "wsel": wsel.reshape(2 * EXPERTS, -1),
        "tri": np.ascontiguousarray(np.broadcast_to(tri, (P, tri.size))),
    }
    nc = bacc.Bacc("TRN2", target_bir_lowering=False, num_devices=1)
    arrays, a = {}, {}
    for name, v in ins.items():
        arrays[f"in_{name}"] = np.ascontiguousarray(v)
        a[name] = nc.dram_tensor(f"in_{name}", v.shape, mybir.dt.from_np(v.dtype), kind="ExternalInput").ap()
    a["y"] = nc.dram_tensor("out_y", ins["x"].shape, F32, kind="ExternalOutput").ap()
    build(nc, a)
    r = run_bass_kernel_spmd(nc, [arrays], core_ids=[0])
    return r.results[0]["out_y"].reshape(arr(x).shape)
```

```python
from contextlib import ExitStack

import concourse.bass as bass
from concourse import mybir
from concourse.alu_op_type import AluOpType as ALU

F32 = mybir.dt.float32
F16 = mybir.dt.float16
I32 = mybir.dt.int32
ACT = mybir.ActivationFunctionType
AX_X = mybir.AxisListType.X

P = 128
SEQ, DM, CTX = 64, 256, 64
KC = DM // P
TOK = 256
TT = TOK // P
NB = TOK // SEQ
HEADS, HD = 16, 16
KVH, G, HQ = 8, 4, 8
NPAIR = KVH // 2
EXPERTS, FEXP, FSHARED = 8, 176, 352
FT = 14
FTR = EXPERTS * FEXP // P
FTS = FT - FTR
FPAD = FT * P
assert FTR * P == EXPERTS * FEXP and FTS * P >= FSHARED
CONV = 4
EPS = 1e-5

SX = 16.0
SW = 64.0
S_PROJ = SX * SW
SS = 2.0 * SX
SG = SS * SW
SM = 2.0 * S_PROJ
SN = 8.0
SK = 16.0
S_MAX = 64.0
SH = 4.0
MAGIC = 1597463007.0
START = 64


class Signal:

    def __init__(self, sem, per):
        self.sem, self.per = sem, per

    def at(self, block, k):
        return block * self.per + (k + START)


def build(nc, a):
    ctx = ExitStack()
    with ctx:
        def sb(name, shape, dt=F32):
            return ctx.enter_context(nc.sbuf_tensor(name, shape, dt))

        def bank(name):
            return ctx.enter_context(nc.psum_tensor(name, [P, 512], F32))

        signals = []

        def signal(name, per=1):
            s = Signal(ctx.enter_context(nc.semaphore(name)), per)
            signals.append(s)
            return s

        bank_a = [bank("bank_a0"), bank("bank_a1")]
        bank_b = [bank("bank_b0"), bank("bank_b1")]
        bank_v = bank("bank_v")
        bank_gu = [bank("bank_gu0"), bank("bank_gu1")]
        bank_dn = bank("bank_dn")

        wqkv = [sb(f"wqkv_{p}", [P, KC, 768], F16) for p in "hl"]
        wgate = [sb(f"wgate_{p}", [P, KC, 528], F16) for p in "hl"]
        wo = [sb(f"wo_{p}", [P, KC, DM], F16) for p in "hl"]
        wrt = [sb(f"wrt_{p}", [P, KC, EXPERTS], F16) for p in "hl"]
        wfg = [sb(f"wfg_{p}", [P, KC, FPAD], F16) for p in "hl"]
        wfu = [sb(f"wfu_{p}", [P, KC, FPAD], F16) for p in "hl"]
        wfd = [sb(f"wfd_{p}", [P, FT, DM], F16) for p in "hl"]
        bias2 = sb("bias2", [33, 528], F16)
        ones2 = sb("ones2", [33, P], F16)
        stage = [sb(f"stage{n}", [P, FPAD]) for n in range(2)]
        bias_f = sb("bias_f", [33, 528])
        convw = sb("convw", [P, KC, CONV])
        convb = sb("convb", [P, KC])
        convb16 = sb("convb16", [P, KC])
        rows = sb("rows", [P, 4, DM])
        ident = sb("ident", [P, P])
        ident16 = sb("ident16", [P, P], F16)
        center = sb("center", [P, P])
        kmask = sb("kmask", [P, KVH, SEQ], F16)
        wsel = sb("wsel", [2 * EXPERTS, FTR, P], F16)
        tri = sb("tri", [P, 80])
        tri4 = tri[:, 0:16].rearrange("p (a b) -> p a b", b=4)
        tri8 = tri[:, 16:80].rearrange("p (a b) -> p a b", b=8)
        power = sb("power", [P, TT])

        x_in = sb("x_in", [P, TT, DM])
        x_res = sb("x_res", [P, TT, DM])
        st1 = sb("st1", [P, TT, 6]); mv1 = sb("mv1", [P, TT, 2]); ve1 = sb("ve1", [P, TT]); rs1 = sb("rs1", [P, TT])
        xn = sb("xn", [P, TT, DM])
        xt_h = sb("xt_h", [P, KC, TOK], F16); xt_l = sb("xt_l", [P, KC, TOK], F16)
        cacc = sb("cacc", [P, KC, NB, SEQ])
        cth = sb("cth", [P, KC, TOK]); csil = sb("csil", [P, KC, TOK])
        ct_h = sb("ct_h", [P, KC, TOK], F16); ct_l = sb("ct_l", [P, KC, TOK], F16)
        qk = sb("qk", [P, TT, 512]); qk_sq = sb("qk_sq", [P, TT, 512])
        gate_t = sb("gate_t", [P, TT, 512])
        gam = sb("gam", [P, TT, DM])
        bv = sb("bv", [P, TT, DM]); bkn = sb("bkn", [P, TT, DM]); qn = sb("qn", [P, TT, DM])
        ss_qk = sb("ss_qk", [P, TT, 32]); r_qk = sb("r_qk", [P, TT, 32]); t_qk = sb("t_qk", [P, TT, 32])
        at = sb("at", [P, TT, KC, 2, SEQ])
        memt = sb("memt", [P, TT, KC, P])
        msq = qk_sq[:, 0, :].rearrange("p (t d) -> p t d", t=TT); ss_m = sb("ss_m", [P, TT, HEADS]); v_m = sb("v_m", [P, TT, HEADS])
        r_m = sb("r_m", [P, TT, HEADS]); t_m = sb("t_m", [P, TT, HEADS])
        m1 = sb("m1", [P, TT, DM]); o1 = sb("o1", [P, TT, DM])
        sum_o = sb("sum_o", [P, TT, HEADS]); oc = sb("oc", [P, TT, DM]); osq = qk_sq[:, 1, :].rearrange("p (t d) -> p t d", t=TT)
        ss_o = sb("ss_o", [P, TT, HEADS]); v_o = sb("v_o", [P, TT, HEADS])
        r_o = sb("r_o", [P, TT, HEADS]); t_o = sb("t_o", [P, TT, HEADS])
        o2 = sb("o2", [P, TT, DM]);  o5 = sb("o5", [P, TT, DM])
        ot_h = sb("ot_h", [P, KC, TOK], F16); ot_l = sb("ot_l", [P, KC, TOK], F16)
        x1 = sb("x1", [P, TT, DM])
        ctxs = sb("ctxs", [P, NB, CTX])
        k2 = sb("k2", [SEQ, NB, 3 * CTX], F16)
        kt = sb("kt", [P, NB, SEQ], F16); ktl = sb("ktl", [CTX, NB, SEQ], F16)
        kb = sb("kb", [P, NB, KVH, SEQ], F16)
        kl = sb("kl", [CTX + NB * KVH, NB, KVH, SEQ], F16)
        vblk = sb("vblk", [P, NB, NPAIR, 32])
        st2 = sb("st2", [P, TT, 6]); mv2 = sb("mv2", [P, TT, 2]); ve2 = sb("ve2", [P, TT]); rs2 = sb("rs2", [P, TT])
        xq = sb("xq", [P, TT, DM])
        qs = sb("qs", [P, NB, G, SEQ], F16)
        qm = sb("qm", [CTX + NB * KVH, NB, G, SEQ], F16)
        mx = sb("mx", [P, 2, NB, KVH])
        prob = [sb(f"prob{n}", [P, 512]) for n in range(4)]
        avs = sb("avs", [P, TT, G, 2, SEQ])
        orec = sb("orec", [P, TT, G, NPAIR, 2])
        oatt = sb("oatt", [P, TT, DM])
        x2 = sb("x2", [P, TT, DM])
        x3 = sb("x3", [P, TT, DM])
        st3 = sb("st3", [P, TT, 6]); mv3 = sb("mv3", [P, TT, 2]); ve3 = sb("ve3", [P, TT]); rs3 = sb("rs3", [P, TT])
        hn = sb("hn", [P, TT, DM])
        ht_h = sb("ht_h", [P, KC, TOK], F16); ht_l = sb("ht_l", [P, KC, TOK], F16)
        lmax = sb("lmax", [P, TT]); lneg = sb("lneg", [P, TT]); lexp = sb("lexp", [P, TT, EXPERTS])
        lsum = sb("lsum", [P, TT]); lrec = sb("lrec", [P, TT]); prb = sb("prb", [P, TT, EXPERTS])
        gs = sb("gs", [P, TT, 4]); ggt = sb("ggt", [P, TT, 4, 4]); geq = sb("geq", [P, TT, 4, 4])
        gcnt = sb("gcnt", [P, TT, 4, 4]); grank = sb("grank", [P, TT * 4])
        pm = sb("pm", [P, TT, EXPERTS])
        egt = sb("egt", [P, TT, 8, 8]); eeq = sb("eeq", [P, TT, 8, 8])
        ecnt = sb("ecnt", [P, TT, 8, 8]); erank = sb("erank", [P, TT * 8]); wts = sb("wts", [P, TT, EXPERTS])
        whl = sb("whl", [P, TT, 16], F16)
        wt = sb("wt", [16, TOK], F16)
        wx = sb("wx", [P, FTR, TOK])
        ff_tanh = [sb(f"ff_tanh{n}", [P, TOK]) for n in range(2)]
        ff_g = [sb(f"ff_g{n}", [P, TOK]) for n in range(2)]
        ff_u = [sb(f"ff_u{n}", [P, TOK]) for n in range(2)]
        ff_w = [sb(f"ff_w{n}", [P, TOK]) for n in range(2)]
        hid_h = [sb(f"hid_h{n}", [P, TOK], F16) for n in range(2)]
        hid_l = [sb(f"hid_l{n}", [P, TOK], F16) for n in range(2)]
        y_sb = sb("y_sb", [P, TT, DM])

        def plain(name):
            return ctx.enter_context(nc.semaphore(name))

        cst_loaded = plain("cst_loaded")
        stage_loaded = [plain(f"stage_loaded{n}") for n in range(2)]
        stage_split = plain("stage_split")
        stage_high = plain("stage_high")
        cst_act = plain("cst_act")
        cst_dve = plain("cst_dve")
        cst_pool = plain("cst_pool")
        primed = plain("primed")
        held = plain("held")

        x_loaded = signal("x_loaded", 16)
        x_kept = signal("x_kept")
        ln1_stat = signal("ln1_stat", 5)
        ln1_rstd = signal("ln1_rstd")
        xn_ready = signal("xn_ready", TT)
        xt_ps = signal("xt_ps")
        xt_high = signal("xt_high")
        xt_low = signal("xt_low")
        conv_first = signal("conv_first", KC)
        conv_taps = signal("conv_taps", KC * (CONV - 1))
        conv_tanh = signal("conv_tanh")
        conv_silu = signal("conv_silu")
        ct_high = signal("ct_high")
        ct_low = signal("ct_low")
        qk_ps = signal("qk_ps", TT)
        vg_ps = signal("vg_ps", TT)
        gate_ps = signal("gate_ps", TT)
        qk_kept = signal("qk_kept", TT)
        qk_square = signal("qk_square", TT)
        gate_tanh = signal("gate_tanh", TT)
        gam_tanh = signal("gam_tanh", TT)
        v_gated = signal("v_gated", TT)
        qk_sums = signal("qk_sums", TT)
        qk_norm = signal("qk_norm", 12)
        bk_ready = signal("bk_ready")
        bkn_ready = signal("bkn_ready")
        qn_ready = signal("qn_ready")
        bg_ps = signal("bg_ps", TT)
        decay_ready = signal("decay_ready", TT)
        mem_ready = signal("mem_ready", TT * KC)
        ctr_ps = signal("ctr_ps")
        mem_square = signal("mem_square")
        mem_norm = signal("mem_norm", 13)
        m1_ready = signal("m1_ready")
        m2_ready = signal("m2_ready")
        m3_ready = signal("m3_ready")
        o1_ready = signal("o1_ready")
        out_center = signal("out_center", 2)
        out_square = signal("out_square")
        out_norm = signal("out_norm", 13)
        o2_ready = signal("o2_ready")
        o3_ready = signal("o3_ready")
        o4_ready = signal("o4_ready")
        o5_ready = signal("o5_ready")
        ot_ps = signal("ot_ps")
        ot_high = signal("ot_high")
        ot_low = signal("ot_low")
        mix_ps = signal("mix_ps")
        x1_ready = signal("x1_ready")
        ctx_loaded = signal("ctx_loaded", 32)
        k_high = signal("k_high")
        k_low = signal("k_low")
        v_block = signal("v_block", 2)
        kt_ps = signal("kt_ps")
        kt_kept = signal("kt_kept", 2)
        k_masked = signal("k_masked", 2)
        ln2_stat = signal("ln2_stat", 5)
        ln2_rstd = signal("ln2_rstd")
        xq_ready = signal("xq_ready", TT)
        qt_ps = signal("qt_ps", TT)
        q_high = signal("q_high", TT)
        q_low = signal("q_low", TT)
        q_again = signal("q_again")
        row_ps = signal("row_ps", 2 * NB)
        row_max = signal("row_max", 2 * NB)
        maxt_ps = signal("maxt_ps")
        maxt_kept = signal("maxt_kept")
        col_ps = signal("col_ps", 2 * NB)
        col_exp = signal("col_exp", 2 * NB)
        val_ps = signal("val_ps", NB)
        val_kept = signal("val_kept", NB)
        att_ps = signal("att_ps", TT)
        att_norm = signal("att_norm", 3 * TT)
        x2_ready = signal("x2_ready", TT)
        ln3_stat = signal("ln3_stat", 5)
        ln3_rstd = signal("ln3_rstd")
        hn_ready = signal("hn_ready", TT)
        x2_kept = signal("x2_kept")
        ht_ps = signal("ht_ps")
        ht_high = signal("ht_high")
        ht_low = signal("ht_low")
        logit_ps = signal("logit_ps")
        logit_exp = signal("logit_exp", TT)
        route = signal("route", 20)
        wt_ps = signal("wt_ps")
        wt_kept = signal("wt_kept")
        wx_ps = signal("wx_ps", 6)
        wx_kept = signal("wx_kept", 6)
        gu_ps = signal("gu_ps", FT)
        tanh_done = signal("tanh_done", FT)
        silu_done = signal("silu_done", FT)
        up_done = signal("up_done", FT)
        weighted = signal("weighted", FTR)
        hid_high = signal("hid_high", FT)
        hid_low = signal("hid_low", FT)
        down_ps = signal("down_ps", FT)
        y_based = signal("y_based")
        y_ready = signal("y_ready")
        y_stored = signal("y_stored", 16)

        def flat(t, lo=0, hi=None):
            return t[:, lo:hi, :].rearrange("p a b -> p (a b)")

        loads = [(a["wqkv"], flat(wqkv[0]), flat(wqkv[1]), SW), (a["wgate"], flat(wgate[0]), flat(wgate[1]), SW),
                 (a["wo"], flat(wo[0]), flat(wo[1]), SW), (a["kmask"], flat(kmask), None, 1.0)]
        loads += [(a["maxsel"][:, 1024 * n:1024 * n + 1024],
                   kl[CTX:, 2 * n:2 * n + 2, :, :].rearrange("p b h s -> p (b h s)"), None, S_MAX) for n in range(2)]
        loads += [(a["wrt"], flat(wrt[0]), flat(wrt[1]), SW), (a["wsel"], flat(wsel), None, 1.0)]
        loads += [(a[name][:, c * FPAD:(c + 1) * FPAD], flat(w[0], c, c + 1), flat(w[1], c, c + 1), SW)
                  for name, w in (("wfg", wfg), ("wfu", wfu)) for c in range(KC)]
        loads += [(a["wfd"][:, c * FPAD:(c + 1) * FPAD], flat(wfd[0], 7 * c, 7 * c + 7), flat(wfd[1], 7 * c, 7 * c + 7), SW)
                  for c in range(2)]

        WQKV, WGATE, WO, KMASK, MAXSEL, WRT, WSEL, WFU, WFD = 0, 1, 2, 3, 5, 6, 7, 11, 13

        def splits_before(n):
            return sum(low is not None for _, _, low, _ in loads[:n])

        consts = [
            (ident[:, :], a["ident"]), (center[:, :], a["center"]), (tri[:, :], a["tri"]),
            (convw[:, :, :], a["convw"]), (convb[:, :], a["convb"]),
            (bias_f[:, :], a["bias"]),
        ] + [(rows[:, n, :], a[name].partition_broadcast(P)) for n, name in enumerate(("mn_w", "mn_b", "gn_w", "gn_b"))]

        x_blocks = a["x"].rearrange("(n t p) d -> n p t d", p=P, t=TT)
        y_blocks = a["y"].rearrange("(n t p) d -> n p t d", p=P, t=TT)
        c_blocks = a["ctx"].rearrange("(n b) t d -> n t b d", b=NB)
        BLOCKS = x_blocks.shape[0]
        LAGS = 8
        ROUTER_BEHIND = 2

        block = ctx.enter_context(nc.Block())

        def turned_queries(t, odd):
            return bank_b[t][64 * odd:64 * odd + 64, 0:2 * P].rearrange("p (g b s) -> p g b s", g=2, b=2)

        def query_heads(q, base, t, odd):
            return q[base:base + 64, 2 * t:2 * t + 2, odd:odd + 3:2, :].rearrange("p b g s -> p g b s")

        def blocks(j):
            return [j - n if not isinstance(j, int) or 0 <= j - n < BLOCKS else None for n in range(LAGS + 1)]

        def on(i, step, *args):
            if i is not None:
                step(i, *args)

        def once(i, step, n):
            if isinstance(i, int) and i == 0:
                step(i, n)

        def need(engine, i, n):
            if isinstance(i, int) and i == 0:
                engine.wait_ge(stage_high, n + 1)
                engine.wait_ge(stage_split, splits_before(n + 1))

        @block.sync
        def _(sp):
            def load_x(i):
                sp.wait_ge(xn_ready.sem, xn_ready.at(i, 0))
                sp.sem_inc(held, 1)
                sp.wait_ge(x_kept.sem, x_kept.at(i, 0))
                sp.sem_inc(held, 1)
                sp.dma_start(x_in[:, :, :], x_blocks[i]).then_inc(x_loaded.sem, 16)

            def load_next_x(i):
                if not isinstance(i, int) or i + 1 < BLOCKS:
                    load_x(i + 1)

            def load_ctx(i):
                sp.wait_ge(k_low.sem, k_low.at(i, 0))
                sp.sem_inc(held, 1)
                sp.wait_ge(v_block.sem, v_block.at(i, 0))
                sp.sem_inc(held, 1)
                sp.wait_ge(k_high.sem, k_high.at(i, 0))
                sp.sem_inc(held, 1)
                for half in range(2):
                    sp.dma_start(ctxs[64 * half:64 * half + 64, :, :], c_blocks[i]).then_inc(ctx_loaded.sem, 16)

            def store_y(i):
                sp.wait_ge(y_ready.sem, y_ready.at(i, 1))
                sp.sem_inc(held, 1)
                sp.dma_start(y_blocks[i], y_sb[:, :, :]).then_inc(y_stored.sem, 16)

            sp.wait_ge(primed, 1)
            load_x(0)
            for dst, src in consts:
                sp.dma_start(dst, src).then_inc(cst_loaded, 16)

            def load_weight(i, n):
                src = loads[n][0]
                if n >= 2:
                    sp.wait_ge(stage_high, n - 1)
                    if splits_before(n - 1):
                        sp.wait_ge(stage_split, splits_before(n - 1))
                sp.dma_start(stage[n % 2][0:src.shape[0], 0:src.shape[1]], src).then_inc(stage_loaded[n % 2], 16)

            def turn(j):
                b = blocks(j)
                once(b[5], load_weight, 6)
                on(b[5], load_next_x)
                for n in range(7, 13):
                    once(b[5], load_weight, n)
                once(b[4], load_weight, 0)
                once(b[5], load_weight, 13)
                once(b[4], load_weight, 1)
                on(b[4], load_ctx)
                on(b[8], store_y)
                for n in range(2, 6):
                    once(b[4], load_weight, n)

            for j in range(LAGS):
                turn(j)
            with sp.Fori(LAGS, BLOCKS - 1) as j:
                turn(j)
            for j in range(BLOCKS - 1, BLOCKS + LAGS):
                turn(j)
            sp.wait_ge(y_stored.sem, y_stored.at(BLOCKS, 0))

        @block.gpsimd
        def _(pool):
            for s in signals:
                pool.sem_inc(s.sem, START)
            pool.sem_inc(primed, 1)
            pool.memset(power[:, :], -0.5).then_inc(cst_pool, 1)
            pool.memset(at[:, :, :, :, :], 0.0).then_inc(cst_pool, 1)
            pool.memset(vblk[:, :, :, :], 0.0).then_inc(cst_pool, 1)
            pool.memset(ones2[:, :], 0.0).then_inc(cst_pool, 1)
            pool.wait_ge(cst_pool, 4)
            pool.memset(vblk[0:64, :, :, 16:17], 1.0).then_inc(cst_pool, 1)
            pool.memset(vblk[64:128, :, :, 17:18], 1.0).then_inc(cst_pool, 1)
            pool.wait_ge(cst_pool, 6)
            pool.memset(ones2[0:1, :], SS).then_inc(cst_pool, 1)
            pool.memset(ones2[32:33, :], SS).then_inc(cst_pool, 1)

            def rstd(i, stat, done, ve, rs, free):
                pool.wait_ge(free.sem, free.at(i, 0))
                pool.wait_ge(stat.sem, stat.at(i, 5))
                pool.tensor_tensor(rs[:, :], ve[:, :], power[:, :], ALU.pow).then_inc(done.sem, 1)

            def norm1_rstd(i):
                rstd(i, ln1_stat, ln1_rstd, ve1, rs1, xn_ready)

            def norm2_rstd(i):
                rstd(i, ln2_stat, ln2_rstd, ve2, rs2, xq_ready)

            def norm3_rstd(i):
                rstd(i, ln3_stat, ln3_rstd, ve3, rs3, hn_ready)

            def silu_low(i):
                pool.wait_ge(ct_high.sem, ct_high.at(i, 1))
                pool.wait_ge(conv_silu.sem, conv_silu.at(i, 1))
                pool.wait_ge(gate_ps.sem, gate_ps.at(i, 0))
                pool.tensor_tensor(ct_l[:, :, :], csil[:, :, :], ct_h[:, :, :], ALU.subtract).then_inc(ct_low.sem, 1)

            def keys_times_values(i):
                pool.wait_ge(v_gated.sem, v_gated.at(i, TT))
                pool.wait_ge(qk_kept.sem, qk_kept.at(i, TT))
                pool.tensor_tensor(bv[:, :, :], bv[:, :, :], qk[:, :, DM:2 * DM], ALU.mult).then_inc(bk_ready.sem, 1)

            def head_bcast(r, lo=0):
                return r[:, :, lo:lo + HEADS].unsqueeze(3).broadcast_to([P, TT, HEADS, HD])

            def by_head(t):
                return t.rearrange("p t (h d) -> p t h d", d=HD)

            def keys_normed(i):
                pool.wait_ge(qk_norm.sem, qk_norm.at(i, 12))
                pool.wait_ge(bk_ready.sem, bk_ready.at(i, 1))
                pool.wait_ge(bg_ps.sem, bg_ps.at(i, 0))
                pool.tensor_tensor(by_head(bkn[:, :, :]), by_head(bv[:, :, :]), head_bcast(r_qk, HEADS),
                                   ALU.mult).then_inc(bkn_ready.sem, 1)

            def queries_normed(i):
                pool.wait_ge(qk_norm.sem, qk_norm.at(i, 12))
                pool.wait_ge(qk_kept.sem, qk_kept.at(i, TT))
                pool.wait_ge(o1_ready.sem, o1_ready.at(i, 0))
                pool.tensor_tensor(by_head(qn[:, :, :]), by_head(qk[:, :, 0:DM]), head_bcast(r_qk, 0),
                                   ALU.mult).then_inc(qn_ready.sem, 1)

            def row(t, n):
                return t[:, n:n + 1, :].broadcast_to([P, TT, DM])

            def mem_weight(i):
                pool.wait_ge(m1_ready.sem, m1_ready.at(i, 1))
                pool.tensor_tensor(m1[:, :, :], m1[:, :, :], row(rows, 0), ALU.mult).then_inc(m2_ready.sem, 1)

            def mem_bias(i):
                pool.wait_ge(m2_ready.sem, m2_ready.at(i, 1))
                pool.tensor_tensor(m1[:, :, :], m1[:, :, :], row(rows, 1), ALU.add).then_inc(m3_ready.sem, 1)

            def mem_times_queries(i):
                pool.wait_ge(m3_ready.sem, m3_ready.at(i, 1))
                pool.wait_ge(qn_ready.sem, qn_ready.at(i, 1))
                pool.wait_ge(out_center.sem, out_center.at(i, 0))
                pool.tensor_tensor(o1[:, :, :], m1[:, :, :], qn[:, :, :], ALU.mult).then_inc(o1_ready.sem, 1)

            def out_weight(i):
                pool.wait_ge(o2_ready.sem, o2_ready.at(i, 1))
                pool.tensor_tensor(o2[:, :, :], o2[:, :, :], row(rows, 2), ALU.mult).then_inc(o3_ready.sem, 1)

            def out_bias(i):
                pool.wait_ge(o3_ready.sem, o3_ready.at(i, 1))
                pool.tensor_tensor(o2[:, :, :], o2[:, :, :], row(rows, 3), ALU.add).then_inc(o4_ready.sem, 1)

            def attention_residual(i, t):
                pool.wait_ge(att_norm.sem, att_norm.at(i, 3 * t + 3))
                pool.wait_ge(hn_ready.sem, hn_ready.at(i, 0))
                pool.wait_ge(x2_kept.sem, x2_kept.at(i, 0))
                pool.wait_ge(x1_ready.sem, x1_ready.at(i, 1))
                pool.tensor_tensor(x2[:, t, :], oatt[:, t, :], x1[:, t, :], ALU.add).then_inc(x2_ready.sem, 1)

            def weigh(i, k):
                pool.wait_ge(up_done.sem, up_done.at(i, k + 1))
                pool.wait_ge(wx_kept.sem, wx_kept.at(i, (k - FTS) // 2 + 1))
                b, n = (i, k - 1) if k >= FTS + 2 else (i - 1, FT - (k - FTS))
                pool.wait_ge(hid_high.sem, hid_high.at(b, n))
                pool.wait_ge(hid_low.sem, hid_low.at(b, n))
                pool.tensor_tensor(ff_w[k % 2][:, :], ff_u[k % 2][:, :], wx[:, k - FTS, :], ALU.mult).then_inc(weighted.sem, 1)

            def hidden_low(i, k):
                src = ff_u if k < FTS else ff_w
                pool.wait_ge(hid_high.sem, hid_high.at(i, k + 1))
                if k >= FTS:
                    pool.wait_ge(weighted.sem, weighted.at(i, k - FTS + 1))
                pool.wait_ge(down_ps.sem, down_ps.at(i, k - 1))
                pool.tensor_tensor(hid_l[k % 2][:, :], src[k % 2][:, :], hid_h[k % 2][:, :],
                                   ALU.subtract).then_inc(hid_low.sem, 1)

            def turn(j):
                b = blocks(j)
                on(b[7], hidden_low, 11)
                on(b[4], mem_weight)
                on(b[4], mem_bias)
                on(b[4], mem_times_queries)
                on(b[7], weigh, 12)
                on(b[7], weigh, 13)
                on(b[3], norm1_rstd)
                on(b[7], hidden_low, 12)
                on(b[7], hidden_low, 13)
                on(b[6], hidden_low, 0)
                on(b[4], out_weight)
                on(b[4], out_bias)
                on(b[6], hidden_low, 1)
                on(b[5], attention_residual, 0)
                on(b[6], hidden_low, 2)
                on(b[6], weigh, 3)
                on(b[5], attention_residual, 1)
                on(b[6], weigh, 4)
                on(b[6], hidden_low, 3)
                on(b[5], norm3_rstd)
                on(b[6], hidden_low, 4)
                on(b[6], weigh, 5)
                on(b[3], silu_low)
                on(b[4], norm2_rstd)
                on(b[6], hidden_low, 5)
                on(b[6], weigh, 6)
                on(b[6], weigh, 7)
                on(b[6], hidden_low, 6)
                on(b[6], weigh, 8)
                on(b[3], keys_times_values)
                on(b[3], keys_normed)
                on(b[6], hidden_low, 7)
                on(b[6], hidden_low, 8)
                on(b[6], weigh, 9)
                on(b[6], hidden_low, 9)
                on(b[6], weigh, 10)
                on(b[3], queries_normed)
                on(b[6], weigh, 11)
                on(b[6], hidden_low, 10)

            pool.wait_ge(cst_dve, 2)
            pool.wait_ge(cst_pool, 8)
            for j in range(LAGS):
                turn(j)
            with pool.Fori(LAGS, BLOCKS) as j:
                turn(j)
            for j in range(BLOCKS, BLOCKS + LAGS):
                turn(j)

        @block.scalar
        def _(act):
            act.wait_ge(cst_loaded, 16 * len(consts))
            act.activation(ident16[:, :], ident[:, :], ACT.Copy).then_inc(cst_act, 1)
            act.activation(convb16[:, :], convb[:, :], ACT.Copy, scale=SX).then_inc(cst_act, 1)
            act.activation(bias2[:, :], bias_f[:, :], ACT.Copy, scale=SW).then_inc(cst_act, 1)

            def weight_high(i, n):
                src, high, _, scale = loads[n]
                act.wait_ge(stage_loaded[n % 2], 16 * (n // 2 + 1))
                act.activation(high, stage[n % 2][0:src.shape[0], 0:src.shape[1]], ACT.Copy,
                               scale=scale).then_inc(stage_high, 1)

            def keep_x(i):
                act.wait_ge(x_loaded.sem, x_loaded.at(i, 16))
                act.wait_ge(x1_ready.sem, x1_ready.at(i, 0))
                act.activation(x_res[:, :, :], x_in[:, :, :], ACT.Copy).then_inc(x_kept.sem, 1)

            def x_transposed(i):
                act.wait_ge(xt_ps.sem, xt_ps.at(i, 1))
                act.wait_ge(vg_ps.sem, vg_ps.at(i, 0))
                psum = bank_a[0][:, :].rearrange("p (c t) -> p c t", c=KC)
                act.activation(xt_h[:, :, :], psum, ACT.Copy).then_inc(xt_high.sem, 1)

            def conv_start(i):
                act.wait_ge(xt_ps.sem, xt_ps.at(i, 1))
                act.wait_ge(conv_silu.sem, conv_silu.at(i, 0))
                psum = bank_a[0][:, :].rearrange("p (c t) -> p c t", c=KC)
                for c in range(KC):
                    act.activation(cacc[:, c, :, :].rearrange("p b s -> p (b s)"), psum[:, c, :], ACT.Identity,
                                   scale=convw[:, c, CONV - 1:CONV], bias=convb16[:, c:c + 1]).then_inc(conv_first.sem, 1)

            def conv_activation(i):
                act.wait_ge(conv_taps.sem, conv_taps.at(i, KC * (CONV - 1)))
                act.wait_ge(conv_silu.sem, conv_silu.at(i, 0))
                act.activation(cth[:, :, :], cacc[:, :, :, :].rearrange("p c b s -> p c (b s)"), ACT.Tanh,
                               scale=0.5 / SX).then_inc(conv_tanh.sem, 1)

            def silu_high(i):
                act.wait_ge(conv_silu.sem, conv_silu.at(i, 1))
                act.wait_ge(gate_ps.sem, gate_ps.at(i, 0))
                act.activation(ct_h[:, :, :], csil[:, :, :], ACT.Copy).then_inc(ct_high.sem, 1)

            def qk_out(i, t):
                b = bank_a[(t + 1) % 2]
                act.wait_ge(qk_ps.sem, qk_ps.at(i, t + 1))
                act.wait_ge(qn_ready.sem, qn_ready.at(i, 0))
                act.activation(qk[:, t, :], b[:, :], ACT.Copy).then_inc(qk_kept.sem, 1)
                prior = out_norm if t else mem_norm
                act.wait_ge(prior.sem, prior.at(i, 0))
                act.activation(qk_sq[:, t, :], b[:, :], ACT.Square).then_inc(qk_square.sem, 1)

            def gamma_out(i, t):
                b = bank_a[t % 2]
                act.wait_ge(vg_ps.sem, vg_ps.at(i, t + 1))
                act.wait_ge(bg_ps.sem, bg_ps.at(i, 0))
                src = b[:, DM:DM + HEADS].unsqueeze(2).broadcast_to([P, HEADS, HD])
                act.activation(gam[:, t, :].rearrange("p (h d) -> p h d", d=HD), src, ACT.Tanh,
                               scale=0.5 / SG).then_inc(gam_tanh.sem, 1)

            def gates_out(i, t):
                b = bank_a[(t + 1) % 2]
                act.wait_ge(gate_ps.sem, gate_ps.at(i, t + 1))
                act.wait_ge(o5_ready.sem, o5_ready.at(i, 0))
                act.activation(gate_t[:, t, :], b[:, :], ACT.Tanh, scale=0.5 / SG).then_inc(gate_tanh.sem, 1)

            def decay(i, t):
                b = bank_a[(t + 1) % 2][:, DM:2 * DM].rearrange("p (c b s) -> p c b s", c=KC, b=2)
                act.wait_ge(bg_ps.sem, bg_ps.at(i, t + 1))
                act.wait_ge(mem_ready.sem, mem_ready.at(i, KC * (t + 1) - TT * KC))
                for c in range(KC):
                    ins = act.activation(at[:, t, c, :, 1:SEQ], b[:, c, :, 1:SEQ], ACT.Copy, scale=0.5, bias=0.5)
                ins.then_inc(decay_ready.sem, 1)

            def mem_squares(i):
                act.wait_ge(ctr_ps.sem, ctr_ps.at(i, 1))
                act.wait_ge(mem_norm.sem, mem_norm.at(i, 0))
                act.activation(msq[:, :, :], bank_a[1][:, :].rearrange("p (t d) -> p t d", t=TT),
                               ACT.Square).then_inc(mem_square.sem, 1)

            def out_squares(i):
                act.wait_ge(out_center.sem, out_center.at(i, 2))
                act.wait_ge(out_norm.sem, out_norm.at(i, 0))
                act.activation(osq[:, :, :], oc[:, :, :], ACT.Square).then_inc(out_square.sem, 1)

            def out_transposed(i):
                act.wait_ge(ot_ps.sem, ot_ps.at(i, 1))
                act.wait_ge(mix_ps.sem, mix_ps.at(i, 0))
                act.activation(ot_h[:, :, :], bank_a[0][:, :].rearrange("p (c t) -> p c t", c=KC),
                               ACT.Copy).then_inc(ot_high.sem, 1)

            def keys_values(i):
                act.wait_ge(ctx_loaded.sem, ctx_loaded.at(i, 32))
                act.wait_ge(kt_ps.sem, kt_ps.at(i, 0))
                act.activation(k2[:, :, 0:2 * CTX].rearrange("p b (r d) -> p b r d", r=2),
                               ctxs[0:SEQ, :, :].unsqueeze(2).broadcast_to([SEQ, NB, 2, CTX]),
                               ACT.Copy, scale=SK).then_inc(k_high.sem, 1)
                act.wait_ge(val_ps.sem, val_ps.at(i, 0))
                for half in range(2):
                    src = ctxs[64 * half:64 * half + 64, :, :].rearrange("p b (j h d) -> p b j h d", j=NPAIR, h=2)
                    act.activation(vblk[64 * half:64 * half + 64, :, :, 8 * half:8 * half + 8],
                                   src[:, :, :, half, :], ACT.Copy).then_inc(v_block.sem, 1)

            def keys_transposed(i):
                act.wait_ge(kt_ps.sem, kt_ps.at(i, 1))
                act.wait_ge(k_masked.sem, k_masked.at(i, 0))
                psum = bank_v[:, 0:256].bitcast(F16)
                act.activation(kt[:, :, :].rearrange("p b s -> p (b s)"), psum[:, 0:256], ACT.Copy).then_inc(kt_kept.sem, 1)
                act.activation(ktl[:, :, :].rearrange("p b s -> p (b s)"), psum[0:CTX, 256:512], ACT.Copy).then_inc(kt_kept.sem, 1)

            def queries_high(i, t):
                act.wait_ge(qt_ps.sem, qt_ps.at(i, t + 1))
                act.wait_ge(col_ps.sem, col_ps.at(i, 0))
                for odd in range(2):
                    ins = act.activation(query_heads(qs, 0, t, odd), turned_queries(t, odd), ACT.Copy)
                ins.then_inc(q_high.sem, 1)

            def maxima_transposed(i):
                act.wait_ge(maxt_ps.sem, maxt_ps.at(i, 1))
                act.wait_ge(col_ps.sem, col_ps.at(i, 0))
                act.activation(qm[CTX:, :, :, :].rearrange("p b g s -> p b (g s)"),
                               bank_v[0:NB * KVH, 0:256].unsqueeze(1).broadcast_to([NB * KVH, NB, 256]), ACT.Copy,
                               scale=1.0 / S_MAX).then_inc(maxt_kept.sem, 1)

            def exps(i, n):
                act.wait_ge(col_ps.sem, col_ps.at(i, n + 1))
                act.wait_ge(val_ps.sem, val_ps.at(i, n // 2 - 1))
                act.activation(prob[n % 4][:, :], bank_b[n % 2][:, :], ACT.Exp,
                               scale=1.0 / (SX * SK * HQ ** 0.5)).then_inc(col_exp.sem, 1)

            def values_out(i, b):
                act.wait_ge(val_ps.sem, val_ps.at(i, b + 1))
                act.wait_ge(att_ps.sem, att_ps.at(i, b // 2 + 1 - TT))
                act.activation(avs[:, b // 2, :, b % 2, :],
                               bank_v[:, 256 * (b % 2):256 * (b % 2) + 256].rearrange("p (g s) -> p g s", g=G),
                               ACT.Copy).then_inc(val_kept.sem, 1)

            def keep_y(i):
                act.wait_ge(x2_kept.sem, x2_kept.at(i, 1))
                act.wait_ge(y_stored.sem, y_stored.at(i, 0))
                act.activation(y_sb[:, :, :], x3[:, :, :], ACT.Copy).then_inc(y_based.sem, 1)

            def keep_x2(i):
                act.wait_ge(x2_ready.sem, x2_ready.at(i, TT))
                act.wait_ge(y_based.sem, y_based.at(i, 0))
                act.activation(x3[:, :, :], x2[:, :, :], ACT.Copy).then_inc(x2_kept.sem, 1)

            def h_transposed(i):
                act.wait_ge(ht_ps.sem, ht_ps.at(i, 1))
                act.wait_ge(gu_ps.sem, gu_ps.at(i, 0))
                act.wait_ge(logit_ps.sem, logit_ps.at(i, 0))
                act.activation(ht_h[:, :, :], bank_a[0][:, :].rearrange("p (c t) -> p c t", c=KC),
                               ACT.Copy).then_inc(ht_high.sem, 1)

            def router_exp(i):
                act.wait_ge(route.sem, route.at(i, 2))
                for t in range(TT):
                    act.activation(lexp[:, t, :], bank_a[1][:, EXPERTS * t:EXPERTS * (t + 1)], ACT.Exp,
                                   scale=1.0 / S_PROJ, bias=lneg[:, t:t + 1]).then_inc(logit_exp.sem, 1)

            def weights_transposed(i):
                act.wait_ge(wt_ps.sem, wt_ps.at(i, 1))
                act.wait_ge(wx_ps.sem, wx_ps.at(i, 0))
                act.activation(wt[:, :], bank_a[0][0:16, 0:128].bitcast(F16), ACT.Copy).then_inc(wt_kept.sem, 1)

            def weights_spread(i, n):
                act.wait_ge(wx_ps.sem, wx_ps.at(i, n + 1))
                w = min(2, FTR - 2 * n)
                act.wait_ge(weighted.sem, weighted.at(i - 1, 2 * n + w))
                act.activation(wx[:, 2 * n:2 * n + w, :].rearrange("p k t -> p (k t)"),
                               bank_a[(n + 1) % 2][:, 0:w * TOK], ACT.Copy).then_inc(wx_kept.sem, 1)

            def expert_tanh(i, k):
                act.wait_ge(gu_ps.sem, gu_ps.at(i, k + 1))
                act.wait_ge(silu_done.sem, silu_done.at(i, k - 1))
                act.activation(ff_tanh[k % 2][:, :], bank_gu[k % 2][:, 0:TOK], ACT.Tanh,
                               scale=0.5 / S_PROJ).then_inc(tanh_done.sem, 1)

            def expert_high(i, k):
                if k >= FTS:
                    act.wait_ge(weighted.sem, weighted.at(i, k - FTS + 1))
                else:
                    act.wait_ge(up_done.sem, up_done.at(i, k + 1))
                act.wait_ge(down_ps.sem, down_ps.at(i, k - 1))
                src = ff_u if k < FTS else ff_w
                act.activation(hid_h[k % 2][:, :], src[k % 2][:, :], ACT.Copy).then_inc(hid_high.sem, 1)

            def turn(j):
                b = blocks(j)
                on(b[7], exps, 6)
                on(b[8], expert_tanh, 1)
                on(b[7], values_out, 2)
                on(b[7], exps, 7)
                on(b[8], weights_transposed)
                on(b[8], expert_tanh, 2)
                on(b[8], expert_high, 0)
                once(b[6], weight_high, 10)
                on(b[7], values_out, 3)
                on(b[8], weights_spread, 0)
                on(b[8], weights_spread, 1)
                once(b[6], weight_high, 11)
                on(b[8], expert_high, 1)
                on(b[8], weights_spread, 2)
                on(b[8], weights_spread, 3)
                on(b[8], expert_tanh, 3)
                on(b[8], expert_high, 2)
                on(b[8], weights_spread, 4)
                on(b[8], weights_spread, 5)
                on(b[6], keys_values)
                on(b[8], expert_tanh, 4)
                on(b[6], out_transposed)
                on(b[8], expert_high, 3)
                once(b[6], weight_high, 12)
                on(b[8], expert_tanh, 5)
                on(b[5], x_transposed)
                on(b[5], conv_start)
                once(b[6], weight_high, 13)
                on(b[8], expert_high, 4)
                once(b[5], weight_high, 0)
                once(b[5], weight_high, 1)
                on(b[5], conv_activation)
                on(b[8], expert_tanh, 6)
                on(b[8], expert_tanh, 7)
                on(b[5], silu_high)
                on(b[8], expert_high, 5)
                on(b[5], qk_out, 0)
                on(b[5], gamma_out, 0)
                once(b[5], weight_high, 2)
                on(b[6], keys_transposed)
                on(b[5], gates_out, 0)
                on(b[5], keep_x)
                on(b[6], queries_high, 0)
                once(b[5], weight_high, 3)
                on(b[6], queries_high, 1)
                on(b[8], expert_high, 6)
                on(b[8], expert_tanh, 8)
                on(b[5], qk_out, 1)
                on(b[8], expert_tanh, 9)
                once(b[5], weight_high, 4)
                on(b[5], gamma_out, 1)
                once(b[5], weight_high, 5)
                on(b[8], expert_high, 7)
                on(b[5], gates_out, 1)
                once(b[5], weight_high, 6)
                on(b[8], expert_high, 8)
                on(b[8], expert_tanh, 10)
                on(b[8], expert_tanh, 11)
                on(b[5], decay, 0)
                on(b[5], decay, 1)
                on(b[8], keep_y)
                on(b[8], expert_high, 9)
                once(b[5], weight_high, 7)
                on(b[5], mem_squares)
                on(b[6], maxima_transposed)
                once(b[5], weight_high, 8)
                on(b[8], expert_tanh, 12)
                on(b[8], expert_high, 10)
                on(b[7], keep_x2)
                once(b[5], weight_high, 9)
                on(b[6], exps, 0)
                on(b[6], exps, 1)
                on(b[8], expert_high, 11)
                on(b[8], expert_tanh, 13)
                on(b[6], exps, 2)
                on(b[6], exps, 3)
                on(b[7], h_transposed)
                on(b[6], values_out, 0)
                on(b[7], router_exp)
                on(b[6], exps, 4)
                on(b[7], expert_tanh, 0)
                on(b[6], values_out, 1)
                on(b[6], exps, 5)
                on(b[8], expert_high, 12)
                on(b[5], out_squares)
                on(b[8], expert_high, 13)

            act.wait_ge(cst_pool, 8)
            act.wait_ge(primed, 1)
            for j in range(LAGS):
                turn(j)
            with act.Fori(LAGS, BLOCKS) as j:
                turn(j)
            for j in range(BLOCKS, BLOCKS + LAGS):
                turn(j)

        @block.tensor
        def _(pe):
            pe.wait_ge(cst_loaded, 16 * len(consts))
            pe.wait_ge(cst_act, 3)
            pe.wait_ge(cst_dve, 2)
            pe.wait_ge(cst_pool, 8)

            def product(out, lhs, rhs, first=True, last=True):
                terms = [(l, r) for lp, rp in ((0, 0), (1, 0), (0, 1)) for l, r in zip(lhs[lp], rhs[rp])]
                for n, (l, r) in enumerate(terms):
                    ins = pe.matmul(out, l, r, start=first and n == 0, stop=last and n == len(terms) - 1,
                                    skip_group_check=True)
                return ins

            def chunks(pair, cols):
                return [[t[:, c, cols] for c in range(KC)] for t in pair]

            def turned(src, b):
                for t in range(TT):
                    for c in range(KC):
                        ins = pe.transpose(b[:, c * TOK + t * P:c * TOK + (t + 1) * P],
                                           src[:, t, c * P:(c + 1) * P], ident[:, :])
                return ins

            def turn_x(i):
                pe.wait_ge(xn_ready.sem, xn_ready.at(i, TT))
                pe.wait_ge(ot_low.sem, ot_low.at(i, 0))
                pe.wait_ge(ot_high.sem, ot_high.at(i, 0))
                turned(xn, bank_a[0]).then_inc(xt_ps.sem, 1)

            def project_qk(i, t):
                toks = slice(t * P, (t + 1) * P)
                need(pe, i, WQKV)
                pe.wait_ge(xt_high.sem, xt_high.at(i, 1))
                pe.wait_ge(xt_low.sem, xt_low.at(i, 1))
                if t == 0:
                    pe.wait_ge(x1_ready.sem, x1_ready.at(i, 0))
                else:
                    pe.wait_ge(v_gated.sem, v_gated.at(i, t))
                    pe.wait_ge(gam_tanh.sem, gam_tanh.at(i, t))
                product(bank_a[(t + 1) % 2][:, 0:512], chunks((xt_h, xt_l), toks),
                        chunks(wqkv, slice(0, 512))).then_inc(qk_ps.sem, 1)

            def project_v_gamma(i, t):
                toks = slice(t * P, (t + 1) * P)
                b = bank_a[t % 2]
                if t == 0:
                    pe.wait_ge(conv_taps.sem, conv_taps.at(i, KC * (CONV - 1)))
                    pe.wait_ge(conv_first.sem, conv_first.at(i, KC))
                else:
                    pe.wait_ge(gate_tanh.sem, gate_tanh.at(i, t))
                need(pe, i, WQKV)
                pe.wait_ge(xt_high.sem, xt_high.at(i, 1))
                pe.wait_ge(xt_low.sem, xt_low.at(i, 1))
                product(b[:, 0:DM], chunks((xt_h, xt_l), toks), chunks(wqkv, slice(512, 768)))
                need(pe, i, WGATE)
                pe.wait_ge(ct_high.sem, ct_high.at(i, 1))
                pe.wait_ge(ct_low.sem, ct_low.at(i, 1))
                product(b[:, DM:DM + HEADS], chunks((ct_h, ct_l), toks), chunks(wgate, slice(512, 528)), last=False)
                pe.matmul(b[:, DM:DM + HEADS], ones2[:, :], bias2[:, 512:528], start=False, stop=True,
                          skip_group_check=True).then_inc(vg_ps.sem, 1)

            def project_gates(i, t):
                toks = slice(t * P, (t + 1) * P)
                b = bank_a[(t + 1) % 2]
                need(pe, i, WGATE)
                pe.wait_ge(qk_square.sem, qk_square.at(i, t + 1))
                pe.wait_ge(ct_high.sem, ct_high.at(i, 1))
                pe.wait_ge(ct_low.sem, ct_low.at(i, 1))
                product(b[:, 0:512], chunks((ct_h, ct_l), toks), chunks(wgate, slice(0, 512)), last=False)
                pe.matmul(b[:, 0:512], ones2[:, :], bias2[:, 0:512], start=False, stop=True,
                          skip_group_check=True).then_inc(gate_ps.sem, 1)

            def turn_b_gamma(i, t):
                b = bank_a[(t + 1) % 2]
                pe.wait_ge(bkn_ready.sem, bkn_ready.at(i, 1))
                pe.wait_ge(gam_tanh.sem, gam_tanh.at(i, TT))
                if t == 0:
                    pe.wait_ge(v_gated.sem, v_gated.at(i, TT))
                else:
                    pe.wait_ge(gate_tanh.sem, gate_tanh.at(i, TT))
                for n, src in enumerate((bkn, gam)):
                    for c in range(KC):
                        ins = pe.transpose(b[:, (KC * n + c) * P:(KC * n + c + 1) * P],
                                           src[:, t, c * P:(c + 1) * P], ident[:, :])
                ins.then_inc(bg_ps.sem, 1)

            def center_mem(i):
                pe.wait_ge(mem_ready.sem, mem_ready.at(i, TT * KC))
                for t in range(TT):
                    for c in range(KC):
                        ins = pe.matmul(bank_a[1][:, t * DM + c * P:t * DM + (c + 1) * P], memt[:, t, c, :],
                                        center[:, :], start=True, stop=True, skip_group_check=True)
                ins.then_inc(ctr_ps.sem, 1)

            def turn_out(i):
                pe.wait_ge(o5_ready.sem, o5_ready.at(i, 1))
                pe.wait_ge(wx_kept.sem, wx_kept.at(i - ROUTER_BEHIND, 6))
                turned(o5, bank_a[0]).then_inc(ot_ps.sem, 1)

            def project_out(i):
                need(pe, i, WO)
                pe.wait_ge(ot_high.sem, ot_high.at(i, 1))
                pe.wait_ge(ot_low.sem, ot_low.at(i, 1))
                pe.wait_ge(m1_ready.sem, m1_ready.at(i, 1))
                for t in range(TT):
                    ins = product(bank_a[1][:, t * DM:(t + 1) * DM], chunks((ot_h, ot_l), slice(t * P, (t + 1) * P)),
                                  chunks(wo, slice(0, DM)))
                ins.then_inc(mix_ps.sem, 1)

            def turn_keys(i):
                pe.wait_ge(k_high.sem, k_high.at(i, 1))
                pe.wait_ge(k_low.sem, k_low.at(i, 1))
                pe.wait_ge(val_kept.sem, val_kept.at(i, 0))
                pe.sem_inc(held, 1)
                psum = bank_v[:, 0:256].bitcast(F16)
                for b in range(NB):
                    pe.transpose(psum[:, SEQ * b:SEQ * (b + 1)], k2[:, b, 0:2 * CTX], ident16[0:SEQ, 0:SEQ])
                    ins = pe.transpose(psum[0:CTX, 256 + SEQ * b:256 + SEQ * (b + 1)], k2[:, b, 2 * CTX:3 * CTX],
                                       ident16[0:SEQ, 0:SEQ])
                ins.then_inc(kt_ps.sem, 1)

            def turn_queries(i, t):
                pe.wait_ge(xq_ready.sem, xq_ready.at(i, t + 1))
                pe.wait_ge(att_norm.sem, att_norm.at(i, 3 * (t + 1) - 3 * TT))
                pe.sem_inc(held, 1)
                for gp in range(2):
                    ins = pe.transpose(bank_b[t][:, gp * P:(gp + 1) * P], xq[:, t, gp * P:(gp + 1) * P], ident[:, :])
                ins.then_inc(qt_ps.sem, 1)

            def scores_by_row(i, n):
                b, gp = n // 2, n % 2
                if n == 0:
                    pe.wait_ge(k_masked.sem, k_masked.at(i, 2))
                    pe.wait_ge(q_low.sem, q_low.at(i, TT))
                elif n >= 2:
                    pe.wait_ge(row_max.sem, row_max.at(i, n - 1))
                pe.matmul(bank_b[n % 2][:, :], qs[0:64, b, 2 * gp:2 * gp + 2, :].rearrange("p g s -> p (g s)"),
                          kb[0:64, b, :, :].rearrange("p h s -> p (h s)"), start=True, stop=True,
                          skip_group_check=True).then_inc(row_ps.sem, 1)

            def turn_maxima(i):
                pe.wait_ge(row_max.sem, row_max.at(i, 2 * NB))
                pe.wait_ge(kt_kept.sem, kt_kept.at(i, 2))
                for gp in range(2):
                    ins = pe.transpose(bank_v[0:NB * KVH, gp * P:(gp + 1) * P],
                                       mx[:, gp, :, :].rearrange("p b h -> p (b h)"), ident[:, :])
                ins.then_inc(maxt_ps.sem, 1)

            def scores_by_column(i, n):
                b, jp = n // 2, n % 2
                need(pe, i, MAXSEL)
                if n == 0:
                    pe.wait_ge(maxt_kept.sem, maxt_kept.at(i, 1))
                    pe.wait_ge(q_again.sem, q_again.at(i, 1))
                if n >= 2:
                    pe.wait_ge(col_exp.sem, col_exp.at(i, n - 1))
                q = qs[:, b, :, :].rearrange("p g s -> p (g s)")
                for h in range(2):
                    j = 2 * jp + h
                    out = bank_b[n % 2][:, 256 * h:256 * h + 256]
                    pe.matmul(out, kb[:, b, 2 * j:2 * j + 2, :].rearrange("p h s -> p (h s)"), q,
                              start=True, stop=False, skip_group_check=True)
                    ins = pe.matmul(out, kl[:, b, 2 * j:2 * j + 2, :].rearrange("p h s -> p (h s)"),
                                    qm[:, b, :, :].rearrange("p g s -> p (g s)"), start=False, stop=True,
                                    skip_group_check=True)
                ins.then_inc(col_ps.sem, 1)

            def values(i, b):
                pe.wait_ge(col_exp.sem, col_exp.at(i, 2 * b + 2))
                pe.wait_ge(val_kept.sem, val_kept.at(i, b))
                pe.wait_ge(v_block.sem, v_block.at(i, 2))
                for j in range(NPAIR):
                    ins = pe.matmul(bank_v[32 * j:32 * j + 32, 256 * (b % 2):256 * (b % 2) + 256], vblk[:, b, j, :],
                                    prob[(2 * b + j // 2) % 4][:, 256 * (j % 2):256 * (j % 2) + 256], start=True,
                                    stop=True, skip_group_check=True)
                ins.then_inc(val_ps.sem, 1)

            def turn_values(i, t):
                pe.wait_ge(val_kept.sem, val_kept.at(i, 2 * t + 2))
                pe.wait_ge(col_exp.sem, col_exp.at(i, 2 * NB))
                for g in range(G):
                    ins = pe.transpose(bank_b[t][:, g * P:(g + 1) * P], avs[:, t, g, :, :].rearrange("p b s -> p (b s)"), ident[:, :])
                ins.then_inc(att_ps.sem, 1)

            def turn_h(i):
                pe.wait_ge(hn_ready.sem, hn_ready.at(i, TT))
                if not isinstance(i, int) or i + ROUTER_BEHIND < BLOCKS:
                    pe.wait_ge(mem_ready.sem, mem_ready.at(i + ROUTER_BEHIND, TT * KC))
                    pe.wait_ge(m1_ready.sem, m1_ready.at(i + ROUTER_BEHIND, 1))
                else:
                    pe.wait_ge(wx_kept.sem, wx_kept.at(i, 0))
                turned(hn, bank_a[0]).then_inc(ht_ps.sem, 1)

            def router_logits(i):
                need(pe, i, WRT)
                pe.wait_ge(ht_high.sem, ht_high.at(i, 1))
                pe.wait_ge(ht_low.sem, ht_low.at(i, 1))
                for t in range(TT):
                    ins = product(bank_a[1][:, EXPERTS * t:EXPERTS * (t + 1)],
                                  chunks((ht_h, ht_l), slice(t * P, (t + 1) * P)), chunks(wrt, slice(0, EXPERTS)))
                ins.then_inc(logit_ps.sem, 1)

            def turn_weights(i):
                pe.wait_ge(route.sem, route.at(i, 20))
                psum = bank_a[0][0:16, 0:128].bitcast(F16)
                for t in range(TT):
                    ins = pe.transpose(psum[:, t * P:(t + 1) * P], whl[:, t, :], ident16[:, :])
                ins.then_inc(wt_ps.sem, 1)

            def spread_weights(i, n):
                need(pe, i, WSEL)
                if n == 0:
                    pe.wait_ge(wt_kept.sem, wt_kept.at(i, 1))
                    pe.wait_ge(logit_exp.sem, logit_exp.at(i, TT))
                if n >= 2:
                    pe.wait_ge(wx_kept.sem, wx_kept.at(i, n - 1))
                for k in range(2 * n, min(2 * n + 2, FTR)):
                    ins = pe.matmul(bank_a[(n + 1) % 2][:, (k % 2) * TOK:(k % 2 + 1) * TOK], wsel[:, k, :], wt[:, :],
                                    start=True, stop=True, skip_group_check=True)
                ins.then_inc(wx_ps.sem, 1)

            def gate_up(i, k):
                cols = slice(k * P, (k + 1) * P)
                need(pe, i, WFU)
                if k == 0:
                    pe.wait_ge(ht_high.sem, ht_high.at(i, 1))
                    pe.wait_ge(ht_low.sem, ht_low.at(i, 1))
                pe.wait_ge(up_done.sem, up_done.at(i, k - 1))
                h = chunks((ht_h, ht_l), slice(0, TOK))
                product(bank_gu[k % 2][:, 0:TOK], chunks(wfg, cols), h)
                product(bank_gu[k % 2][:, TOK:2 * TOK], chunks(wfu, cols), h).then_inc(gu_ps.sem, 1)

            def down(i, k):
                need(pe, i, WFD)
                pe.wait_ge(hid_high.sem, hid_high.at(i, k + 1))
                pe.wait_ge(hid_low.sem, hid_low.at(i, k + 1))
                if k == 0:
                    pe.wait_ge(y_ready.sem, y_ready.at(i, 0))
                for t in range(TT):
                    toks = slice(t * P, (t + 1) * P)
                    hh, hl = hid_h[k % 2], hid_l[k % 2]
                    for n, (l, r) in enumerate(((hh, wfd[0]), (hl, wfd[0]), (hh, wfd[1]))):
                        ins = pe.matmul(bank_dn[:, t * DM:(t + 1) * DM], l[:, toks], r[:, k, :],
                                        start=k == 0 and t == 0 and n == 0, stop=k == FT - 1 and n == 2,
                                        skip_group_check=True)
                ins.then_inc(down_ps.sem, 1)

            def turn(j):
                b = blocks(j)
                on(b[2], scores_by_row, 5)
                on(b[1], turn_b_gamma, 0)
                on(b[1], turn_b_gamma, 1)
                on(b[4], down, 7)
                on(b[2], scores_by_row, 6)
                on(b[2], scores_by_row, 7)
                on(b[1], center_mem)
                on(b[4], down, 8)
                on(b[2], turn_maxima)
                on(b[4], gate_up, 12)
                on(b[4], down, 9)
                on(b[2], scores_by_column, 0)
                on(b[2], scores_by_column, 1)
                on(b[4], gate_up, 13)
                on(b[2], scores_by_column, 2)
                on(b[2], scores_by_column, 3)
                on(b[3], turn_h)
                on(b[2], values, 0)
                on(b[2], scores_by_column, 4)
                on(b[4], down, 10)
                on(b[2], scores_by_column, 5)
                on(b[3], router_logits)
                on(b[3], gate_up, 0)
                on(b[2], values, 1)
                on(b[3], gate_up, 1)
                on(b[2], scores_by_column, 6)
                on(b[2], scores_by_column, 7)
                on(b[4], down, 11)
                on(b[2], values, 2)
                on(b[4], down, 12)
                on(b[3], gate_up, 2)
                on(b[4], down, 13)
                on(b[3], turn_weights)
                on(b[2], turn_values, 0)
                on(b[2], values, 3)
                on(b[3], spread_weights, 0)
                on(b[3], spread_weights, 1)
                on(b[3], gate_up, 3)
                on(b[3], spread_weights, 2)
                on(b[3], spread_weights, 3)
                on(b[3], down, 0)
                on(b[2], turn_values, 1)
                on(b[3], spread_weights, 4)
                on(b[3], spread_weights, 5)
                on(b[3], gate_up, 4)
                on(b[1], turn_out)
                on(b[3], down, 1)
                on(b[3], gate_up, 5)
                on(b[0], turn_x)
                on(b[1], project_out)
                on(b[3], down, 2)
                on(b[3], gate_up, 6)
                on(b[3], gate_up, 7)
                on(b[3], down, 3)
                on(b[1], turn_keys)
                on(b[0], project_qk, 0)
                on(b[3], down, 4)
                on(b[0], project_v_gamma, 0)
                on(b[0], project_gates, 0)
                on(b[1], turn_queries, 0)
                on(b[3], gate_up, 8)
                on(b[1], turn_queries, 1)
                on(b[0], project_qk, 1)
                on(b[0], project_v_gamma, 1)
                on(b[3], down, 5)
                on(b[3], gate_up, 9)
                on(b[1], scores_by_row, 0)
                on(b[0], project_gates, 1)
                on(b[1], scores_by_row, 1)
                on(b[3], down, 6)
                on(b[3], gate_up, 10)
                on(b[1], scores_by_row, 2)
                on(b[1], scores_by_row, 3)
                on(b[3], gate_up, 11)
                on(b[1], scores_by_row, 4)

            pe.wait_ge(primed, 1)
            for j in range(LAGS):
                turn(j)
            with pe.Fori(LAGS, BLOCKS) as j:
                turn(j)
            for j in range(BLOCKS, BLOCKS + LAGS):
                turn(j)

        @block.vector
        def _(dve):
            dve.wait_ge(cst_loaded, 16 * len(consts))
            dve.tensor_scalar(rows[:, 2:4, :], rows[:, 2:4, :], SN, None, ALU.mult).then_inc(cst_dve, 1)
            dve.wait_ge(cst_act, 3)
            dve.scalar_tensor_tensor(bias2[32:33, :], bias_f[32:33, :], SW, bias2[32:33, :], ALU.mult,
                                     ALU.subtract).then_inc(cst_dve, 1)

            def weight_low(i, n):
                src, high, low, scale = loads[n]
                dve.wait_ge(stage_high, n + 1)
                dve.scalar_tensor_tensor(low, stage[n % 2][:, 0:src.shape[1]], scale, high, ALU.mult,
                                         ALU.subtract).then_inc(stage_split, 1)

            def inverse_root(i, chain, k, n, y, t, v):
                dve.wait_ge(chain.sem, chain.at(i, k + n))
                if n == 0:
                    ins = dve.tensor_scalar(y.bitcast(I32), v.bitcast(I32), -0.5, MAGIC, ALU.mult, ALU.add)
                elif n == 10:
                    ins = dve.tensor_scalar(y, y, -0.125, None, ALU.mult)
                elif n % 3 == 1:
                    ins = dve.scalar_tensor_tensor(t, y, 0.25 ** (n // 3), y, ALU.mult, ALU.mult)
                elif n % 3 == 2:
                    ins = dve.tensor_tensor(t, t, v, ALU.mult)
                else:
                    ins = dve.scalar_tensor_tensor(y, t, -3.0, y, ALU.add, ALU.mult)
                ins.then_inc(chain.sem, 1)

            def norm_stats(i, x, st, mv, ve, stat, ready, ready_k, rstd):
                dve.wait_ge(ready.sem, ready.at(i, ready_k))
                for t in range(TT):
                    dve.bn_stats(st[:, t, :], x[:, t, :]).then_inc(stat.sem, 1)
                for t in range(TT):
                    dve.wait_ge(stat.sem, stat.at(i, t + 1))
                    dve.sem_inc(held, 1)
                    dve.bn_aggr(mv[:, t, :], st[:, t, :]).then_inc(stat.sem, 1)
                dve.wait_ge(stat.sem, stat.at(i, 4))
                dve.wait_ge(rstd.sem, rstd.at(i, 0))
                dve.tensor_scalar(ve[:, :], mv[:, :, 1], 1.0 / SX ** 2, EPS / SX ** 2, ALU.mult,
                                  ALU.add).then_inc(stat.sem, 1)

            def norm_apply(i, x, mv, rs, out, rstd, done, free, view=lambda z: z, out_view=lambda z: z):
                dve.wait_ge(rstd.sem, rstd.at(i, 1))
                dve.wait_ge(free.sem, free.at(i, 0))
                for t in range(TT):
                    dve.tensor_scalar(out_view(out[:, t, :]), view(x[:, t, :]), mv[:, t, 0:1], rs[:, t:t + 1], ALU.subtract,
                                      ALU.mult).then_inc(done.sem, 1)

            def norm1_stats(i):
                norm_stats(i, x_in, st1, mv1, ve1, ln1_stat, x_loaded, 16, ln1_rstd)

            def norm1_apply(i):
                norm_apply(i, x_in, mv1, rs1, xn, ln1_rstd, xn_ready, xt_ps)

            def norm2_stats(i):
                norm_stats(i, x1, st2, mv2, ve2, ln2_stat, x1_ready, 1, ln2_rstd)

            def norm2_apply(i):
                norm_apply(i, x1, mv2, rs2, xq, ln2_rstd, xq_ready, qt_ps,
                           view=lambda z: z.rearrange("p (h g d) -> p h g d", h=KVH, g=G),
                           out_view=lambda z: z.rearrange("p (g h d) -> p h g d", h=KVH, g=G))

            def norm3_stats(i):
                norm_stats(i, x2, st3, mv3, ve3, ln3_stat, x2_ready, TT, ln3_rstd)

            def norm3_apply(i):
                norm_apply(i, x2, mv3, rs3, hn, ln3_rstd, hn_ready, ht_ps)

            def x_low(i):
                dve.wait_ge(conv_first.sem, conv_first.at(i, KC))
                dve.wait_ge(xt_high.sem, xt_high.at(i, 1))
                psum = bank_a[0][:, :].rearrange("p (c t) -> p c t", c=KC)
                dve.wait_ge(vg_ps.sem, vg_ps.at(i, 0))
                dve.tensor_tensor(xt_l[:, :, :], psum, xt_h[:, :, :], ALU.subtract).then_inc(xt_low.sem, 1)

            def conv(i, tap):
                psum = bank_a[0][:, :].rearrange("p (c b s) -> p c b s", c=KC, b=NB)
                for c in range(KC):
                    if tap == 1:
                        dve.wait_ge(conv_first.sem, conv_first.at(i, KC))
                        dve.wait_ge(xt_high.sem, xt_high.at(i, 1))
                    else:
                        dve.wait_ge(conv_taps.sem, conv_taps.at(i, KC * (tap - 2) + c + 1))
                    dve.scalar_tensor_tensor(cacc[:, c, :, tap:SEQ], psum[:, c, :, 0:SEQ - tap],
                                             convw[:, c, CONV - 1 - tap:CONV - tap], cacc[:, c, :, tap:SEQ],
                                             ALU.mult, ALU.add).then_inc(conv_taps.sem, 1)

            def silu(i):
                dve.wait_ge(conv_tanh.sem, conv_tanh.at(i, 1))
                dve.wait_ge(ct_low.sem, ct_low.at(i, 0))
                dve.wait_ge(ct_high.sem, ct_high.at(i, 0))
                dve.scalar_tensor_tensor(csil[:, :, :], cth[:, :, :], 1.0, cacc[:, :, :, :].rearrange("p c b s -> p c (b s)"),
                                         ALU.add, ALU.mult).then_inc(conv_silu.sem, 1)

            def gate_values(i, t):
                dve.wait_ge(gate_tanh.sem, gate_tanh.at(i, t + 1))
                dve.wait_ge(vg_ps.sem, vg_ps.at(i, t + 1))
                dve.wait_ge(gam_tanh.sem, gam_tanh.at(i, t + 1))
                dve.wait_ge(bkn_ready.sem, bkn_ready.at(i, 0))
                dve.scalar_tensor_tensor(bv[:, t, :], gate_t[:, t, 0:DM], 1.0, bank_a[t % 2][:, 0:DM],
                                         ALU.add, ALU.mult).then_inc(v_gated.sem, 1)

            def qk_sum(i, t):
                dve.wait_ge(qk_square.sem, qk_square.at(i, t + 1))
                dve.wait_ge(qk_norm.sem, qk_norm.at(i, 0))
                dve.tensor_reduce(ss_qk[:, t, :], qk_sq[:, t, :].rearrange("p (h d) -> p h d", d=HD), AX_X,
                                  ALU.add).then_inc(qk_sums.sem, 1)

            def flat_heads(t):
                return t[:, :, :].rearrange("p t h -> p (t h)")

            def qk_root(i, n):
                if n == 0:
                    dve.wait_ge(qk_sums.sem, qk_sums.at(i, TT))
                    dve.wait_ge(qn_ready.sem, qn_ready.at(i, 0))
                    dve.wait_ge(bkn_ready.sem, bkn_ready.at(i, 0))
                    dve.tensor_scalar(flat_heads(ss_qk), flat_heads(ss_qk), S_PROJ ** 2 * 1e-24, None,
                                      ALU.max).then_inc(qk_norm.sem, 1)
                else:
                    inverse_root(i, qk_norm, 1, n - 1, flat_heads(r_qk), flat_heads(t_qk), flat_heads(ss_qk))

            def scan(i, t):
                b = bank_a[(t + 1) % 2]
                dve.wait_ge(decay_ready.sem, decay_ready.at(i, t + 1))
                dve.wait_ge(ctr_ps.sem, ctr_ps.at(i, 0))
                for c in range(KC):
                    dve.tensor_tensor_scan(memt[:, t, c, :], at[:, t, c, :, :].rearrange("p b s -> p (b s)"),
                                           b[:, c * P:(c + 1) * P], 0.0, ALU.mult, ALU.add).then_inc(mem_ready.sem, 1)

            def head_root(i, n, sq, ss, v, r, t, norm, squared, scale):
                if n == 0:
                    dve.wait_ge(squared.sem, squared.at(i, 1))
                    dve.tensor_reduce(flat_heads(ss), sq[:, :, :].rearrange("p t (h d) -> p (t h) d", d=HD), AX_X,
                                      ALU.add).then_inc(norm.sem, 1)
                elif n == 1:
                    dve.wait_ge(norm.sem, norm.at(i, 1))
                    dve.tensor_scalar(flat_heads(v), flat_heads(ss), 1.0 / HD, EPS * scale ** 2, ALU.mult,
                                      ALU.add).then_inc(norm.sem, 1)
                else:
                    inverse_root(i, norm, 2, n - 2, flat_heads(r), flat_heads(t), flat_heads(v))

            def mem_root(i, n):
                head_root(i, n, msq, ss_m, v_m, r_m, t_m, mem_norm, mem_square, SM)

            def out_root(i, n):
                head_root(i, n, osq, ss_o, v_o, r_o, t_o, out_norm, out_square, 1.0)

            def heads(t):
                return t.rearrange("p t (h d) -> p (t h) d", d=HD)

            def per_head(r):
                return r[:, :, :].rearrange("p t h -> p (t h)").unsqueeze(2).broadcast_to([P, TT * HEADS, HD])

            def mem_scaled(i):
                dve.wait_ge(mem_norm.sem, mem_norm.at(i, 13))
                dve.wait_ge(o1_ready.sem, o1_ready.at(i, 0))
                dve.tensor_tensor(heads(m1[:, :, :]), bank_a[1][:, :].rearrange("p (h d) -> p h d", d=HD), per_head(r_m),
                                  ALU.mult).then_inc(m1_ready.sem, 1)

            def out_sums(i):
                dve.wait_ge(o1_ready.sem, o1_ready.at(i, 1))
                dve.tensor_reduce(sum_o[:, :, :].rearrange("p t h -> p (t h)"), heads(o1[:, :, :]), AX_X,
                                  ALU.add).then_inc(out_center.sem, 1)

            def center_out(i):
                dve.wait_ge(out_center.sem, out_center.at(i, 1))
                dve.scalar_tensor_tensor(heads(oc[:, :, :]), per_head(sum_o), -1.0 / HD, heads(o1[:, :, :]), ALU.mult,
                                         ALU.add).then_inc(out_center.sem, 1)

            def out_scaled(i):
                dve.wait_ge(out_norm.sem, out_norm.at(i, 13))
                dve.wait_ge(o5_ready.sem, o5_ready.at(i, 0))
                dve.tensor_tensor(heads(o2[:, :, :]), heads(oc[:, :, :]), per_head(r_o), ALU.mult).then_inc(o2_ready.sem, 1)

            def gate_out(i):
                dve.wait_ge(o4_ready.sem, o4_ready.at(i, 1))
                dve.wait_ge(ot_ps.sem, ot_ps.at(i, 0))
                dve.scalar_tensor_tensor(o5[:, :, :], gate_t[:, :, DM:2 * DM], 1.0, o2[:, :, :], ALU.add,
                                         ALU.mult).then_inc(o5_ready.sem, 1)

            def out_low(i):
                dve.wait_ge(ot_high.sem, ot_high.at(i, 1))
                dve.wait_ge(mix_ps.sem, mix_ps.at(i, 0))
                dve.tensor_tensor(ot_l[:, :, :], bank_a[0][:, :].rearrange("p (c t) -> p c t", c=KC), ot_h[:, :, :],
                                  ALU.subtract).then_inc(ot_low.sem, 1)

            def mixer_residual(i):
                dve.wait_ge(mix_ps.sem, mix_ps.at(i, 1))
                dve.wait_ge(x_kept.sem, x_kept.at(i, 1))
                dve.wait_ge(x2_ready.sem, x2_ready.at(i, 0))
                dve.scalar_tensor_tensor(x1[:, :, :], bank_a[1][:, :].rearrange("p (t d) -> p t d", t=TT),
                                         1.0 / (2.0 * SN * SW), x_res[:, :, :], ALU.mult, ALU.add).then_inc(x1_ready.sem, 1)

            def keys_low(i):
                dve.wait_ge(k_high.sem, k_high.at(i, 1))
                dve.scalar_tensor_tensor(k2[:, :, 2 * CTX:3 * CTX], ctxs[0:SEQ, :, :], SK, k2[:, :, 0:CTX], ALU.mult,
                                         ALU.subtract).then_inc(k_low.sem, 1)

            def mask_keys(i):
                need(dve, i, KMASK)
                dve.wait_ge(kt_kept.sem, kt_kept.at(i, 2))
                dve.wait_ge(col_ps.sem, col_ps.at(i, 0))
                for src, dst, rows_ in ((kt, kb, P), (ktl, kl, CTX)):
                    dve.tensor_tensor(dst[0:rows_, :, :, :], src[:, :, :].unsqueeze(2).broadcast_to([rows_, NB, KVH, SEQ]),
                                      kmask[0:rows_, :, :].unsqueeze(1).broadcast_to([rows_, NB, KVH, SEQ]),
                                      ALU.mult).then_inc(k_masked.sem, 1)

            def queries_low(i, t):
                dve.wait_ge(q_high.sem, q_high.at(i, t + 1))
                for odd in range(2):
                    ins = dve.tensor_tensor(query_heads(qs, 64, t, odd), turned_queries(t, odd),
                                            query_heads(qs, 0, t, odd), ALU.subtract)
                ins.then_inc(q_low.sem, 1)

            def queries_again(i):
                dve.wait_ge(q_high.sem, q_high.at(i, TT))
                dve.wait_ge(col_ps.sem, col_ps.at(i, 0))
                dve.tensor_copy(qm[0:CTX, :, :, :].rearrange("p b g s -> p (b g s)"),
                                qs[0:CTX, :, :, :].rearrange("p b g s -> p (b g s)")).then_inc(q_again.sem, 1)

            def maxima(i, n):
                b, gp = n // 2, n % 2
                dve.wait_ge(row_ps.sem, row_ps.at(i, n + 1))
                if n == 0:
                    dve.wait_ge(maxt_ps.sem, maxt_ps.at(i, 0))
                dve.tensor_reduce(mx[:, gp, b, :], bank_b[n % 2][:, :].rearrange("p (h s) -> p h s", s=SEQ), AX_X,
                                  ALU.max).then_inc(row_max.sem, 1)

            def attention_norm(i, t):
                cols = bank_b[t][:, :].rearrange("p (g j m) -> p g j m", g=G, j=NPAIR)
                dve.wait_ge(att_ps.sem, att_ps.at(i, t + 1))
                dve.wait_ge(x2_ready.sem, x2_ready.at(i, t + 1 - TT))
                dve.reciprocal(orec[:, t, :, :, :], cols[:, :, :, 16:18]).then_inc(att_norm.sem, 1)
                dve.wait_ge(att_norm.sem, att_norm.at(i, 3 * t + 1))
                out = oatt[:, t, :].rearrange("p (j h g d) -> p g j h d", j=NPAIR, h=2, g=G)
                for h in range(2):
                    dve.tensor_tensor(out[:, :, :, h, :], cols[:, :, :, 8 * h:8 * h + 8],
                                      orec[:, t, :, :, h:h + 1].broadcast_to([P, G, NPAIR, HQ]),
                                      ALU.mult).then_inc(att_norm.sem, 1)

            def h_low(i):
                dve.wait_ge(ht_high.sem, ht_high.at(i, 1))
                dve.wait_ge(gu_ps.sem, gu_ps.at(i, 0))
                dve.tensor_tensor(ht_l[:, :, :], bank_a[0][:, :].rearrange("p (c t) -> p c t", c=KC), ht_h[:, :, :],
                                  ALU.subtract).then_inc(ht_low.sem, 1)

            def per_group(t):
                return t[:, :, :].rearrange("p t (g e) -> p (t g) e", e=2)

            def softmax(i, n):
                logits = bank_a[1][:, 0:TT * EXPERTS].rearrange("p (t e) -> p t e", e=EXPERTS)
                if n == 0:
                    dve.wait_ge(logit_ps.sem, logit_ps.at(i, 1))
                    ins = dve.tensor_reduce(lmax[:, :], logits, AX_X, ALU.max)
                else:
                    dve.wait_ge(route.sem, route.at(i, n))
                if n == 1:
                    ins = dve.tensor_scalar(lneg[:, :], lmax[:, :], -1.0 / S_PROJ, None, ALU.mult)
                elif n == 2:
                    dve.wait_ge(logit_exp.sem, logit_exp.at(i, TT))
                    ins = dve.tensor_reduce(lsum[:, :], lexp[:, :, :], AX_X, ALU.add)
                elif n == 3:
                    ins = dve.reciprocal(lrec[:, :], lsum[:, :])
                elif n == 4:
                    ins = dve.tensor_tensor(prb[:, :, :], lexp[:, :, :],
                                            lrec[:, :].unsqueeze(2).broadcast_to([P, TT, EXPERTS]), ALU.mult)
                elif n == 5:
                    ins = dve.tensor_reduce(gs[:, :, :].rearrange("p t g -> p (t g)"), per_group(prb), AX_X, ALU.max)
                ins.then_inc(route.sem, 1)

            def rank(i, n, k, v, gt, eq, cnt, out, before, size):
                shape = [P, TT, size, size]
                other, own = v[:, :, :].unsqueeze(2).broadcast_to(shape), v[:, :, :].unsqueeze(3).broadcast_to(shape)
                dve.wait_ge(route.sem, route.at(i, k if n < 2 else k + n))
                if n == 0:
                    ins = dve.tensor_tensor(gt[:, :, :, :], other, own, ALU.is_gt)
                elif n == 1:
                    ins = dve.tensor_tensor(eq[:, :, :, :], other, own, ALU.is_equal)
                elif n == 2:
                    ins = dve.tensor_tensor(eq[:, :, :, :], eq[:, :, :, :], before.unsqueeze(1).broadcast_to(shape), ALU.mult)
                elif n == 3:
                    ins = dve.tensor_tensor(cnt[:, :, :, :], gt[:, :, :, :], eq[:, :, :, :], ALU.add)
                else:
                    ins = dve.tensor_reduce(out[:, :], cnt[:, :, :, :].rearrange("p t a b -> p (t a) b"), AX_X, ALU.add)
                ins.then_inc(route.sem, 1)

            def group_rank(i, n):
                rank(i, n, 6, gs, ggt, geq, gcnt, grank, tri4, 4)

            def keep_groups(i):
                dve.wait_ge(route.sem, route.at(i, 11))
                dve.scalar_tensor_tensor(per_group(pm), grank[:, :].unsqueeze(2).broadcast_to([P, TT * 4, 2]), 2.0,
                                         per_group(prb), ALU.is_lt, ALU.mult).then_inc(route.sem, 1)

            def expert_rank(i, n):
                rank(i, n, 12, pm, egt, eeq, ecnt, erank, tri8, 8)

            def keep_experts(i):
                dve.wait_ge(route.sem, route.at(i, 17))
                dve.scalar_tensor_tensor(wts[:, :, :].rearrange("p t e -> p (t e)"), erank[:, :], 2.0,
                                         pm[:, :, :].rearrange("p t e -> p (t e)"), ALU.is_lt,
                                         ALU.mult).then_inc(route.sem, 1)

            def weights_high(i):
                dve.wait_ge(route.sem, route.at(i, 18))
                dve.wait_ge(wt_ps.sem, wt_ps.at(i, 0))
                dve.tensor_scalar(whl[:, :, 0:8], wts[:, :, :], SW, None, ALU.mult).then_inc(route.sem, 1)

            def weights_low(i):
                dve.wait_ge(route.sem, route.at(i, 19))
                dve.scalar_tensor_tensor(whl[:, :, 8:16], wts[:, :, :], SW, whl[:, :, 0:8], ALU.mult,
                                         ALU.subtract).then_inc(route.sem, 1)

            def expert_silu(i, k):
                dve.wait_ge(tanh_done.sem, tanh_done.at(i, k + 1))
                dve.scalar_tensor_tensor(ff_g[k % 2][:, :], ff_tanh[k % 2][:, :], 1.0, bank_gu[k % 2][:, 0:TOK], ALU.add,
                                         ALU.mult).then_inc(silu_done.sem, 1)

            def expert_up(i, k):
                scale = SH / (2.0 * S_PROJ ** 2) * (1.0 if k < FTS else 4.0)
                dve.wait_ge(silu_done.sem, silu_done.at(i, k + 1))
                b, n = (i, k - 2) if k >= 2 else (i - 1, k - 2 + FT)
                if n >= FTS:
                    dve.wait_ge(weighted.sem, weighted.at(b, n - FTS + 1))
                else:
                    dve.wait_ge(hid_low.sem, hid_low.at(b, n + 1))
                dve.scalar_tensor_tensor(ff_u[k % 2][:, :], ff_g[k % 2][:, :], scale, bank_gu[k % 2][:, TOK:2 * TOK],
                                         ALU.mult, ALU.mult).then_inc(up_done.sem, 1)

            def expert_residual(i):
                dve.wait_ge(down_ps.sem, down_ps.at(i, FT))
                dve.wait_ge(y_based.sem, y_based.at(i, 1))
                dve.scalar_tensor_tensor(y_sb[:, :, :], bank_dn[:, :].rearrange("p (t d) -> p t d", t=TT),
                                         1.0 / (SH * SW), y_sb[:, :, :], ALU.mult, ALU.add).then_inc(y_ready.sem, 1)

            def turn(j):
                b = blocks(j)
                on(b[3], qk_root, 6)
                on(b[3], gate_values, 1)
                on(b[3], qk_root, 7)
                on(b[3], qk_root, 8)
                once(b[3], weight_low, 6)
                on(b[6], expert_up, 9)
                for n in range(9, 12):
                    on(b[3], qk_root, n)
                on(b[4], maxima, 2)
                on(b[4], maxima, 3)
                on(b[6], expert_silu, 10)
                on(b[4], maxima, 4)
                on(b[4], maxima, 5)
                on(b[3], scan, 0)
                on(b[3], scan, 1)
                on(b[4], maxima, 6)
                on(b[4], maxima, 7)
                on(b[6], expert_up, 10)
                on(b[4], queries_again)
                for n in range(0, 3):
                    on(b[3], mem_root, n)
                on(b[6], expert_silu, 11)
                for n in range(3, 7):
                    on(b[3], mem_root, n)
                on(b[6], expert_up, 11)
                for n in range(7, 10):
                    on(b[3], mem_root, n)
                once(b[3], weight_low, 8)
                for n in range(10, 13):
                    on(b[3], mem_root, n)
                on(b[3], mem_scaled)
                on(b[6], expert_silu, 12)
                on(b[2], norm1_stats)
                on(b[6], expert_up, 12)
                once(b[3], weight_low, 9)
                on(b[5], h_low)
                on(b[6], expert_silu, 13)
                on(b[5], softmax, 0)
                on(b[5], softmax, 1)
                on(b[6], expert_up, 13)
                for n in range(2, 5):
                    on(b[5], softmax, n)
                on(b[3], out_sums)
                on(b[5], softmax, 5)
                on(b[3], center_out)
                on(b[5], group_rank, 0)
                on(b[5], group_rank, 1)
                on(b[5], expert_silu, 0)
                on(b[5], group_rank, 2)
                on(b[5], group_rank, 3)
                on(b[3], out_root, 0)
                on(b[5], group_rank, 4)
                on(b[5], expert_up, 0)
                on(b[3], out_root, 1)
                on(b[5], keep_groups)
                on(b[3], out_root, 2)
                on(b[5], expert_rank, 0)
                on(b[5], expert_rank, 1)
                on(b[3], out_root, 3)
                on(b[5], expert_rank, 2)
                on(b[3], out_root, 4)
                on(b[5], expert_rank, 3)
                once(b[3], weight_low, 10)
                on(b[3], out_root, 5)
                on(b[5], expert_rank, 4)
                on(b[3], out_root, 6)
                on(b[5], keep_experts)
                on(b[3], out_root, 7)
                on(b[5], weights_high)
                on(b[3], out_root, 8)
                on(b[5], weights_low)
                on(b[3], out_root, 9)
                on(b[3], out_root, 10)
                on(b[5], expert_silu, 1)
                on(b[3], out_root, 11)
                on(b[3], out_root, 12)
                on(b[5], expert_up, 1)
                on(b[3], out_scaled)
                on(b[5], expert_silu, 2)
                on(b[6], expert_residual)
                once(b[3], weight_low, 11)
                on(b[2], norm1_apply)
                on(b[5], expert_up, 2)
                on(b[4], attention_norm, 0)
                on(b[5], expert_silu, 3)
                on(b[3], gate_out)
                on(b[5], expert_up, 3)
                on(b[4], attention_norm, 1)
                on(b[3], keys_low)
                on(b[5], expert_silu, 4)
                on(b[3], out_low)
                once(b[3], weight_low, 12)
                on(b[5], expert_up, 4)
                on(b[4], norm3_stats)
                on(b[5], expert_silu, 5)
                on(b[5], expert_up, 5)
                for n in range(1, 4):
                    on(b[2], conv, n)
                on(b[2], x_low)
                on(b[3], mixer_residual)
                on(b[2], silu)
                on(b[3], norm2_stats)
                on(b[5], expert_silu, 6)
                on(b[4], norm3_apply)
                once(b[3], weight_low, 13)
                on(b[5], expert_up, 6)
                on(b[5], expert_silu, 7)
                once(b[2], weight_low, 0)
                on(b[3], norm2_apply)
                on(b[5], expert_up, 7)
                once(b[2], weight_low, 1)
                on(b[2], qk_sum, 0)
                once(b[2], weight_low, 2)
                on(b[2], gate_values, 0)
                on(b[3], mask_keys)
                on(b[3], queries_low, 0)
                on(b[3], queries_low, 1)
                on(b[2], qk_sum, 1)
                on(b[5], expert_silu, 8)
                for n in range(0, 3):
                    on(b[2], qk_root, n)
                on(b[5], expert_up, 8)
                on(b[2], qk_root, 3)
                on(b[3], maxima, 0)
                on(b[2], qk_root, 4)
                on(b[5], expert_silu, 9)
                on(b[2], qk_root, 5)
                on(b[3], maxima, 1)

            dve.wait_ge(primed, 1)
            for j in range(LAGS):
                turn(j)
            with dve.Fori(LAGS, BLOCKS) as j:
                turn(j)
            for j in range(BLOCKS, BLOCKS + LAGS):
                turn(j)


def kernel(x, ctx_512, L0_attn_Wq, L0_attn_Wk, L0_attn_Wv, L0_attn_Wo, L0_attn_conv_w, L0_attn_conv_b,
           L0_attn_Wig, L0_attn_b_ig, L0_attn_Wog, L0_attn_b_og, L0_attn_Wg, L0_attn_b_g, L0_attn_gn_w,
           L0_attn_gn_b, L0_attn_mn_w, L0_attn_mn_b, L0_ffn_gate_weight, L0_ffn_gate_w, L0_ffn_up_w,
           L0_ffn_down_w, L0_ffn_sh_gate_w, L0_ffn_sh_up_w, L0_ffn_sh_down_w):
    import numpy as np
    import concourse.bacc as bacc
    from concourse.bass_utils import run_bass_kernel_spmd

    arr = np.asarray

    def by_partition(w):
        return np.ascontiguousarray(w.reshape(-1, P, w.shape[1]).transpose(1, 0, 2).reshape(P, -1))

    def padded(w, n):
        return np.concatenate([w, np.zeros((n - w.shape[0], w.shape[1]), w.dtype)], 0)

    def hidden_rows(routed, shared):
        return np.concatenate([padded(shared, FTS * P), routed.reshape(-1, DM)], 0)

    eye = np.eye(P, dtype=np.float32)
    same_head = np.kron(np.eye(P // HD, dtype=np.float32), np.ones((HD, HD), np.float32))
    kmask = np.zeros((P, KVH, SEQ), np.float32)
    for p in range(P):
        kmask[p, (p % CTX) // HQ] = 1.0
    maxsel = np.zeros((NB, KVH, NB, NPAIR, 2, SEQ), np.float32)
    for b in range(NB):
        for h in range(KVH):
            maxsel[b, h, b, h // 2, h % 2] = -1.0
    wsel = np.zeros((2, EXPERTS, FTR * P), np.float32)
    for e in range(EXPERTS):
        wsel[:, e, e * FEXP:(e + 1) * FEXP] = 1.0 / (4.0 * SW)
    tri = np.concatenate([np.tril(np.ones((n, n), np.float32), -1).reshape(-1) for n in (4, 8)])

    b = np.concatenate([arr(L0_attn_b_ig), arr(L0_attn_b_og), arr(L0_attn_b_g)])[None, :]
    zeros = np.zeros((31, b.shape[1]), b.dtype)
    bias = np.concatenate([b, zeros, b], 0)

    ins = {
        "x": arr(x).reshape(-1, DM), "ctx": arr(ctx_512),
        "wqkv": by_partition(np.concatenate([arr(w).T for w in (L0_attn_Wq, L0_attn_Wk, L0_attn_Wv)], 1)),
        "wgate": by_partition(np.concatenate([arr(w).T for w in (L0_attn_Wig, L0_attn_Wog, L0_attn_Wg)], 1)),
        "bias": bias,
        "wo": by_partition(arr(L0_attn_Wo).T), "wrt": by_partition(arr(L0_ffn_gate_weight).T),
        "wfg": by_partition(hidden_rows(arr(L0_ffn_gate_w), arr(L0_ffn_sh_gate_w)).T),
        "wfu": by_partition(hidden_rows(arr(L0_ffn_up_w), arr(L0_ffn_sh_up_w)).T),
        "wfd": by_partition(hidden_rows(arr(L0_ffn_down_w).transpose(0, 2, 1), arr(L0_ffn_sh_down_w).T)),
        "convw": np.ascontiguousarray(arr(L0_attn_conv_w).reshape(KC, P, CONV).transpose(1, 0, 2)),
        "convb": np.ascontiguousarray(arr(L0_attn_conv_b).reshape(KC, P).T),
        "mn_w": arr(L0_attn_mn_w), "mn_b": arr(L0_attn_mn_b), "gn_w": arr(L0_attn_gn_w), "gn_b": arr(L0_attn_gn_b),
        "ident": eye, "center": eye - same_head / HD, "kmask": kmask.reshape(P, -1),
        "maxsel": maxsel.reshape(NB * KVH, -1), "wsel": wsel.reshape(2 * EXPERTS, -1),
        "tri": np.ascontiguousarray(np.broadcast_to(tri, (P, tri.size))),
    }
    nc = bacc.Bacc("TRN2", target_bir_lowering=False, num_devices=1)
    arrays, a = {}, {}
    for name, v in ins.items():
        arrays[f"in_{name}"] = np.ascontiguousarray(v)
        a[name] = nc.dram_tensor(f"in_{name}", v.shape, mybir.dt.from_np(v.dtype), kind="ExternalInput").ap()
    a["y"] = nc.dram_tensor("out_y", ins["x"].shape, F32, kind="ExternalOutput").ap()
    build(nc, a)
    r = run_bass_kernel_spmd(nc, [arrays], core_ids=[0])
    return r.results[0]["out_y"].reshape(arr(x).shape)
```
